# Optimizing a Trainium2 kernel written in Bass

```python
import numpy as np
import jax
import jax.numpy as jnp

def _softmax(x, axis=-1):
    return jax.nn.softmax(x, axis=axis)

def _gelu(x):
    return jax.nn.gelu(x, approximate=True)

def _silu(x):
    return jax.nn.silu(x)

def _sigmoid(x):
    return jax.nn.sigmoid(x)

def _layernorm(x, axis=-1, eps=1e-05):
    m = jnp.mean(x, axis=axis, keepdims=True)
    v = jnp.var(x, axis=axis, keepdims=True)
    return (x - m) / jnp.sqrt(v + eps)

def _scatter_add(tgt, idx, src, axis=0):
    return tgt.at[idx].add(src)

def _segment_sum(src, seg, n):
    return jax.ops.segment_sum(src, seg, n)
kernel_name = 'mk_adaln_ffn_d2_seqx_r4_9e93fd'

def setup_inputs(seed: int=0):
    np.random.seed(seed)
    _w = jnp.asarray

    def _rec_inputs():
        import jax
        import jax.numpy as jnp
        _rk = jax.random.key(seed)
        x = -0.000125 + 0.9999 * jax.random.normal(jax.random.fold_in(_rk, 1), (32, 64, 1024), jnp.float32)
        _lenS = 64 - jax.random.randint(jax.random.fold_in(_rk, 7), (32,), 0, max(1, 64 // 4) + 1, jnp.int32)
        _lenS2 = 64 - jax.random.randint(jax.random.fold_in(_rk, 8), (32,), 0, max(1, 64 // 4) + 1, jnp.int32)
        cond_128 = 0.0061147 + 1.02565 * jax.random.normal(jax.random.fold_in(_rk, 11), (32, 128), jnp.float32)
        fside_S_0 = -0.022604 + 0.987366 * jax.random.normal(jax.random.fold_in(_rk, 12), (64,), jnp.float32)
        return (x, cond_128, fside_S_0)
    x, cond_128, fside_S_0 = _rec_inputs()

    def _L0_cond_setup():
        import jax, jax.numpy as jnp
        import numpy as np
        K = 8
        T = 1.0
        D_EMBD = 128
        IN_C = 64
        OUT_C = 64
        BS = 32
        H = 1024
        HID = 128
        key = jax.random.key(seed)
        ks = jax.random.split(key, 10)
        s = lambda fan_in: 1.0 / np.sqrt(fan_in)
        return {'x': jax.random.normal(ks[0], (BS, IN_C, H), dtype=jnp.float32), 'embedding': jax.random.normal(ks[1], (BS, D_EMBD), dtype=jnp.float32), 'W0': jax.random.normal(ks[2], (D_EMBD, HID), dtype=jnp.float32) * s(D_EMBD), 'b0': jnp.zeros((HID,), dtype=jnp.float32), 'W1': jax.random.normal(ks[3], (HID, HID), dtype=jnp.float32) * s(HID), 'b1': jnp.zeros((HID,), dtype=jnp.float32), 'W2': jax.random.normal(ks[4], (HID, K), dtype=jnp.float32) * s(HID), 'b2': jnp.zeros((K,), dtype=jnp.float32), 'weight': jax.random.normal(ks[5], (K, OUT_C, IN_C, 1), dtype=jnp.float32) * s(IN_C), 'bias_k': jax.random.normal(ks[6], (K, OUT_C), dtype=jnp.float32) * 0.1}
    _L0_cond_all = _L0_cond_setup()
    _L0_cond_in = {k: v for k, v in _L0_cond_all.items() if k in ('W0', 'b0', 'W1', 'b1', 'W2', 'b2', 'weight', 'bias_k')}
    del _L0_cond_all

    def _L0_ffn_setup():
        import jax, jax.numpy as jnp
        import numpy as np
        B, T, D_IN, D_OUT = (8, 512, 1024, 1024)
        N_LORAS, RANK = (16, 32)
        SCALING = 1.0
        key = jax.random.key(seed)
        ks = jax.random.split(key, 8)
        std = 1.0 / D_IN ** 0.5
        x = jax.random.normal(ks[0], (B, T, D_IN), dtype=jnp.float32)
        idx = jax.random.randint(ks[1], (B,), 0, N_LORAS)
        gate = jax.nn.one_hot(idx, N_LORAS, dtype=jnp.float32)
        kernel = jax.random.normal(ks[2], (D_IN, D_OUT), dtype=jnp.float32) * std
        bias = jnp.zeros((D_OUT,), dtype=jnp.float32)
        lora_A = jax.random.normal(ks[3], (N_LORAS, RANK, D_IN), dtype=jnp.float32) * std
        lora_B = jax.random.normal(ks[4], (N_LORAS, D_OUT, RANK), dtype=jnp.float32) * 0.01
        lora_A_shared = jax.random.normal(ks[5], (RANK, D_IN), dtype=jnp.float32) * std
        lora_B_shared = jax.random.normal(ks[6], (D_OUT, RANK), dtype=jnp.float32) * 0.01
        return {'x': x, 'gate': gate, 'kernel': kernel, 'bias': bias, 'lora_A': lora_A, 'lora_B': lora_B, 'lora_A_shared': lora_A_shared, 'lora_B_shared': lora_B_shared}
    _L0_ffn_all = _L0_ffn_setup()
    _L0_ffn_in = {k: v for k, v in _L0_ffn_all.items() if k in ('gate', 'kernel', 'bias', 'lora_A', 'lora_B', 'lora_A_shared', 'lora_B_shared')}
    del _L0_ffn_all

    def _L1_cond_setup():
        import jax, jax.numpy as jnp
        import numpy as np
        from jax import lax
        N, C_IN, L = (32, 64, 1024)
        C_OUT, K, GROUPS = (64, 9, 4)
        C_DIM, PAD, STRIDE = (128, 4, 1)
        key = jax.random.key(seed)
        k1, k2, k3, k4, k5 = jax.random.split(key, 5)
        x = jax.random.normal(k1, (N, C_IN, L), dtype=jnp.float32)
        c = jax.random.normal(k2, (N, C_DIM), dtype=jnp.float32)
        weight = jax.random.normal(k3, (C_OUT, C_IN // GROUPS, K), dtype=jnp.float32)
        c_weight = jax.random.normal(k4, (C_OUT, C_DIM), dtype=jnp.float32)
        bias = jax.random.normal(k5, (C_OUT,), dtype=jnp.float32)
        return {'x': x, 'c': c, 'weight': weight, 'c_weight': c_weight, 'bias': bias}
    _L1_cond_all = _L1_cond_setup()
    _L1_cond_in = {k: v for k, v in _L1_cond_all.items() if k in ('weight', 'c_weight')}
    del _L1_cond_all

    def _L1_ffn_setup():
        import jax, jax.numpy as jnp
        import numpy as np
        M = 1024
        K = 1024

        def _make_2to4_mask(key, shape):
            scores = jax.random.normal(key, shape)
            g = scores.reshape(shape[0], shape[1] // 4, 4)
            rank = jnp.argsort(jnp.argsort(-jnp.abs(g), axis=-1), axis=-1)
            return (rank < 2).reshape(shape).astype(jnp.float32)
        key = jax.random.key(seed)
        k_x, k_w12, k_b12, k_w3, k_b3, k_m = jax.random.split(key, 6)
        x = jax.random.normal(k_x, (4, 512, K), dtype=jnp.float32)
        w12_dense = jax.random.normal(k_w12, (2 * M, K), dtype=jnp.float32) * (1.0 / np.sqrt(K))
        mask12 = _make_2to4_mask(k_m, (2 * M, K))
        w12 = w12_dense * mask12
        b12 = jax.random.normal(k_b12, (2 * M,), dtype=jnp.float32) * 0.01
        w3 = jax.random.normal(k_w3, (M, M), dtype=jnp.float32) * (1.0 / np.sqrt(M))
        b3 = jax.random.normal(k_b3, (M,), dtype=jnp.float32) * 0.01
        return {'x': x, 'w12': w12, 'b12': b12, 'w3': w3, 'b3': b3}
    _L1_ffn_all = _L1_ffn_setup()
    _L1_ffn_in = {k: v for k, v in _L1_ffn_all.items() if k in ('w12', 'b12', 'w3', 'b3')}
    del _L1_ffn_all
    return {'x': x, 'cond_128': cond_128, 'fside_S_0': fside_S_0, 'L0_cond_W0': _L0_cond_in['W0'], 'L0_cond_b0': _L0_cond_in['b0'], 'L0_cond_W1': _L0_cond_in['W1'], 'L0_cond_b1': _L0_cond_in['b1'], 'L0_cond_W2': _L0_cond_in['W2'], 'L0_cond_b2': _L0_cond_in['b2'], 'L0_cond_weight': _L0_cond_in['weight'], 'L0_cond_bias_k': _L0_cond_in['bias_k'], 'L0_ffn_gate': _L0_ffn_in['gate'], 'L0_ffn_kernel': _L0_ffn_in['kernel'], 'L0_ffn_bias': _L0_ffn_in['bias'], 'L0_ffn_lora_A': _L0_ffn_in['lora_A'], 'L0_ffn_lora_B': _L0_ffn_in['lora_B'], 'L0_ffn_lora_A_shared': _L0_ffn_in['lora_A_shared'], 'L0_ffn_lora_B_shared': _L0_ffn_in['lora_B_shared'], 'L1_cond_weight': _L1_cond_in['weight'], 'L1_cond_c_weight': _L1_cond_in['c_weight'], 'L1_ffn_w12': _L1_ffn_in['w12'], 'L1_ffn_b12': _L1_ffn_in['b12'], 'L1_ffn_w3': _L1_ffn_in['w3'], 'L1_ffn_b3': _L1_ffn_in['b3']}

def reference(x, cond_128, fside_S_0, L0_cond_W0, L0_cond_b0, L0_cond_W1, L0_cond_b1, L0_cond_W2, L0_cond_b2, L0_cond_weight, L0_cond_bias_k, L0_ffn_gate, L0_ffn_kernel, L0_ffn_bias, L0_ffn_lora_A, L0_ffn_lora_B, L0_ffn_lora_A_shared, L0_ffn_lora_B_shared, L1_cond_weight, L1_cond_c_weight, L1_ffn_w12, L1_ffn_b12, L1_ffn_w3, L1_ffn_b3):
    import jax
    import jax.numpy as jnp

    def _L0_cond_ref(x, embedding, W0, b0, W1, b1, W2, b2, weight, bias_k):
        import jax, jax.numpy as jnp
        import numpy as np
        K = 8
        T = 1.0
        D_EMBD = 128
        IN_C = 64
        OUT_C = 64
        BS = 32
        H = 1024
        HID = 128
        h = jax.nn.gelu(embedding @ W0 + b0, approximate=False)
        h = jax.nn.gelu(h @ W1 + b1, approximate=False)
        att = jax.nn.softmax((h @ W2 + b2) / T, axis=-1)
        agg_w = jnp.einsum('bk,koi->boi', att, weight[..., 0])
        agg_b = att @ bias_k
        out = jnp.einsum('boi,bih->boh', agg_w, x) + agg_b[:, :, None]
        return out

    def _L0_ffn_ref(x, gate, kernel, bias, lora_A, lora_B, lora_A_shared, lora_B_shared):
        import jax, jax.numpy as jnp
        import numpy as np
        B, T, D_IN, D_OUT = (8, 512, 1024, 1024)
        N_LORAS, RANK = (16, 32)
        SCALING = 1.0
        base_out = jnp.matmul(x, kernel) + bias
        b = gate.shape[0]
        x_flat = x.reshape(b, -1, x.shape[-1])
        A_eff = jnp.einsum('bn,nri->bri', gate, lora_A)
        B_eff = jnp.einsum('bn,nor->bor', gate, lora_B)
        Ax = jnp.einsum('bri,bti->btr', A_eff, x_flat)
        delta_flat = jnp.einsum('bor,btr->bto', B_eff, Ax)
        Ax_s = jnp.einsum('ri,bti->btr', lora_A_shared, x_flat)
        delta_flat = delta_flat + jnp.einsum('or,btr->bto', lora_B_shared, Ax_s)
        delta = delta_flat.reshape(x.shape[:-1] + (kernel.shape[-1],))
        return base_out + (SCALING * delta).astype(base_out.dtype)

    def _L1_cond_ref(x, c, weight, c_weight, bias):
        import jax, jax.numpy as jnp
        import numpy as np
        from jax import lax
        N, C_IN, L = (32, 64, 1024)
        C_OUT, K, GROUPS = (64, 9, 4)
        C_DIM, PAD, STRIDE = (128, 4, 1)
        out = lax.conv_general_dilated(x, weight, window_strides=(STRIDE,), padding=[(PAD, PAD)], dimension_numbers=('NCH', 'OIH', 'NCH'), feature_group_count=GROUPS)
        ctx = jnp.einsum('nd,od->no', c, c_weight)
        out = out + ctx[:, :, None] + bias[None, :, None]
        return out

    def _L1_ffn_ref(x, w12, b12, w3, b3):
        import jax, jax.numpy as jnp
        import numpy as np
        M = 1024
        K = 1024

        def _make_2to4_mask(key, shape):
            scores = jax.random.normal(key, shape)
            g = scores.reshape(shape[0], shape[1] // 4, 4)
            rank = jnp.argsort(jnp.argsort(-jnp.abs(g), axis=-1), axis=-1)
            return (rank < 2).reshape(shape).astype(jnp.float32)
        x12 = jnp.einsum('bsk,mk->bsm', x, w12) + b12
        x1, x2 = jnp.split(x12, 2, axis=-1)
        x4 = jax.nn.silu(x1) * x2
        return jnp.einsum('bsm,nm->bsn', x4, w3) + b3
    x = x + _L0_ffn_ref(_L0_cond_ref(x, cond_128, L0_cond_W0, L0_cond_b0, L0_cond_W1, L0_cond_b1, L0_cond_W2, L0_cond_b2, L0_cond_weight, L0_cond_bias_k), L0_ffn_gate, L0_ffn_kernel, L0_ffn_bias, L0_ffn_lora_A, L0_ffn_lora_B, L0_ffn_lora_A_shared, L0_ffn_lora_B_shared)
    x = x + _L1_ffn_ref(_L1_cond_ref(x, cond_128, L1_cond_weight, L1_cond_c_weight, fside_S_0), L1_ffn_w12, L1_ffn_b12, L1_ffn_w3, L1_ffn_b3)
    return x

_drawn_inputs = setup_inputs


def setup_inputs(seed=0):
    import zlib

    import numpy as np

    out = dict(_drawn_inputs(seed))
    spreads = {'L0_cond_b0': (0.0, 0.684),
     'L0_cond_b1': (0.0, 0.408),
     'L0_cond_b2': (0.0, 0.386),
     'L0_ffn_bias': (0.0, 0.1)}
    factors = {'L0_ffn_gate': 2.992,
     'L0_ffn_lora_A': 3.154,
     'L0_ffn_lora_B': 3.152,
     'L0_ffn_lora_A_shared': 3.193,
     'L0_ffn_lora_B_shared': 3.174,
     'L1_ffn_b12': 64.0,
     'L1_ffn_b3': 64.0}
    for name, (base, spread) in spreads.items():
        noise = np.random.default_rng([zlib.crc32(name.encode()), seed]).standard_normal(out[name].shape)
        drawn = base * np.exp(spread * noise) if base else spread * noise
        out[name] = jnp.asarray(drawn.astype(out[name].dtype))
    for name, factor in factors.items():
        out[name] = (out[name] * factor).astype(out[name].dtype)
    return out
```

```python
import numpy as np
import concourse.bass as bass
from concourse import mybir
from contextlib import ExitStack

F32 = mybir.dt.float32
F32R = mybir.dt.float32r
ALU = mybir.AluOpType
ACT = mybir.ActivationFunctionType
AX = mybir.AxisListType

P = 128
NB, NC, NL = 32, 64, 1024
ROWS = NB * NC
TILES = ROWS // P
KT = NL // P
HALF = 512
NE, ND = 8, 128
NG, ROWS_G = 8, ROWS // 8
TG = ROWS_G // P
NLORA, RANK = 16, 32
PH, BLK = 8, NL // 8
CG, GRP, TAPS = 16, 4, 9
PAD = TAPS // 2
RB = ROWS // HALF
NJ = NL // P


def layered_kernel(nc, x, cond, fside, c0_w0, c0_b0, c0_w1, c0_b1, c0_w2, c0_b2, c0_weight, c0_bias_k,
                   f0_gate, f0_kernel, f0_bias, lora_a, lora_b, lora_a_s, lora_b_s,
                   c1_weight, c1_c_weight, w12, b12, w3, b3, out):
    ds = bass.ds
    x_rows = x.rearrange("b c l -> (b c) l")
    out_rows = out.rearrange("b c l -> (b c) l")

    x1_dram = nc.dram_tensor("x1_scratch", [ROWS, NL], F32).ap()
    h_dram = nc.dram_tensor("h_scratch", [NJ, P, ROWS], F32).ap()
    mix_dram = nc.dram_tensor("mix_scratch", [NB, NC, NC], F32).ap()
    lb_dram = nc.dram_tensor("lora_b_scratch", [NG + 1, RANK, NL], F32).ap()

    ctx = ExitStack()
    with ctx:
        BASE = -(-nc.sbuf_base // 64) * 64

        def at(name, shape, kb, dt=F32):
            return nc.alloc_sbuf_tensor_at(name, shape, dt, offset=BASE + int(kb * 1024))

        def sem(name):
            return ctx.enter_context(nc.semaphore(name))

        wk_hi = at("wk_hi", [P, KT, NL], 0, F32R)
        wk_lo = at("wk_lo", [P, KT, NL], 32, F32R)
        NA = (NG + 1) * RANK
        la_hi = at("la_hi", [P, KT, NA], 64, F32R)
        la_lo = at("la_lo", [P, KT, NA], 73, F32R)
        la_g = [at(f"la_g{s}", [P, KT, P], 82.5 + 4 * s, F32R) for s in range(2)]
        y_hi = [at(f"y_hi{s}", [P, TG, KT, P], 96 + 16 * s, F32R) for s in range(2)]
        y_lo = [at(f"y_lo{s}", [P, TG, KT, P], 104 + 16 * s, F32R) for s in range(2)]
        x_in = [at(f"x_in{s}", [P, NL], 128 + 4 * s) for s in range(4)]
        x1_t = [at(f"x1_t{s}", [P, NL], 144.25 + 4 * s) for s in range(2)]
        y_f = [at(f"y_f{s}", [P, HALF], 152.25 + 2 * s) for s in range(2)]
        z_f = [at(f"z_f{s}", [P, ROWS_G], 156.25 + s) for s in range(2)]
        lb_g = [at(f"lb_g{s}", [P, NL], 158.25 + 4 * s) for s in range(2)]
        y_bias = at("y_bias", [P, ROWS], 166.25)
        mix = at("mix", [P, TILES, P], 174.25)
        c_bias = at("c_bias", [P, ROWS], 182.25)
        taps = at("taps", [P, GRP, 2, P], 190.25)
        f_bias = at("f_bias", [P, NL], 194.25)
        ident = at("ident", [P, P], 198.25)
        b12_s = at("b12_s", [P, 2, NJ], 198.75)
        b1_j = at("b1_j", [P, 1], 198.875)
        raw = [at(f"raw{s}", [P, NL], 199.75 + 4 * s) for s in range(2)]
        la_raw = at("la_raw", [P, GRP, NL], 96)
        lb_t = at("lb_t", [P, GRP, NL], 112)
        expert = at("expert", [NE, NC * NC], 48)
        mix_t = at("mix_t", [NB, NC, NC], 16)
        gate_e = at("gate_e", [P, 4, NG, RANK], 148.25)
        spread = at("spread", [P, ROWS], 158.25)
        lb_c = at("lb_c", [P, 2, NL], 158.25)
        wpad = at("wpad", [NC, 24, CG], 152.25)
        lbs_t = at("lbs_t", [RANK, NL], 152.25)
        cw_raw = at("cw_raw", [NC, ND], 156.25)
        w9_raw = at("w9_raw", [NC, CG, TAPS], 157.25)
        sel = at("sel", [NLORA, 4, P], 190.25)
        las_raw = at("las_raw", [RANK, NL], 140)
        ones = at("ones", [P, P], 136)
        w0_s = at("w0_s", [P, P], 136.5)
        w1_s = at("w1_s", [P, P], 137)
        emb_s = at("emb_s", [NB, ND], 137.5)
        emb_t = at("emb_t", [ND, NB], 138)
        cw_t = at("cw_t", [ND, NC], 138.125)
        biask_s = at("biask_s", [NE, NC], 138.375)
        fside_s = at("fside_s", [P, NC], 138.625)
        h1_s = at("h1_s", [P, NB], 138.875)
        h2_s = at("h2_s", [P, NB], 139)
        gate_c = at("gate_c", [P, 4 * NG], 139.125)
        m32 = at("m32", [P, RANK], 139.25)
        w2_s = at("w2_s", [P, NE], 139.375)
        gate_t = at("gate_t", [NLORA, NG], 139.40625)
        b0_s = at("b0_s", [P, 1], 139.4375)
        b1_s = at("b1_s", [P, 1], 139.46875)
        b2_s = at("b2_s", [NB, NE], 139.5)
        lg = at("lg", [NB, NE], 139.53125)
        ex = at("ex", [NB, NE], 139.5625)
        att = at("att", [NB, NE], 139.59375)
        nmax = at("nmax", [NB, 1], 139.625)
        esum = at("esum", [NB, 1], 139.65625)
        rsum = at("rsum", [NB, 1], 139.6875)
        att_t = at("att_t", [NE, NB], 139.75)
        c_hi = at("c_hi", [P, PH, ROWS], 0, F32R)
        c_lo = at("c_lo", [P, PH, ROWS], 64, F32R)
        x8 = [at(f"x8_{s}", [P, 4 * GRP, BLK + 1], 128 + 8.0625 * s) for s in range(2)]
        c_f = [at(f"c_f{s}", [P, HALF], 144.25 + 2 * s) for s in range(4)]
        w_t = [at(f"w_t{s}", [P, NL], 152.25 + 4 * s) for s in range(2)]
        w12_hi = [at("w12_hi0", [P, 2, PH, P], 166.25, F32R), at("w12_hi1", [P, 2, PH, P], 128, F32R)]
        w12_lo = [at("w12_lo0", [P, 2, PH, P], 174.25, F32R), at("w12_lo1", [P, 2, PH, P], 136, F32R)]
        silu_s = [at(f"silu_s{s}", [P, HALF], 144.25 + 2 * s) for s in range(2)]
        h_s = [at(f"h_s{s}", [P, HALF], k) for s, k in enumerate((148.25, 150.25, 160.25, 162.25))]
        w3_hi = [at("w3_hi0", [P, NJ, HALF], 166.25, F32R), at("w3_hi1", [P, NJ, HALF], 0, F32R)]
        w3_lo = [at("w3_lo0", [P, NJ, HALF], 182.25, F32R), at("w3_lo1", [P, NJ, HALF], 16, F32R)]
        h_in = [at(f"h_in{s}", [P, NJ, P], 32 + 4 * s) for s in range(2)]
        h_hi = [at(f"h_hi{s}", [P, NJ, P], 40 + 4 * s, F32R) for s in range(2)]
        h_lo = [at(f"h_lo{s}", [P, NJ, P], 48 + 4 * s, F32R) for s in range(2)]
        x1_in = [at(f"x1_in{s}", [P, NL], 56 + 4 * s) for s in range(2)]
        res = [at(f"res{s}", [P, NL], 64 + 4 * s) for s in range(2)]
        b3_s = at("b3_s", [P, NL], 72)

        ps = ctx.enter_context(nc.psum_tensor("ps", [P, 8 * HALF], F32))

        def bank(n, k=1):
            return ps[:, n * HALF:(n + k) * HALF]

        small_in = sem("small_in")
        la_in, las_in = sem("la_in"), sem("las_in")
        expert_in, fbias_in, b12_in = sem("expert_in"), sem("fbias_in"), sem("b12_in")
        raw_in = [sem(f"raw_in{s}") for s in range(2)]
        raw_free = sem("raw_free")
        x_loaded = [sem(f"x_loaded{s}") for s in range(4)]
        lb_loaded = [sem(f"lb_loaded{s}") for s in range(2)]
        consts_made = sem("consts_made")
        mix_zeroed, wpad_zeroed = sem("mix_zeroed"), sem("wpad_zeroed")
        setup_chain = sem("setup_chain")
        cond_t, cond_taken = sem("cond_t"), sem("cond_taken")
        h1_mm, h1_act, h2_mm, h2_act = sem("h1_mm"), sem("h1_act"), sem("h2_mm"), sem("h2_act")
        lg_mm, nmax_made, exp_made = sem("lg_mm"), sem("nmax_made"), sem("exp_made")
        att_made, att_mm, att_taken = sem("att_made"), sem("att_mm"), sem("att_taken")
        spread_made = sem("spread_made")
        wpad_made, taps_mm, taps_made = sem("wpad_made"), sem("taps_mm"), sem("taps_made")
        las_mm, las_hi_made, las_lo_made = sem("las_mm"), sem("las_hi_made"), sem("las_lo_made")
        gate_made = sem("gate_made")
        lb_turned = sem("lb_turned")
        ring_mm = sem("ring_mm")
        ring_taken = sem("ring_taken")
        la_hi_made = sem("la_hi_made")
        mix_stored, mix_loaded = sem("mix_stored"), sem("mix_loaded")
        lb_stored = sem("lb_stored")
        wk_hi_made, wk_lo_made = sem("wk_hi_made"), sem("wk_lo_made")
        la_gathered = sem("la_gathered")
        y_mm = sem("y_mm")
        y_taken = sem("y_taken")
        y_hi_made, y_lo_made = sem("y_hi_made"), sem("y_lo_made")
        z_mm, z_taken = sem("z_mm"), sem("z_taken")
        u_mm = sem("u_mm")
        xb_made = sem("xb_made")
        x1_made = sem("x1_made")
        x1_stored = [sem(f"x1_stored{s}") for s in range(2)]
        pads_made = sem("pads_made")
        x8_loaded = [sem(f"x8_loaded{s}") for s in range(2)]
        conv_mm = sem("conv_mm")
        c_taken = sem("c_taken")
        c_hi_made = sem("c_hi_made")
        c_lo_made = sem("c_lo_made")
        turned = sem("turned")
        w_hi_made, w_lo_made = sem("w_hi_made"), sem("w_lo_made")
        g1_mm = sem("g1_mm")
        g2_mm = sem("g2_mm")
        b1_made = sem("b1_made")
        silu_made = sem("silu_made")
        h_made = sem("h_made")
        h_stored = [sem(f"h_stored{s}") for s in range(RB)]
        b3_in = sem("b3_in")
        h_loaded = [sem(f"h_loaded{s}") for s in range(2)]
        x1_loaded = [sem(f"x1_loaded{s}") for s in range(2)]
        h_hi_made, h_lo_made = sem("h_hi_made"), sem("h_lo_made")
        res_made = sem("res_made")
        o_mm = sem("o_mm")
        out_made = sem("out_made")
        out_stored = [sem(f"out_stored{s}") for s in range(2)]

        N_SMALL = 12
        N_RING = 24
        N_RAW0 = 4 + 1 + KT
        W12_USES = 2 * NJ

        def raw_value(n):
            s = n % 2
            early = (N_RAW0 + 1 - s) // 2
            uses = n // 2 + 1
            return s, 16 * uses if n < N_RAW0 else 16 * early + 64 * (uses - early)

        def raw_value_w12(j, half):
            s, first = raw_value(N_RAW0 + half)
            return s, j * 64 + first

        block = ctx.enter_context(nc.Block())

        @block.sync
        def _(sp):
            def load_raw(n, src, rows=P):
                if n >= 2:
                    sp.wait_ge(raw_free, n - 1)
                sp.dma_start(raw[n % 2][0:rows, :], src).then_inc(raw_in[n % 2], 16)

            sp.dma_start(expert[:, :], c0_weight.rearrange("k o i a -> k (o i a)")).then_inc(expert_in, 16)
            sp.dma_start(la_raw[:, :, :], lora_a.rearrange("(k n) r i -> (n r) k i", k=4)).then_inc(la_in, 16)
            lb_v = lora_b.rearrange("(k n) (b o) r -> k (n b) (o r)", k=4, b=32)
            for k in range(4):
                load_raw(k, lb_v[k])
            load_raw(4, lora_b_s.rearrange("(b o) r -> b (o r)", b=32), rows=32)
            for t in range(2):
                sp.dma_start(x_in[t][:, :], x_rows[t * P:(t + 1) * P, :]).then_inc(x_loaded[t], 16)
            for k in range(KT):
                load_raw(5 + k, f0_kernel[k * P:(k + 1) * P, :])
            sp.wait_ge(ring_taken, N_RING)
            for t in range(2, 4):
                sp.dma_start(x_in[t][:, :], x_rows[t * P:(t + 1) * P, :]).then_inc(x_loaded[t], 16)

            def load_lb(g, s, first):
                for top in (0, 2 * RANK):
                    sp.dma_start(lb_g[s][top:top + RANK, :], lb_dram[g]).then_inc(lb_loaded[s], 16)
                    if first:
                        sp.dma_start(lb_g[s][top + RANK:top + 2 * RANK, :], lb_dram[NG]).then_inc(lb_loaded[s], 16)

            sp.wait_ge(lb_stored, 48)
            for g in range(2):
                load_lb(g, g, True)
            with sp.Fori(0, 3) as i:
                for k in range(4):
                    sp.wait_ge(xb_made, i * 4 + k + 3)
                    sp.dma_start(x_in[k][:, :], x_rows[ds((i * 4 + k + 4) * P, P), :]).then_inc(x_loaded[k], 16)
                    if k == 2:
                        sp.wait_ge(u_mm, i * 4 + 6)
                        for top in (0, 2 * RANK):
                            sp.dma_start(lb_g[0][top:top + RANK, :],
                                         lb_dram[ds(i * 2 + 2, 1), :, :].rearrange("a r n -> (a r) n")).then_inc(lb_loaded[0], 16)
                sp.wait_ge(u_mm, i * 4 + 8)
                for top in (0, 2 * RANK):
                    sp.dma_start(lb_g[1][top:top + RANK, :],
                                 lb_dram[ds(i * 2 + 3, 1), :, :].rearrange("a r n -> (a r) n")).then_inc(lb_loaded[1], 16)

            w12_v = w12.rearrange("(h m b j) l -> h j b m l", h=2, m=4, b=32, j=NJ)
            w3_v = w3.rearrange("(c m b) l -> c b m l", c=NJ, m=4, b=32)

            def load_w(n_free, s, src):
                sp.wait_ge(raw_free, n_free)
                for q in range(4):
                    dst = raw[s][32 * q:32 * q + 32, :].rearrange("b (m l) -> b m l", m=4)
                    sp.dma_start(dst, src(q)).then_inc(raw_in[s], 16)

            def load_w12(j):
                for half in range(2):
                    s, _ = raw_value(N_RAW0 + half)
                    load_w(N_RAW0 + half - 1 + j * 2, s,
                           lambda q: w12_v[half, j, :, :, 256 * q:256 * q + 256] if isinstance(j, int) else
                           w12_v[half, ds(j, 1), :, :, 256 * q:256 * q + 256].rearrange("a b m l -> (a b) m l"))

            def load_w3(c):
                n = N_RAW0 + W12_USES + c
                load_w(n - 1, n % 2, lambda q: w3_v[c, :, :, 256 * q:256 * q + 256])

            load_w12(0)
            x1_v = x1_dram.rearrange("(g c) e -> c g e", c=CG)

            def load_x8(cb, s):
                for p in range(PH):
                    q = (p + PAD) % PH
                    j0 = 1 if p >= PAD else 0
                    sp.dma_start(x8[s][q * CG:(q + 1) * CG, :, j0:j0 + BLK],
                                 x1_v[:, ds(cb * 4 * GRP, 4 * GRP), p * BLK:(p + 1) * BLK]).then_inc(x8_loaded[s], 16)

            sp.wait_ge(y_mm, 2 * TILES)
            sp.wait_ge(xb_made, TILES)
            for cb in range(2):
                for s in range(2):
                    sp.wait_ge(x1_stored[s], 16 * (cb + 1))
                load_x8(cb, cb)
            for s in range(2):
                sp.wait_ge(x1_stored[s], 16 * TILES // 2)
            with sp.Fori(0, 3) as i:
                for k in range(2):
                    sp.wait_ge(conv_mm, i * 8 + 4 * k + 4)
                    load_x8(i * 2 + 2 + k, k)

            load_w12(1)
            with sp.Fori(2, NJ) as j:
                load_w12(j)
            for c in range(NJ):
                load_w3(c)
                if c == 3:
                    sp.wait_ge(g2_mm, 4 + NJ * RB)
                    sp.dma_start(b3_s[:, :], b3.partition_broadcast(P)).then_inc(b3_in, 16)
                    for t in range(2):
                        sp.dma_start(x1_in[t][:, :], x1_dram[t * P:(t + 1) * P, :]).then_inc(x1_loaded[t], 16)
                    sp.wait_ge(h_stored[0], 16 * NJ)
                    for t in range(2):
                        sp.dma_start(h_in[t][:, :, :], h_dram[:, :, t * P:(t + 1) * P].rearrange("j p r -> p j r")).then_inc(h_loaded[t], 16)
            for rb in range(1, RB):
                sp.wait_ge(h_stored[rb], 16 * NJ)
            with sp.Fori(1, TILES // 2) as i:
                for s in range(2):
                    t = i * 2 + s
                    sp.wait_ge(h_lo_made, i * 2 + s - 1)
                    sp.dma_start(h_in[s][:, :, :], h_dram[:, :, ds(t * P, P)].rearrange("j p r -> p j r")).then_inc(h_loaded[s], 16)
                    sp.wait_ge(res_made, i * 2 + s - 1)
                    sp.dma_start(x1_in[s][:, :], x1_dram[ds(t * P, P), :]).then_inc(x1_loaded[s], 16)

        @block.gpsimd
        def _(pool):
            pool.memset(ident[:, :], 0.0).then_inc(consts_made, 1)
            pool.memset(sel[:, :, :], 0.0).then_inc(consts_made, 1)
            pool.memset(ones[:, :], 1.0).then_inc(consts_made, 1)
            pool.wait_ge(consts_made, 3)
            pool.affine_select(out=ident[:, :], in_=ident[:, :], compare_op=ALU.not_equal, fill=1.0,
                               base=0, pattern=[[-1, P]], channel_multiplier=1).then_inc(consts_made, 1)
            sel_v = sel[:, :, :].rearrange("n k (a r) -> n k a r", r=RANK)
            pool.affine_select(out=sel_v, in_=sel_v, compare_op=ALU.not_equal, fill=1.0,
                               base=0, pattern=[[-4, 4], [-1, 4], [0, RANK]], channel_multiplier=1).then_inc(consts_made, 1)
            pool.memset(wpad[:, :, :], 0.0).then_inc(wpad_zeroed, 1)
            pool.memset(mix[:, :, :], 0.0).then_inc(mix_zeroed, 1)

            pool.wait_ge(ring_taken, 16)
            pool.dma_start(mix_dram.rearrange("b i o -> b (i o)"), mix_t[:, :, :].rearrange("b i o -> b (i o)")).then_inc(mix_stored, 16)
            pool.wait_ge(mix_stored, 16)
            pool.wait_ge(mix_zeroed, 1)
            mix_v = mix_dram.rearrange("(t a) i o -> a i t o", a=2)
            for a in range(2):
                pool.dma_start(mix[a * NC:(a + 1) * NC, :, a * NC:(a + 1) * NC], mix_v[a]).then_inc(mix_loaded, 16)
            pool.wait_ge(ring_taken, N_RING)
            pool.dma_start(lb_dram[0:NG].rearrange("(k g) r n -> (g r) k n", k=2), lb_c[:, :, :]).then_inc(lb_stored, 16)
            pool.wait_ge(lb_turned, 5)
            pool.dma_start(lb_dram[NG], lbs_t[:, :]).then_inc(lb_stored, 32)

            def gather_la(g, s):
                for src, c0 in ((la_hi, 0), (la_lo, 2 * RANK)):
                    ins = pool.tensor_copy(la_g[s][:, :, c0:c0 + RANK], src[:, :, ds(g * RANK, RANK)].bitcast(F32))
                ins.then_inc(la_gathered, 1)

            pool.wait_ge(la_hi_made, 4)
            pool.wait_ge(las_hi_made, 1)
            pool.wait_ge(las_lo_made, 1)
            for s in range(2):
                for src, c0 in ((la_hi, RANK), (la_lo, 3 * RANK)):
                    pool.tensor_copy(la_g[s][:, :, c0:c0 + RANK], src[:, :, NG * RANK:].bitcast(F32))
                gather_la(s, s)

            fb_v = f_bias[:, :].rearrange("p (b q) -> p q b", q=PH)

            def x_plus_bias(slot, s):
                pool.tensor_tensor(x1_t[s][:, :].rearrange("p (q b) -> p q b", q=PH),
                                   x_in[slot][:, :].rearrange("p (b q) -> p q b", q=PH), fb_v, ALU.add).then_inc(xb_made, 1)

            def store_x1(t, s):
                pool.dma_start(x1_dram[ds(t * P, P), :], x1_t[s][:, :]).then_inc(x1_stored[s], 16)

            pool.wait_ge(fbias_in, 16)
            for t in range(2):
                pool.wait_ge(x_loaded[t], 16)
                x_plus_bias(t, t)
            with pool.Fori(0, 3) as i:
                for k in range(4):
                    pool.wait_ge(x1_made, i * 4 + k + 3)
                    store_x1(i * 4 + k, k % 2)
                    if k in (0, 3):
                        g = i * 2 + (2 if k == 0 else 3)
                        pool.wait_ge(z_mm, i * 2 + (1 if k == 0 else 2))
                        gather_la(g, 0 if k == 0 else 1)
                    pool.wait_ge(x1_stored[k % 2], i * 32 + 16 * (k // 2 + 1))
                    pool.wait_ge(x_loaded[(k + 2) % 4], i * 16 + (16 if k < 2 else 32))
                    x_plus_bias((k + 2) % 4, k % 2)
            for t in range(TILES - 4, TILES):
                pool.wait_ge(x1_made, t + 3)
                store_x1(t, t % 2)
                if t + 2 < TILES:
                    pool.wait_ge(x1_stored[t % 2], 16 * (t // 2 + 1))
                    pool.wait_ge(x_loaded[(t + 2) % 4], 16 * ((t + 2) // 4 + 1))
                    x_plus_bias((t + 2) % 4, t % 2)
                if t + 2 == TILES - 1:
                    pool.wait_ge(y_mm, 2 * TILES)
                    pool.wait_ge(xb_made, TILES)
                    for s in range(2):
                        pool.memset(x8[s][0:P // 2, :, 0:1], 0.0)
                        pool.memset(x8[s][P // 2:P, :, BLK:BLK + 1], 0.0).then_inc(pads_made, 1)

            with pool.Fori(0, NJ) as j:
                for rb in range(RB):
                    pool.wait_ge(h_made, j * 4 + rb + 5)
                    pool.dma_start(h_dram[ds(j, 1), :, rb * HALF:(rb + 1) * HALF].rearrange("a p r -> (a p) r"), h_s[rb][:, :]).then_inc(h_stored[rb], 16)

            pool.wait_ge(b3_in, 16)

            def residual(s, loaded, free):
                pool.wait_ge(x1_loaded[s], loaded)
                if free is not None:
                    pool.wait_ge(out_stored[s], free)
                pool.tensor_tensor(res[s][:, :].rearrange("p (b q) -> p q b", q=PH),
                                   x1_in[s][:, :].rearrange("p (q b) -> p q b", q=PH),
                                   b3_s[:, :].rearrange("p (b q) -> p q b", q=PH), ALU.add).then_inc(res_made, 1)

            def store_out(t, s, made):
                pool.wait_ge(out_made, made)
                pool.dma_start(out_rows[ds(t * P, P), :], res[s][:, :]).then_inc(out_stored[s], 16)

            for s in range(2):
                residual(s, 16, None)
            with pool.Fori(0, TILES // 2 - 1) as i:
                for s in range(2):
                    store_out(i * 2 + s, s, i * 2 + s + 3)
                    residual(s, i * 16 + 32, i * 16 + 16)
            for s in range(2):
                store_out(TILES - 2 + s, s, TILES - 2 + s + 3)
            for s in range(2):
                pool.wait_ge(out_stored[s], 16 * TILES // 2)

        @block.scalar
        def _(act):
            act.sem_inc(c_taken, 8)
            act.sem_inc(silu_made, 1)
            with nc.allow_non_contiguous_dma(reason="a few columns of small arrays"):
                act.dma_start(emb_s[:, :], cond).then_inc(small_in, 16)
                act.dma_start(w0_s[:, :], c0_w0).then_inc(small_in, 16)
                act.dma_start(cw_raw[:, :], c1_c_weight).then_inc(small_in, 16)
                act.dma_start(gate_t[:, :], f0_gate.rearrange("g n -> n g")).then_inc(small_in, 16)
                act.dma_start(b0_s[:, :], c0_b0.rearrange("(p a) -> p a", a=1)).then_inc(small_in, 16)
                act.dma_start(w1_s[:, :], c0_w1).then_inc(small_in, 16)
                act.dma_start(b1_s[:, :], c0_b1.rearrange("(p a) -> p a", a=1)).then_inc(small_in, 16)
                act.dma_start(w2_s[:, :], c0_w2).then_inc(small_in, 16)
                act.dma_start(b2_s[:, :], c0_b2.partition_broadcast(NB)).then_inc(small_in, 16)
                act.dma_start(w9_raw[:, :, :], c1_weight).then_inc(small_in, 16)
                act.dma_start(biask_s[:, :], c0_bias_k).then_inc(small_in, 16)
                act.dma_start(fside_s[:, :], fside.partition_broadcast(P)).then_inc(small_in, 16)
                act.dma_start(las_raw[:, :], lora_a_s).then_inc(las_in, 16)
                act.dma_start(f_bias[:, :], f0_bias.partition_broadcast(P)).then_inc(fbias_in, 16)
                act.dma_start(b12_s[:, :, :], b12.rearrange("(h p j) -> p h j", h=2, j=NJ)).then_inc(b12_in, 16)

            act.wait_ge(small_in, 16 * N_SMALL)
            act.wait_ge(h1_mm, 1)
            act.activation(h1_s[:, :], bank(0)[:, 160:192], ACT.Gelu, bias=b0_s[:, :]).then_inc(h1_act, 1)
            act.wait_ge(h2_mm, 1)
            act.activation(h2_s[:, :], bank(0)[:, 192:224], ACT.Gelu, bias=b1_s[:, :]).then_inc(h2_act, 1)
            act.wait_ge(nmax_made, 1)
            act.activation(ex[:, :], lg[:, :], ACT.Exp, bias=nmax[:, :], accum_out=esum[:, :]).then_inc(exp_made, 1)
            for n in range(4):
                act.wait_ge(ring_mm, 4 + n + 1)
                act.activation(la_hi[:, 2 * n:2 * n + 2, 0:NG * RANK],
                               bank(4 + n)[:, :].rearrange("p (a c) -> p a c", a=2), ACT.Copy).then_inc(la_hi_made, 1)
            act.wait_ge(las_mm, 1)
            act.activation(la_hi[:, :, NG * RANK:], bank(3)[:, 0:KT * RANK].rearrange("p (k r) -> p k r", r=RANK),
                           ACT.Copy).then_inc(las_hi_made, 1)
            for k in range(KT):
                if k == 4:
                    act.wait_ge(mix_stored, 16)
                s, value = raw_value(5 + k)
                act.wait_ge(raw_in[s], value)
                act.activation(wk_hi[:, k, :].rearrange("p (q b) -> p q b", q=PH),
                               raw[s][:, :].rearrange("p (b q) -> p q b", q=PH), ACT.Copy).then_inc(wk_hi_made, 1)

            def split_y(t, s, a):
                act.wait_ge(u_mm, t + 1)
                for h in range(2):
                    act.wait_ge(y_taken, t * 2 + h + 1)
                    act.activation(y_hi[s][:, a, 4 * h:4 * h + 4, :].rearrange("p k r -> p (k r)"),
                                   y_f[h][:, :], ACT.Copy).then_inc(y_hi_made, 1)

            act.wait_ge(ring_mm, N_RING)
            split_y(0, 0, 0)
            split_y(1, 0, 1)
            with act.Fori(0, 3) as i:
                for k in range(2, 6):
                    split_y(i * 4 + k, (k // 2) % 2, k % 2)
            for k in range(2, 4):
                split_y(TILES - 4 + k, 1, k % 2)

            def w12_hi_part(j, s, first=False):
                for half in range(2):
                    act.wait_ge(turned, j * 2 + half + 1)
                    if half == 0 and not first:
                        act.wait_ge(g2_mm, j * 4)
                    act.activation(w12_hi[s][:, half, :, :].rearrange("p q m -> p (q m)"), w_t[half][:, :],
                                   ACT.Copy).then_inc(w_hi_made, 1)

            w12_hi_part(0, 0, True)
            with act.Fori(0, 4) as i:
                for k in range(8):
                    act.wait_ge(c_taken, i * 8 + k + 9)
                    act.activation(c_hi[:, :, ds((i * 8 + k) * NC, NC)].rearrange("p q (g o) -> p q g o", g=GRP),
                                   c_f[k % 4][:, :].rearrange("p (g q o) -> p q g o", g=GRP, q=PH),
                                   ACT.Copy).then_inc(c_hi_made, 1)

            def silu(j, rb):
                if rb == 0:
                    act.wait_ge(silu_made, j * 4 + 1)
                    act.activation(b1_j[:, :], b12_s[:, 0, ds(j, 1)], ACT.Copy).then_inc(b1_made, 1)
                    act.wait_ge(b1_made, j + 1)
                act.wait_ge(g1_mm, j * 4 + rb + 1)
                act.wait_ge(h_made, j * 4 + rb + 3)
                act.activation(silu_s[rb % 2][:, :], bank(2 * rb), ACT.Silu, bias=b1_j[:, :]).then_inc(silu_made, 1)

            def w3_hi_part(c):
                half, col = c // 4, (c % 4) * P
                act.wait_ge(turned, W12_USES + c + 1)
                act.activation(w3_hi[half][:, :, col:col + P], w_t[c % 2][:, :].rearrange("p (j n) -> p j n", j=NJ),
                               ACT.Copy).then_inc(w_hi_made, 1)

            act.wait_ge(conv_mm, NB)
            act.wait_ge(b12_in, 16)
            with act.Fori(0, 3) as i:
                for k in range(2):
                    j = i * 2 + k
                    silu(j, 0)
                    w12_hi_part(i * 2 + k + 1, 1 - k)
                    for rb in range(1, RB):
                        silu(j, rb)
            silu(6, 0)
            w12_hi_part(7, 1)
            for rb in range(1, RB):
                silu(6, rb)
            silu(7, 0)
            for c in range(2):
                w3_hi_part(c)
            silu(7, 1)
            for c in range(2, 4):
                w3_hi_part(c)
            silu(7, 2)
            silu(7, 3)

            def h_hi_part(t, s, loaded):
                act.wait_ge(h_loaded[s], loaded)
                act.wait_ge(o_mm, t + 1)
                act.activation(h_hi[s][:, :, :], h_in[s][:, :, :], ACT.Copy).then_inc(h_hi_made, 1)

            act.wait_ge(g2_mm, 4 + NJ * RB)
            h_hi_part(0, 0, 16)
            for c in range(4, 8):
                w3_hi_part(c)
            h_hi_part(1, 1, 16)
            with act.Fori(1, TILES // 2) as i:
                for s in range(2):
                    h_hi_part(i * 2 + s, s, i * 16 + 16)

        @block.vector
        def _(dve):
            steps = [0]

            def link(ins):
                steps[0] += 1
                ins.then_inc(setup_chain, 1)
                dve.wait_ge(setup_chain, steps[0])

            dve.sem_inc(x1_made, 2)
            dve.sem_inc(c_lo_made, 4)
            dve.sem_inc(h_made, 4)
            dve.sem_inc(out_made, 2)

            dve.wait_ge(cond_t, 1)
            link(dve.tensor_copy(emb_t[:, :], bank(0)[:, 0:NB]))
            link(dve.tensor_copy(cw_t[:, :], bank(0)[:, 64:128]))
            dve.tensor_copy(gate_c[:, :], bank(0)[:, 128:160]).then_inc(cond_taken, 1)
            dve.tensor_tensor(spread[:, :].rearrange("d (b o) -> d b o", b=NB),
                              emb_t[:, :].unsqueeze(2).to_broadcast([ND, NB, NC]),
                              cw_t[:, :].unsqueeze(1).to_broadcast([ND, NB, NC]), ALU.mult).then_inc(spread_made, 1)
            link(dve.tensor_tensor(m32[:, :], ident[:, 0:32], ident[:, 32:64], ALU.add))
            link(dve.tensor_tensor(m32[:, :], m32[:, :], ident[:, 64:96], ALU.add))
            link(dve.tensor_tensor(m32[:, :], m32[:, :], ident[:, 96:128], ALU.add))
            dve.wait_ge(cond_taken, 1)
            dve.tensor_tensor(gate_e[:, :, :, :].rearrange("p k g r -> p (k g) r"),
                              gate_c[:, :].unsqueeze(2).to_broadcast([P, 4 * NG, RANK]),
                              m32[:, :].unsqueeze(1).to_broadcast([P, 4 * NG, RANK]), ALU.mult).then_inc(gate_made, 1)
            dve.wait_ge(wpad_zeroed, 1)
            dve.tensor_copy(wpad[:, 8:8 + TAPS, :], w9_raw[:, :, :].rearrange("o c k -> o k c")).then_inc(wpad_made, 1)
            for n in range(4):
                dve.wait_ge(ring_mm, n + 1)
                dve.tensor_tensor(c_bias[:, n * HALF:(n + 1) * HALF].rearrange("p (b o) -> p b o", o=NC),
                                  bank(4 + n).rearrange("p (b o) -> p b o", o=NC),
                                  fside_s[:, :].unsqueeze(1).to_broadcast([P, NB // 4, NC]), ALU.add).then_inc(ring_taken, 1)
            dve.wait_ge(taps_mm, 1)
            for half in range(2):
                last = dve.tensor_copy(taps[:, :, half, :].rearrange("p g (q o) -> p g q o", q=PH),
                                       bank(1 + half).rearrange("p (q g o) -> p g q o", q=PH, g=GRP))
            last.then_inc(taps_made, 1)
            dve.wait_ge(lg_mm, 1)
            link(dve.tensor_tensor(lg[:, :], bank(0)[0:NB, 224:232], b2_s[:, :], ALU.add))
            dve.reduce_max(nmax[:, :], lg[:, :], AX.X, negate=True).then_inc(nmax_made, 1)

            lb_tv = lb_t[:, :, :].rearrange("p k (b o) -> p k o b", b=32)

            def turn_lb(k):
                s, value = raw_value(k)
                dve.wait_ge(raw_in[s], value)
                dve.transpose(lb_tv[:, k], raw[s][:, :].rearrange("p (o r) -> p o r", r=RANK)).then_inc(raw_free, 1)

            turn_lb(0)
            turn_lb(1)
            dve.wait_ge(exp_made, 1)
            link(dve.reciprocal(rsum[:, :], esum[:, :]))
            dve.tensor_scalar(att[:, :], ex[:, :], rsum[:, :], None, ALU.mult).then_inc(att_made, 1)
            for n in range(4):
                dve.wait_ge(la_hi_made, n + 1)
                dve.tensor_tensor(la_lo[:, 2 * n:2 * n + 2, 0:NG * RANK], bank(4 + n).rearrange("p (a c) -> p a c", a=2),
                                  la_hi[:, 2 * n:2 * n + 2, 0:NG * RANK], ALU.subtract).then_inc(ring_taken, 1)
            dve.wait_ge(las_hi_made, 1)
            dve.tensor_tensor(la_lo[:, :, NG * RANK:], bank(3)[:, 0:KT * RANK].rearrange("p (k r) -> p k r", r=RANK),
                              la_hi[:, :, NG * RANK:], ALU.subtract).then_inc(las_lo_made, 1)
            dve.wait_ge(att_mm, 1)
            dve.tensor_copy(att_t[:, :], bank(0)[0:NE, 256:256 + NB]).then_inc(att_taken, 1)
            dve.wait_ge(att_taken, 1)
            dve.tensor_tensor(spread[0:NE, :].rearrange("d (b o) -> d b o", b=NB),
                              att_t[:, :].unsqueeze(2).to_broadcast([NE, NB, NC]),
                              biask_s[:, :].unsqueeze(1).to_broadcast([NE, NB, NC]), ALU.mult).then_inc(spread_made, 1)
            turn_lb(2)
            turn_lb(3)
            dve.wait_ge(taps_mm, 1)
            s, value = raw_value(4)
            dve.wait_ge(raw_in[s], value)
            dve.transpose(lbs_t[:, :].rearrange("p (q b o) -> p o q b", b=32, q=PH),
                          raw[s][0:32, :].rearrange("p (o q r) -> p o q r", r=RANK, q=PH)).then_inc(raw_free, 1)
            dve.wait_ge(raw_free, 5)
            dve.sem_inc(lb_turned, 5)
            for n in range(8):
                dve.wait_ge(ring_mm, 8 + n + 1)
                dve.tensor_copy(mix_t[:, :, 8 * n:8 * n + 8].rearrange("b i o -> b o i"),
                                bank(4 + n % 4)[0:NB, :].rearrange("b (o i) -> b o i", o=8)).then_inc(ring_taken, 1)
            for n in range(4):
                dve.wait_ge(ring_mm, 16 + n + 1)
                dve.tensor_copy(y_bias[:, n * HALF:(n + 1) * HALF], bank(4 + n)).then_inc(ring_taken, 1)
            for n in range(4):
                dve.wait_ge(ring_mm, 20 + n + 1)
                half = slice(n % 2 * BLK // 2, (n % 2 + 1) * BLK // 2)
                dve.tensor_copy(lb_c[:, n // 2, :].rearrange("p (q b) -> p b q", q=PH)[:, half, :],
                                bank(4 + n).rearrange("p (b q) -> p b q", q=PH)).then_inc(ring_taken, 1)

            for k in range(KT):
                s, value = raw_value(5 + k)
                dve.wait_ge(raw_in[s], value)
                dve.wait_ge(wk_hi_made, k + 1)
                dve.tensor_tensor(wk_lo[:, k, :].rearrange("p (q b) -> p q b", q=PH),
                                  raw[s][:, :].rearrange("p (b q) -> p q b", q=PH),
                                  wk_hi[:, k, :].rearrange("p (q b) -> p q b", q=PH), ALU.subtract).then_inc(wk_lo_made, 1)
                dve.wait_ge(wk_lo_made, k + 1)
                dve.sem_inc(raw_free, 1)

            def take_y(t, s, a, first=False):
                for h in range(2):
                    dve.wait_ge(y_mm, t * 2 + h + 1)
                    if not first:
                        dve.wait_ge(y_lo_made, t * 2 + h - 1)
                    dve.tensor_tensor(y_f[h][:, :].rearrange("p (k r) -> p k r", r=P),
                                      bank(h).rearrange("p (k r) -> p k r", r=P),
                                      y_bias[:, ds(t * P, P)].unsqueeze(1).to_broadcast([P, 4, P]), ALU.add).then_inc(y_taken, 1)
                for h in range(2):
                    dve.wait_ge(y_hi_made, t * 2 + h + 1)
                    dve.tensor_tensor(y_lo[s][:, a, 4 * h:4 * h + 4, :].rearrange("p k r -> p (k r)"),
                                      y_f[h][:, :], y_hi[s][:, a, 4 * h:4 * h + 4, :].rearrange("p k r -> p (k r)"),
                                      ALU.subtract).then_inc(y_lo_made, 1)

            def take_z(g, s, first=False):
                dve.wait_ge(z_mm, g + 1)
                if not first:
                    dve.wait_ge(u_mm, g * 2 + 2)
                dve.tensor_copy(z_f[s][:, :], bank(6)[:, 0:ROWS_G]).then_inc(z_taken, 1)

            def take_x1(t, s):
                dve.wait_ge(u_mm, t + 5)
                dve.wait_ge(xb_made, t + 1)
                dve.tensor_tensor(x1_t[s][:, :], bank(2 + 2 * s, 2), x1_t[s][:, :], ALU.add).then_inc(x1_made, 1)

            dve.wait_ge(lb_stored, 48)
            take_y(0, 0, 0, True)
            take_y(1, 0, 1)
            take_z(0, 0, True)
            with dve.Fori(0, 3) as i:
                for k in range(2):
                    t, g = i * 4 + 2 * k, i * 2 + k
                    take_y(t + 2, 1 - k, 0)
                    take_x1(t, 0)
                    take_y(t + 3, 1 - k, 1)
                    take_x1(t + 1, 1)
                    take_z(g + 1, 1 - k)
            take_y(14, 1, 0)
            take_x1(12, 0)
            take_y(15, 1, 1)
            take_x1(13, 1)
            take_z(7, 1)
            take_x1(14, 0)
            take_x1(15, 1)

            def turn(n_in, s, value, half, n_free):
                dve.wait_ge(raw_in[s], value)
                if n_free is not None:
                    dve.wait_ge(w_lo_made, n_free)
                dve.transpose(w_t[half][:, :].rearrange("p (q m b) -> p q m b", q=PH, m=4),
                              raw[s][:, :].rearrange("p (m a q) -> p q m a", m=4, q=PH)).then_inc(turned, 1)
                dve.wait_ge(turned, n_in)
                dve.sem_inc(raw_free, 1)

            def turn_w12(j, first=False):
                for half in range(2):
                    s, value = raw_value_w12(j, half)
                    turn(j * 2 + half + 1, s, value, half, None if first else j * 2 + half - 1)

            def w12_lo_part(j, s):
                for half in range(2):
                    dve.wait_ge(w_hi_made, j * 2 + half + 1)
                    dve.tensor_tensor(w12_lo[s][:, half, :, :].rearrange("p q m -> p (q m)"), w_t[half][:, :],
                                      w12_hi[s][:, half, :, :].rearrange("p q m -> p (q m)"), ALU.subtract).then_inc(w_lo_made, 1)

            def turn_w3(c):
                s, value = raw_value(N_RAW0 + W12_USES + c)
                turn(W12_USES + c + 1, s, value, c % 2, W12_USES + c - 1)

            def w3_lo_part(c):
                half, col = c // 4, (c % 4) * P
                dve.wait_ge(w_hi_made, W12_USES + c + 1)
                dve.tensor_tensor(w3_lo[half][:, :, col:col + P], w_t[c % 2][:, :].rearrange("p (j n) -> p j n", j=NJ),
                                  w3_hi[half][:, :, col:col + P], ALU.subtract).then_inc(w_lo_made, 1)

            turn_w12(0, True)
            w12_lo_part(0, 0)

            for s in range(2):
                dve.wait_ge(x1_stored[s], 16 * TILES // 2)

            def c_lo_part(b, s):
                dve.wait_ge(c_hi_made, b + 1)
                dve.tensor_tensor(c_lo[:, :, ds(b * NC, NC)],
                                  c_f[s][:, :].rearrange("p (g q o) -> p q g o", g=GRP, q=PH),
                                  c_hi[:, :, ds(b * NC, NC)].rearrange("p q (g o) -> p q g o", g=GRP),
                                  ALU.subtract).then_inc(c_lo_made, 1)

            def c_lo_part4(b, s):
                dve.wait_ge(c_hi_made, b + 1)
                dve.tensor_tensor(c_lo[:, :, ds(b * NC, NC)].rearrange("p q (g o) -> p q g o", g=GRP),
                                  c_f[s][:, :].rearrange("p (g q o) -> p q g o", g=GRP, q=PH),
                                  c_hi[:, :, ds(b * NC, NC)].rearrange("p q (g o) -> p q g o", g=GRP),
                                  ALU.subtract).then_inc(c_lo_made, 1)

            with dve.Fori(0, 4) as i:
                for k in range(8):
                    b = i * 8 + k
                    dve.wait_ge(conv_mm, b + 1)
                    dve.wait_ge(c_lo_made, b + 1)
                    dve.tensor_tensor(c_f[k % 4][:, :].rearrange("p (g q o) -> p g q o", g=GRP, q=PH),
                                      bank(k).rearrange("p (g q o) -> p g q o", g=GRP, q=PH),
                                      c_bias[:, ds(b * NC, NC)].rearrange("p (g o) -> p g o", g=GRP)
                                      .unsqueeze(2).to_broadcast([P, GRP, PH, CG]), ALU.add).then_inc(c_taken, 1)
                    if k:
                        c_lo_part4(b - 1, (k - 1) % 4)
                c_lo_part4(i * 8 + 7, 3)

            def hidden(j, rb):
                dve.wait_ge(g2_mm, j * 4 + rb + 5)
                dve.wait_ge(silu_made, j * 4 + rb + 2)
                if not (isinstance(j, int) and j == 0):
                    dve.wait_ge(h_stored[rb], j * 16)
                dve.scalar_tensor_tensor(out=h_s[rb][:, :], in0=bank(2 * rb + 1), scalar=b12_s[:, 1, ds(j, 1)],
                                         in1=silu_s[rb % 2][:, :], op0=ALU.add, op1=ALU.mult).then_inc(h_made, 1)

            dve.wait_ge(b12_in, 16)

            def gate_steps(i):
                for k in range(2):
                    j = i * 2 + k
                    hidden(j, 0)
                    turn_w12(j + 1)
                    hidden(j, 1)
                    w12_lo_part(j + 1, 1 - k)
                    hidden(j, 2)
                    hidden(j, 3)

            gate_steps(0)
            with dve.Fori(1, 3) as i:
                gate_steps(i)
            hidden(6, 0)
            turn_w12(7)
            hidden(6, 1)
            w12_lo_part(7, 1)
            hidden(6, 2)
            hidden(6, 3)
            hidden(7, 0)
            turn_w3(0)
            turn_w3(1)
            hidden(7, 1)
            w3_lo_part(0)
            w3_lo_part(1)
            turn_w3(2)
            turn_w3(3)
            hidden(7, 2)
            w3_lo_part(2)
            w3_lo_part(3)
            turn_w3(4)
            turn_w3(5)
            hidden(7, 3)

            def h_lo_part(t, s):
                dve.wait_ge(h_hi_made, t + 1)
                dve.tensor_tensor(h_lo[s][:, :, :], h_in[s][:, :, :], h_hi[s][:, :, :], ALU.subtract).then_inc(h_lo_made, 1)

            def take_out(t, s):
                dve.wait_ge(o_mm, t + 3)
                dve.wait_ge(res_made, t + 1)
                dve.tensor_tensor(res[s][:, :], bank(2 * s, 2), res[s][:, :], ALU.add).then_inc(out_made, 1)

            h_lo_part(0, 0)
            w3_lo_part(4)
            w3_lo_part(5)
            turn_w3(6)
            turn_w3(7)
            w3_lo_part(6)
            w3_lo_part(7)
            h_lo_part(1, 1)
            with dve.Fori(1, TILES // 2) as i:
                for s in range(2):
                    take_out(i * 2 + s - 2, s)
                    h_lo_part(i * 2 + s, s)
            for s in range(2):
                take_out(TILES - 2 + s, s)

        @block.tensor
        def _(pe):
            pe.sem_inc(u_mm, 4)
            pe.sem_inc(g2_mm, 4)
            pe.sem_inc(o_mm, 2)

            def mm(o, l, r, start, stop):
                return pe.matmul(o, l, r, start=start, stop=stop)

            def products(o, l_hi, l_lo, r_hi, r_lo, first, last):
                for n, (l, r) in enumerate(((l_hi, r_hi), (l_hi, r_lo), (l_lo, r_hi))):
                    for dst, src in zip(o, r):
                        ins = mm(dst, l, src, first and n == 0, last and n == 2)
                return ins

            pe.wait_ge(consts_made, 5)
            pe.wait_ge(small_in, 16 * N_SMALL)
            pe.transpose(bank(0)[:, 0:NB], emb_s[:, :], ident[0:NB, 0:NB])
            pe.transpose(bank(0)[:, 64:128], cw_raw[:, :], ident[0:NC, 0:NC])
            for k in range(4):
                last = mm(bank(0)[:, 128 + NG * k:128 + NG * (k + 1)], sel[:, k, :], gate_t[:, :], True, True)
            last.then_inc(cond_t, 1)
            pe.wait_ge(cond_taken, 1)
            mm(bank(0)[:, 160:192], w0_s[:, :], emb_t[:, :], True, True).then_inc(h1_mm, 1)

            ring = [0]

            def ring_bank():
                n = ring[0]
                ring[0] += 1
                if n >= 4:
                    pe.wait_ge(ring_taken, n - 3)
                return bank(4 + n % 4)

            pe.wait_ge(spread_made, 1)
            for n in range(4):
                mm(ring_bank(), ones[:, :], spread[:, n * HALF:(n + 1) * HALF], True, True).then_inc(ring_mm, 1)
            pe.wait_ge(h1_act, 1)
            mm(bank(0)[:, 192:224], w1_s[:, :], h1_s[:, :], True, True).then_inc(h2_mm, 1)
            pe.wait_ge(wpad_made, 1)
            for half in range(2):
                for q in range(PH):
                    k0 = 8 + 8 * half - q
                    last = pe.transpose(bank(1 + half)[:, q * NC:(q + 1) * NC],
                                        wpad[:, k0:k0 + PH, :].rearrange("o k c -> o (k c)"), ident[0:NC, 0:NC])
            last.then_inc(taps_mm, 1)
            pe.wait_ge(h2_act, 1)
            mm(bank(0)[0:NB, 224:232], h2_s[:, :], w2_s[:, :], True, True).then_inc(lg_mm, 1)
            pe.wait_ge(las_in, 16)
            for k in range(KT):
                last = pe.transpose(bank(3)[:, k * RANK:(k + 1) * RANK], las_raw[:, k * P:(k + 1) * P], ident[0:RANK, 0:RANK])
            last.then_inc(las_mm, 1)
            pe.wait_ge(gate_made, 1)
            pe.wait_ge(la_in, 16)
            for n in range(4):
                dst = ring_bank()
                for a in range(2):
                    for k in range(4):
                        c0 = (2 * n + a) * P
                        last = mm(dst[:, a * ROWS_G:(a + 1) * ROWS_G], la_raw[:, k, c0:c0 + P],
                                  gate_e[:, k, :, :].rearrange("p g r -> p (g r)"), k == 0, k == 3)
                last.then_inc(ring_mm, 1)
            pe.wait_ge(att_made, 1)
            pe.transpose(bank(0)[0:NE, 256:256 + NB], att[:, :], ident[0:NB, 0:NB]).then_inc(att_mm, 1)
            pe.wait_ge(att_taken, 1)
            pe.wait_ge(expert_in, 16)
            for n in range(8):
                mm(ring_bank()[0:NB, :], att_t[:, :], expert[:, n * HALF:(n + 1) * HALF], True, True).then_inc(ring_mm, 1)
            pe.wait_ge(spread_made, 2)
            for n in range(4):
                mm(ring_bank(), ones[0:NE, :], spread[0:NE, n * HALF:(n + 1) * HALF], True, True).then_inc(ring_mm, 1)
            pe.wait_ge(raw_free, 4)
            for n in range(4):
                dst = ring_bank()
                for k in range(4):
                    last = mm(dst, gate_e[:, k, 4 * (n // 2):4 * (n // 2) + 4, :].rearrange("p g r -> p (g r)"),
                              lb_t[:, k, (n % 2) * HALF:(n % 2 + 1) * HALF], k == 0, k == 3)
                last.then_inc(ring_mm, 1)

            def y_tile(t, slot, loaded, first=False):
                pe.wait_ge(x_loaded[slot], loaded)
                for h in range(2):
                    if not first:
                        pe.wait_ge(y_taken, t * 2 + h - 1)
                    for k in range(4):
                        c0 = (4 * h + k) * P
                        last = mm(bank(h)[:, k * P:(k + 1) * P], x_in[slot][:, c0:c0 + P],
                                  mix[:, ds(t, 1), :].rearrange("p a r -> p (a r)"), True, True)
                    last.then_inc(y_mm, 1)

            def z_group(g, s, first=False):
                pe.wait_ge(la_gathered, g + 1)
                pe.wait_ge(y_lo_made, g * 4 + 4)
                if not first:
                    pe.wait_ge(z_taken, g)
                dst = bank(6)[:, 0:ROWS_G]
                for k in range(KT):
                    mm(dst, la_g[s][:, k, :], y_hi[s][:, :, k, :], k == 0, False)
                    last = mm(dst, la_g[s][:, k, :], y_lo[s][:, :, k, :], False, k == KT - 1)
                last.then_inc(z_mm, 1)

            def u_tile(t, s, a, lb_value):
                pe.wait_ge(y_lo_made, t * 2 + 2)
                pe.wait_ge(x1_made, t + 1)
                dst = [bank(2 + 2 * a), bank(3 + 2 * a)]
                for k in range(KT):
                    products(dst, y_hi[s][:, a, k, :], y_lo[s][:, a, k, :],
                             [wk_hi[:, k, 0:HALF], wk_hi[:, k, HALF:]], [wk_lo[:, k, 0:HALF], wk_lo[:, k, HALF:]],
                             k == 0, False)
                if a == 0:
                    pe.wait_ge(lb_loaded[s], lb_value)
                return dst

            def u_lora(dst, t, s, a, g):
                pe.wait_ge(z_taken, g + 1)
                for half in range(2):
                    last = mm(dst[half], z_f[s][:, a * P:(a + 1) * P],
                              lb_g[s][:, half * HALF:(half + 1) * HALF], False, True)
                last.then_inc(u_mm, 1)

            pe.wait_ge(mix_loaded, 32)
            y_tile(0, 0, 16, True)
            y_tile(1, 1, 16)
            z_group(0, 0, True)
            pe.wait_ge(wk_lo_made, KT)
            with pe.Fori(0, 3) as i:
                for k in range(2):
                    t, g = i * 4 + 2 * k, i * 2 + k
                    y_tile(t + 2, (2 * k + 2) % 4, i * 16 + (16 if k == 0 else 32))
                    u_lora(u_tile(t, k, 0, i * 32 + 64), t, k, 0, g)
                    y_tile(t + 3, (2 * k + 3) % 4, i * 16 + (16 if k == 0 else 32))
                    u_lora(u_tile(t + 1, k, 1, None), t + 1, k, 1, g)
                    z_group(g + 1, 1 - k)
            y_tile(14, 2, 64)
            u_lora(u_tile(12, 0, 0, 160), 12, 0, 0, 6)
            y_tile(15, 3, 64)
            u_lora(u_tile(13, 0, 1, None), 13, 0, 1, 6)
            z_group(7, 1)
            u_lora(u_tile(14, 1, 0, 160), 14, 1, 0, 7)
            u_lora(u_tile(15, 1, 1, None), 15, 1, 1, 7)

            pe.wait_ge(taps_made, 1)
            pe.wait_ge(pads_made, 2)
            pe.wait_ge(x1_made, TILES + 2)
            with pe.Fori(0, 4) as i:
                for k in range(8):
                    if k % 4 == 0:
                        pe.wait_ge(x8_loaded[k // 4], i * 128 + 128)
                    pe.wait_ge(c_taken, i * 8 + k + 1)
                    for g in range(GRP):
                        src, dst = x8[k // 4][:, (k % 4) * GRP + g, :], bank(k)[:, g * P:(g + 1) * P]
                        mm(dst, src[:, 0:BLK], taps[:, g, 0, :], True, False)
                        last = mm(dst, src[:, 1:BLK + 1], taps[:, g, 1, :], False, True)
                    last.then_inc(conv_mm, 1)

            def gate_step(j, s):
                pe.wait_ge(w_lo_made, j * 2 + 2)
                for rb in range(RB):
                    pe.wait_ge(h_made, j * 4 + rb + 1)
                    cols = slice(rb * HALF, (rb + 1) * HALF)
                    for half, done in ((0, g1_mm), (1, g2_mm)):
                        for q in range(PH):
                            last = products([bank(2 * rb + half)], w12_hi[s][:, half, q, :], w12_lo[s][:, half, q, :],
                                            [c_hi[:, q, cols]], [c_lo[:, q, cols]], q == 0, q == PH - 1)
                        last.then_inc(done, 1)

            pe.wait_ge(c_lo_made, NB + 4)
            pe.wait_ge(c_taken, NB + 8)
            with pe.Fori(0, NJ // 2) as i:
                for k in range(2):
                    gate_step(i * 2 + k, k)

            def out_tile(t, s, first=False):
                pe.wait_ge(h_lo_made, t + 1)
                pe.wait_ge(out_made, t + 1)
                for half in range(2):
                    if first:
                        pe.wait_ge(w_lo_made, W12_USES + 4 * (half + 1))
                    for j in range(NJ):
                        last = products([bank(2 * s + half)], h_hi[s][:, j, :], h_lo[s][:, j, :],
                                        [w3_hi[half][:, j, :]], [w3_lo[half][:, j, :]], j == 0, j == NJ - 1)
                last.then_inc(o_mm, 1)

            pe.wait_ge(h_made, 4 + 4 * (NJ - 1) + 2)
            out_tile(0, 0, True)
            out_tile(1, 1)
            with pe.Fori(1, TILES // 2) as i:
                for s in range(2):
                    out_tile(i * 2 + s, s)


_INS = ['x', 'cond_128', 'fside_S_0', 'L0_cond_W0', 'L0_cond_b0', 'L0_cond_W1', 'L0_cond_b1', 'L0_cond_W2', 'L0_cond_b2',
        'L0_cond_weight', 'L0_cond_bias_k', 'L0_ffn_gate', 'L0_ffn_kernel', 'L0_ffn_bias', 'L0_ffn_lora_A',
        'L0_ffn_lora_B', 'L0_ffn_lora_A_shared', 'L0_ffn_lora_B_shared', 'L1_cond_weight', 'L1_cond_c_weight',
        'L1_ffn_w12', 'L1_ffn_b12', 'L1_ffn_w3', 'L1_ffn_b3']


def kernel(**inputs):
    import concourse.bacc as bacc
    from concourse.bass_utils import run_bass_kernel_spmd

    nc = bacc.Bacc("TRN2", target_bir_lowering=False, num_devices=1)
    arrays, args = {}, []
    for name in _INS:
        a = np.ascontiguousarray(inputs[name])
        arrays[f"in_{name}"] = a
        args.append(nc.dram_tensor(f"in_{name}", a.shape, mybir.dt.from_np(a.dtype), kind="ExternalInput").ap())
    out = nc.dram_tensor("out", (NB, NC, NL), F32, kind="ExternalOutput").ap()
    layered_kernel(nc, *args, out)
    r = run_bass_kernel_spmd(nc, [arrays], core_ids=[0])
    return r.results[0]["out"]
```

```python
import numpy as np
import concourse.bass as bass
from concourse import mybir
from contextlib import ExitStack

F32 = mybir.dt.float32
F32R = mybir.dt.float32r
ALU = mybir.AluOpType
ACT = mybir.ActivationFunctionType
AX = mybir.AxisListType

P = 128
NB, NC, NL = 32, 64, 1024
ROWS = NB * NC
TILES = ROWS // P
KT = NL // P
HALF = 512
NE, ND = 8, 128
NG, ROWS_G = 8, ROWS // 8
TG = ROWS_G // P
NLORA, RANK = 16, 32
PH, BLK = 8, NL // 8
CG, GRP, TAPS = 16, 4, 9
PAD = TAPS // 2
RB = ROWS // HALF
NJ = NL // P


def layered_kernel(nc, x, cond, fside, c0_w0, c0_b0, c0_w1, c0_b1, c0_w2, c0_b2, c0_weight, c0_bias_k,
                   f0_gate, f0_kernel, f0_bias, lora_a, lora_b, lora_a_s, lora_b_s,
                   c1_weight, c1_c_weight, w12, b12, w3, b3, out):
    ds = bass.ds
    x_rows = x.rearrange("b c l -> (b c) l")
    out_rows = out.rearrange("b c l -> (b c) l")

    x1_dram = nc.dram_tensor("x1_scratch", [ROWS, NL], F32).ap()
    h_dram = nc.dram_tensor("h_scratch", [NJ, P, ROWS], F32).ap()
    mix_dram = nc.dram_tensor("mix_scratch", [NB, NC, NC], F32).ap()
    lb_dram = nc.dram_tensor("lora_b_scratch", [NG + 1, RANK, NL], F32).ap()
    bias_dram = nc.dram_tensor("bias_scratch", [2, ROWS], F32).ap()

    ctx = ExitStack()
    with ctx:
        BASE = -(-nc.sbuf_base // 64) * 64

        def at(name, shape, kb, dt=F32):
            return nc.alloc_sbuf_tensor_at(name, shape, dt, offset=BASE + int(kb * 1024))

        def sem(name):
            return ctx.enter_context(nc.semaphore(name))

        wk_hi = at("wk_hi", [P, KT, NL], 0, F32R)
        wk_lo = at("wk_lo", [P, KT, NL], 32, F32R)
        NA = (NG + 1) * RANK
        la_hi = at("la_hi", [P, KT, NA], 64, F32R)
        la_lo = at("la_lo", [P, KT, NA], 73, F32R)
        la_g = [at(f"la_g{s}", [P, KT, P], 82.5 + 4 * s, F32R) for s in range(2)]
        y_hi = [at(f"y_hi{s}", [P, TG, KT, P], 96 + 16 * s, F32R) for s in range(2)]
        y_lo = [at(f"y_lo{s}", [P, TG, KT, P], 104 + 16 * s, F32R) for s in range(2)]
        x_in = [at(f"x_in{s}", [P, NL], 128 + 4 * s) for s in range(4)]
        x1_t = [at(f"x1_t{s}", [P, NL], 144.25 + 4 * s) for s in range(2)]
        y_f = [at(f"y_f{s}", [P, HALF], 152.25 + 2 * s) for s in range(2)]
        z_f = [at(f"z_f{s}", [P, ROWS_G], 156.25 + s) for s in range(2)]
        lb_g = [at(f"lb_g{s}", [P, NL], 158.25 + 4 * s) for s in range(2)]
        y_bias = at("y_bias", [P, ROWS], 166.25)
        mix = at("mix", [P, TILES, P], 174.25)
        c_bias = at("c_bias", [P, ROWS], 182.25)
        taps = at("taps", [P, GRP, 2, P], 190.25)
        f_bias = at("f_bias", [P, NL], 194.25)
        ident = at("ident", [P, P], 198.25)
        b12_s = at("b12_s", [P, 2, NJ], 198.75)
        b1_j = at("b1_j", [P, 1], 198.875)
        raw = [at(f"raw{s}", [P, NL], k) for s, k in enumerate((199.75, 203.75, 91, 144.25))]
        la_raw = at("la_raw", [P, GRP, NL], 96)
        lb_t = at("lb_t", [P, GRP, NL], 112)
        expert = at("expert", [NE, NC * NC], 48)
        mix_t = at("mix_t", [NB, NC, NC], 16)
        gate_e = at("gate_e", [P, 4, NG, RANK], 148.25)
        lb_c = at("lb_c", [P, 2, NL], 158.25)
        wpad = at("wpad", [NC, 24, CG], 152.25)
        lbs_t = at("lbs_t", [RANK, NL], 152.25)
        cw_raw = at("cw_raw", [NC, ND], 156.25)
        w9_raw = at("w9_raw", [NC, CG, TAPS], 157.25)
        sel = at("sel", [NLORA, 4, P], 190.25)
        las_raw = at("las_raw", [RANK, NL], 186.25)
        small = iter(range(int(182.25 * 32), int(186.25 * 32)))

        def tiny(name, shape):
            k = next(small)
            for _ in range(-(-4 * shape[1] // 32) - 1):
                next(small)
            return at(name, shape, k / 32)

        w0_s, w1_s = tiny("w0_s", [P, P]), tiny("w1_s", [P, P])
        emb_s, emb_t = tiny("emb_s", [NB, ND]), tiny("emb_t", [ND, NB])
        cw_t, biask_s = tiny("cw_t", [ND, NC]), tiny("biask_s", [NE, NC])
        fside_s = tiny("fside_s", [NB, NC])
        yb_c, cb_c = tiny("yb_c", [NB, NC]), tiny("cb_c", [NB, NC])
        h1_s, h2_s = tiny("h1_s", [P, NB]), tiny("h2_s", [P, NB])
        gate_c, m32 = tiny("gate_c", [P, 4 * NG]), tiny("m32", [P, RANK])
        w2_s, gate_t = tiny("w2_s", [P, NE]), tiny("gate_t", [NLORA, NG])
        b0_s, b1_s, b2_s = tiny("b0_s", [P, 1]), tiny("b1_s", [P, 1]), tiny("b2_s", [NB, NE])
        lg, ex, att = tiny("lg", [NB, NE]), tiny("ex", [NB, NE]), tiny("att", [NB, NE])
        nmax, esum, rsum = tiny("nmax", [NB, 1]), tiny("esum", [NB, 1]), tiny("rsum", [NB, 1])
        att_t = tiny("att_t", [NE, NB])
        c_hi = at("c_hi", [P, RB, PH, HALF], 0, F32R)
        c_lo = at("c_lo", [P, RB, PH, HALF], 64, F32R)
        x8 = [at(f"x8_{s}", [P, 4 * GRP, BLK + 1], 128 + 8.0625 * s) for s in range(2)]
        c_f = [at(f"c_f{s}", [P, HALF], 144.25 + 2 * s) for s in range(4)]
        w_t = [at(f"w_t{s}", [P, NL], 152.25 + 4 * s) for s in range(2)]
        w12_hi = [at("w12_hi0", [P, 2, PH, P], 166.25, F32R), at("w12_hi1", [P, 2, PH, P], 128, F32R)]
        w12_lo = [at("w12_lo0", [P, 2, PH, P], 174.25, F32R), at("w12_lo1", [P, 2, PH, P], 136, F32R)]
        silu_s = [at(f"silu_s{s}", [P, HALF], 144.25 + 2 * s) for s in range(2)]
        h_s = [at(f"h_s{s}", [P, HALF], k) for s, k in enumerate((148.25, 150.25, 160.25, 162.25))]
        w3_hi = [at("w3_hi0", [P, NJ, HALF], 166.25, F32R), at("w3_hi1", [P, NJ, HALF], 32, F32R)]
        w3_lo = [at("w3_lo0", [P, NJ, HALF], 182.25, F32R), at("w3_lo1", [P, NJ, HALF], 96, F32R)]
        h_in = [at(f"h_in{s}", [P, NJ, P], 4 * s) for s in range(2)]
        h_hi = [at(f"h_hi{s}", [P, NJ, P], 8 + 4 * s, F32R) for s in range(2)]
        h_lo = [at(f"h_lo{s}", [P, NJ, P], 64 + 4 * s, F32R) for s in range(2)]
        x1_in = [at(f"x1_in{s}", [P, NL], 72 + 4 * s) for s in range(2)]
        res = [at(f"res{s}", [P, NL], 16 + 4 * s) for s in range(2)]
        b3_s = at("b3_s", [P, NL], 24)

        ps = ctx.enter_context(nc.psum_tensor("ps", [P, 8 * HALF], F32))

        def bank(n, k=1):
            return ps[:, n * HALF:(n + k) * HALF]

        cond_in = sem("cond_in")
        mlp_in = sem("mlp_in")
        small_in = sem("small_in")
        gate_in, la_in, las_in = sem("gate_in"), sem("la_in"), sem("las_in")
        expert_in, fbias_in, b12_in = sem("expert_in"), sem("fbias_in"), sem("b12_in")
        raw_in = [sem(f"raw_in{s}") for s in range(4)]
        raw_free = sem("raw_free")
        w_in = [sem(f"w_in{s}") for s in range(2)]
        w_free = sem("w_free")
        x_loaded = [sem(f"x_loaded{s}") for s in range(4)]
        lb_loaded = [sem(f"lb_loaded{s}") for s in range(2)]
        consts_made = sem("consts_made")
        mix_zeroed, wpad_zeroed = sem("mix_zeroed"), sem("wpad_zeroed")
        setup_chain = sem("setup_chain")
        cond_t, emb_taken = sem("cond_t"), sem("emb_taken")
        gate_mm, gate_taken = sem("gate_mm"), sem("gate_taken")
        h1_mm, h1_act, h2_mm, h2_act = sem("h1_mm"), sem("h1_act"), sem("h2_mm"), sem("h2_act")
        lg_mm, nmax_made, exp_made = sem("lg_mm"), sem("nmax_made"), sem("exp_made")
        att_made, att_mm, att_taken = sem("att_made"), sem("att_mm"), sem("att_taken")
        bias_mm, bias_made = sem("bias_mm"), sem("bias_made")
        bias_stored, bias_loaded = sem("bias_stored"), sem("bias_loaded")
        c_bias_loaded = sem("c_bias_loaded")
        wpad_made, taps_mm, taps_made = sem("wpad_made"), sem("taps_mm"), sem("taps_made")
        las_mm, las_hi_made, las_lo_made = sem("las_mm"), sem("las_hi_made"), sem("las_lo_made")
        gate_made = sem("gate_made")
        lb_turned = sem("lb_turned")
        ring_mm = sem("ring_mm")
        ring_taken = sem("ring_taken")
        la_hi_made = sem("la_hi_made")
        mix_stored, mix_loaded = sem("mix_stored"), sem("mix_loaded")
        lb_stored = sem("lb_stored")
        wk_hi_made, wk_lo_made = sem("wk_hi_made"), sem("wk_lo_made")
        la_gathered = sem("la_gathered")
        y_mm = sem("y_mm")
        y_taken = sem("y_taken")
        y_hi_made, y_lo_made = sem("y_hi_made"), sem("y_lo_made")
        z_mm, z_taken = sem("z_mm"), sem("z_taken")
        u_mm = sem("u_mm")
        xb_made = sem("xb_made")
        x1_made = sem("x1_made")
        x1_stored = [sem(f"x1_stored{s}") for s in range(2)]
        pads_made = sem("pads_made")
        x8_loaded = [sem(f"x8_loaded{s}") for s in range(2)]
        conv_mm = sem("conv_mm")
        c_taken = sem("c_taken")
        c_hi_made = sem("c_hi_made")
        c_lo_made = sem("c_lo_made")
        turned = sem("turned")
        w_hi_made, w_lo_made = sem("w_hi_made"), sem("w_lo_made")
        g1_mm = sem("g1_mm")
        g2_mm = sem("g2_mm")
        b1_made = sem("b1_made")
        silu_made = sem("silu_made")
        h_made = sem("h_made")
        h_stored = [sem(f"h_stored{s}") for s in range(RB)]
        b3_in = sem("b3_in")
        h_loaded = [sem(f"h_loaded{s}") for s in range(2)]
        x1_loaded = [sem(f"x1_loaded{s}") for s in range(2)]
        h_hi_made, h_lo_made = sem("h_hi_made"), sem("h_lo_made")
        res_made = sem("res_made")
        o_mm = sem("o_mm")
        out_made = sem("out_made")
        out_stored = [sem(f"out_stored{s}") for s in range(2)]

        N_RING = 16
        RAW_LBS, RAW_WK = 4, 5
        W12_USES = 2 * NJ

        block = ctx.enter_context(nc.Block())

        @block.sync
        def _(sp):
            def load_raw(n, src, rows=P):
                if n >= 4:
                    sp.wait_ge(raw_free, n - 3)
                sp.dma_start(raw[n % 4][0:rows, :], src).then_inc(raw_in[n % 4], 16)

            with nc.allow_non_contiguous_dma(reason="a gate of 8 x 16"):
                sp.dma_start(gate_t[:, :], f0_gate.rearrange("g n -> n g")).then_inc(gate_in, 16)
            sp.dma_start(la_raw[:, :, :], lora_a.rearrange("(k n) r i -> (n r) k i", k=4)).then_inc(la_in, 16)
            sp.dma_start(expert[:, :], c0_weight.rearrange("k o i a -> k (o i a)")).then_inc(expert_in, 16)
            lb_v = lora_b.rearrange("(k n) (b o) r -> k (n b) (o r)", k=4, b=32)
            for k in range(4):
                load_raw(k, lb_v[k])
            for t in range(2):
                sp.dma_start(x_in[t][:, :], x_rows[t * P:(t + 1) * P, :]).then_inc(x_loaded[t], 16)
            load_raw(RAW_LBS, lora_b_s.rearrange("(b o) r -> b (o r)", b=32), rows=32)
            for k in range(KT):
                load_raw(RAW_WK + k, f0_kernel[k * P:(k + 1) * P, :])
            for t in range(2, 4):
                sp.dma_start(x_in[t][:, :], x_rows[t * P:(t + 1) * P, :]).then_inc(x_loaded[t], 16)

            def store_x1(t, s, made):
                sp.wait_ge(x1_made, made)
                sp.dma_start(x1_dram[ds(t * P, P), :], x1_t[s][:, :]).then_inc(x1_stored[s], 16)

            def load_lb(g, s, first):
                for top in (0, 2 * RANK):
                    sp.dma_start(lb_g[s][top:top + RANK, :], lb_dram[g]).then_inc(lb_loaded[s], 16)
                    if first:
                        sp.dma_start(lb_g[s][top + RANK:top + 2 * RANK, :], lb_dram[NG]).then_inc(lb_loaded[s], 16)

            sp.wait_ge(lb_stored, 32)
            for g in range(2):
                load_lb(g, g, True)
            with sp.Fori(0, 3) as i:
                for k in range(4):
                    store_x1(i * 4 + k, k % 2, i * 4 + k + 3)
                    sp.wait_ge(xb_made, i * 4 + k + 3)
                    sp.dma_start(x_in[k][:, :], x_rows[ds((i * 4 + k + 4) * P, P), :]).then_inc(x_loaded[k], 16)
                    if k == 2:
                        sp.wait_ge(u_mm, i * 4 + 6)
                        for top in (0, 2 * RANK):
                            sp.dma_start(lb_g[0][top:top + RANK, :],
                                         lb_dram[ds(i * 2 + 2, 1), :, :].rearrange("a r n -> (a r) n")).then_inc(lb_loaded[0], 16)
                sp.wait_ge(u_mm, i * 4 + 8)
                for top in (0, 2 * RANK):
                    sp.dma_start(lb_g[1][top:top + RANK, :],
                                 lb_dram[ds(i * 2 + 3, 1), :, :].rearrange("a r n -> (a r) n")).then_inc(lb_loaded[1], 16)

            w12_v = w12.rearrange("(h m b j) l -> h j b m l", h=2, m=4, b=32, j=NJ)
            w3_v = w3.rearrange("(c m b) l -> c b m l", c=NJ, m=4, b=32)

            def load_w(s, src):
                for q in range(4):
                    dst = raw[s][32 * q:32 * q + 32, :].rearrange("b (m l) -> b m l", m=4)
                    sp.dma_start(dst, src(q)).then_inc(w_in[s], 16)

            def load_w12(j):
                for half in range(2):
                    if isinstance(j, int):
                        load_w(half, lambda q: w12_v[half, j, :, :, 256 * q:256 * q + 256])
                    else:
                        sp.wait_ge(w_free, j * 2 + half - 1)
                        load_w(half, lambda q: w12_v[half, ds(j, 1), :, :, 256 * q:256 * q + 256]
                               .rearrange("a b m l -> (a b) m l"))

            def load_w3(c):
                sp.wait_ge(w_free, W12_USES + c - 1)
                load_w(c % 2, lambda q: w3_v[c, :, :, 256 * q:256 * q + 256])

            x1_v = x1_dram.rearrange("(g c) e -> c g e", c=CG)

            def load_x8(cb, s):
                for p in range(PH):
                    q = (p + PAD) % PH
                    j0 = 1 if p >= PAD else 0
                    sp.dma_start(x8[s][q * CG:(q + 1) * CG, :, j0:j0 + BLK],
                                 x1_v[:, ds(cb * 4 * GRP, 4 * GRP), p * BLK:(p + 1) * BLK]).then_inc(x8_loaded[s], 16)

            store_x1(TILES - 4, 0, TILES - 1)
            store_x1(TILES - 3, 1, TILES)
            sp.wait_ge(raw_free, RAW_WK + KT)
            load_w12(0)
            sp.wait_ge(y_mm, 2 * TILES)
            sp.wait_ge(xb_made, TILES)
            for cb in range(2):
                for s in range(2):
                    sp.wait_ge(x1_stored[s], 16 * (cb + 1))
                load_x8(cb, cb)
            store_x1(TILES - 2, 0, TILES + 1)
            store_x1(TILES - 1, 1, TILES + 2)
            for s in range(2):
                sp.wait_ge(x1_stored[s], 16 * TILES // 2)
            with sp.Fori(0, 3) as i:
                for k in range(2):
                    sp.wait_ge(conv_mm, i * 8 + 4 * k + 4)
                    load_x8(i * 2 + 2 + k, k)

            def store_h(j, rb):
                sp.wait_ge(h_made, j * 4 + rb + 5)
                sp.dma_start(h_dram[ds(j, 1), :, rb * HALF:(rb + 1) * HALF].rearrange("a p r -> (a p) r"),
                             h_s[rb][:, :]).then_inc(h_stored[rb], 16)

            with sp.Fori(0, NJ - 1) as j:
                load_w12(j + 1)
                for rb in range(RB):
                    store_h(j, rb)

            def load_h(t, s):
                sp.dma_start(h_in[s][:, :, :], h_dram[:, :, ds(t * P, P)].rearrange("j p r -> p j r")).then_inc(h_loaded[s], 16)

            def load_x1(t, s):
                sp.dma_start(x1_in[s][:, :], x1_dram[ds(t * P, P), :]).then_inc(x1_loaded[s], 16)

            load_w3(0)
            load_w3(1)
            store_h(NJ - 1, 0)
            load_w3(2)
            load_w3(3)
            sp.wait_ge(g2_mm, 4 * NJ + 1)
            sp.wait_ge(h_stored[0], 16 * NJ)
            for t in range(2):
                load_h(t, t)
                load_x1(t, t)
            store_h(NJ - 1, 1)
            load_w3(4)
            load_w3(5)
            sp.wait_ge(g2_mm, 4 * NJ + 2)
            sp.dma_start(b3_s[:, :], b3.partition_broadcast(P)).then_inc(b3_in, 16)
            store_h(NJ - 1, 2)
            load_w3(6)
            load_w3(7)
            store_h(NJ - 1, 3)
            for rb in range(1, RB):
                sp.wait_ge(h_stored[rb], 16 * NJ)

            def store_out(t, s, made, cols=slice(0, NL)):
                sp.wait_ge(out_made, made)
                sp.dma_start(out_rows[ds(t * P, P), cols], res[s][:, cols]).then_inc(out_stored[s], 16)

            with sp.Fori(1, TILES // 2) as i:
                for s in range(2):
                    sp.wait_ge(h_lo_made, i * 2 + s - 1)
                    load_h(i * 2 + s, s)
                    sp.wait_ge(res_made, i * 2 + s - 1)
                    load_x1(i * 2 + s, s)
                    store_out(i * 2 + s - 2, s, i * 4 + 2 * s + 2)
            store_out(TILES - 2, 0, 2 * TILES + 2)
            for half in range(2):
                store_out(TILES - 1, 1, 2 * TILES + 3 + half, slice(half * HALF, (half + 1) * HALF))
            sp.wait_ge(out_stored[0], 16 * TILES // 2)
            sp.wait_ge(out_stored[1], 16 * TILES // 2 + 16)

        @block.gpsimd
        def _(pool):
            pool.memset(ident[:, :], 0.0).then_inc(consts_made, 1)
            pool.wait_ge(consts_made, 1)
            pool.affine_select(out=ident[:, :], in_=ident[:, :], compare_op=ALU.not_equal, fill=1.0,
                               base=0, pattern=[[-1, P]], channel_multiplier=1).then_inc(consts_made, 1)
            pool.memset(sel[:, :, :], 0.0).then_inc(consts_made, 1)
            pool.wait_ge(consts_made, 3)
            sel_v = sel[:, :, :].rearrange("n k (a r) -> n k a r", r=RANK)
            pool.affine_select(out=sel_v, in_=sel_v, compare_op=ALU.not_equal, fill=1.0,
                               base=0, pattern=[[-4, 4], [-1, 4], [0, RANK]], channel_multiplier=1).then_inc(consts_made, 1)
            pool.memset(wpad[:, :, :], 0.0).then_inc(wpad_zeroed, 1)
            pool.memset(mix[:, :, :], 0.0).then_inc(mix_zeroed, 1)

            pool.wait_ge(bias_made, 2)
            for n, src in enumerate((yb_c, cb_c)):
                pool.dma_start(bias_dram[n].rearrange("(b o) -> b o", o=NC), src[:, :]).then_inc(bias_stored, 16)
            pool.wait_ge(bias_stored, 32)
            pool.dma_start(y_bias[:, :], bias_dram[0].partition_broadcast(P)).then_inc(bias_loaded, 16)
            pool.wait_ge(ring_taken, 12)
            pool.dma_start(mix_dram.rearrange("b i o -> b (i o)"), mix_t[:, :, :].rearrange("b i o -> b (i o)")).then_inc(mix_stored, 16)
            pool.wait_ge(mix_stored, 16)
            pool.wait_ge(mix_zeroed, 1)
            mix_v = mix_dram.rearrange("(t a) i o -> a i t o", a=2)
            for a in range(2):
                pool.dma_start(mix[a * NC:(a + 1) * NC, :, a * NC:(a + 1) * NC], mix_v[a]).then_inc(mix_loaded, 16)
            pool.wait_ge(lb_turned, 5)
            pool.dma_start(lb_dram[NG], lbs_t[:, :]).then_inc(lb_stored, 16)
            def gather_la(g, s):
                for src, c0 in ((la_hi, 0), (la_lo, 2 * RANK)):
                    ins = pool.tensor_copy(la_g[s][:, :, c0:c0 + RANK], src[:, :, ds(g * RANK, RANK)].bitcast(F32))
                ins.then_inc(la_gathered, 1)

            pool.wait_ge(la_hi_made, 4)
            pool.wait_ge(las_hi_made, 1)
            pool.wait_ge(las_lo_made, 1)
            for s in range(2):
                for src, c0 in ((la_hi, RANK), (la_lo, 3 * RANK)):
                    pool.tensor_copy(la_g[s][:, :, c0:c0 + RANK], src[:, :, NG * RANK:].bitcast(F32))
                gather_la(s, s)
            pool.wait_ge(ring_taken, N_RING)
            pool.dma_start(lb_dram[0:NG].rearrange("(k g) r n -> (g r) k n", k=2), lb_c[:, :, :]).then_inc(lb_stored, 16)

            fb_v = f_bias[:, :].rearrange("p (b q) -> p q b", q=PH)

            def x_plus_bias(slot, s):
                pool.tensor_tensor(x1_t[s][:, :].rearrange("p (q b) -> p q b", q=PH),
                                   x_in[slot][:, :].rearrange("p (b q) -> p q b", q=PH), fb_v, ALU.add).then_inc(xb_made, 1)

            pool.wait_ge(fbias_in, 16)
            pool.wait_ge(wk_lo_made, KT)
            for t in range(2):
                pool.wait_ge(x_loaded[t], 16)
                x_plus_bias(t, t)
            pool.dma_start(c_bias[:, :], bias_dram[1].partition_broadcast(P)).then_inc(c_bias_loaded, 16)
            with pool.Fori(0, 3) as i:
                for k in range(4):
                    if k in (0, 3):
                        g = i * 2 + (2 if k == 0 else 3)
                        pool.wait_ge(z_mm, i * 2 + (1 if k == 0 else 2))
                        gather_la(g, 0 if k == 0 else 1)
                    pool.wait_ge(x1_stored[k % 2], i * 32 + 16 * (k // 2 + 1))
                    pool.wait_ge(x_loaded[(k + 2) % 4], i * 16 + (16 if k < 2 else 32))
                    x_plus_bias((k + 2) % 4, k % 2)
            for t in range(TILES - 4, TILES - 2):
                pool.wait_ge(x1_stored[t % 2], 16 * (t // 2 + 1))
                pool.wait_ge(x_loaded[(t + 2) % 4], 16 * ((t + 2) // 4 + 1))
                x_plus_bias((t + 2) % 4, t % 2)
            pool.wait_ge(y_mm, 2 * TILES)
            pool.wait_ge(xb_made, TILES)
            for s in range(2):
                pool.memset(x8[s][0:P // 2, :, 0:1], 0.0)
                pool.memset(x8[s][P // 2:P, :, BLK:BLK + 1], 0.0).then_inc(pads_made, 1)

            pool.wait_ge(b3_in, 16)

            def residual(s, loaded, free):
                pool.wait_ge(x1_loaded[s], loaded)
                if free is not None:
                    pool.wait_ge(out_stored[s], free)
                pool.tensor_tensor(res[s][:, :].rearrange("p (b q) -> p q b", q=PH),
                                   x1_in[s][:, :].rearrange("p (q b) -> p q b", q=PH),
                                   b3_s[:, :].rearrange("p (b q) -> p q b", q=PH), ALU.add).then_inc(res_made, 1)

            for s in range(2):
                residual(s, 16, None)
            with pool.Fori(0, TILES // 2 - 1) as i:
                for s in range(2):
                    residual(s, i * 16 + 32, i * 16 + 16)

        @block.scalar
        def _(act):
            act.sem_inc(c_taken, 8)
            act.sem_inc(silu_made, 1)
            act.dma_start(emb_s[:, :], cond).then_inc(cond_in, 16)
            act.dma_start(w0_s[:, :], c0_w0).then_inc(cond_in, 16)
            with nc.allow_non_contiguous_dma(reason="a few columns of small arrays"):
                act.dma_start(b0_s[:, :], c0_b0.rearrange("(p a) -> p a", a=1)).then_inc(cond_in, 16)
                act.dma_start(w1_s[:, :], c0_w1).then_inc(mlp_in, 16)
                act.dma_start(b1_s[:, :], c0_b1.rearrange("(p a) -> p a", a=1)).then_inc(mlp_in, 16)
                act.dma_start(w2_s[:, :], c0_w2).then_inc(mlp_in, 16)
                act.dma_start(b2_s[:, :], c0_b2.partition_broadcast(NB)).then_inc(mlp_in, 16)
                act.dma_start(biask_s[:, :], c0_bias_k).then_inc(small_in, 16)
                act.dma_start(cw_raw[:, :], c1_c_weight).then_inc(small_in, 16)
                act.dma_start(fside_s[:, :], fside.partition_broadcast(NB)).then_inc(small_in, 16)
                act.dma_start(w9_raw[:, :, :], c1_weight).then_inc(small_in, 16)
                act.dma_start(las_raw[:, :], lora_a_s).then_inc(las_in, 16)

            def la_hi_part(n):
                act.wait_ge(ring_mm, n + 1)
                act.activation(la_hi[:, 2 * n:2 * n + 2, 0:NG * RANK],
                               bank(4 + n)[:, :].rearrange("p (a c) -> p a c", a=2), ACT.Copy).then_inc(la_hi_made, 1)

            act.wait_ge(cond_in, 48)
            act.wait_ge(h1_mm, 1)
            act.activation(h1_s[:, :], bank(0)[:, 64:96], ACT.Gelu, bias=b0_s[:, :]).then_inc(h1_act, 1)
            la_hi_part(0)
            act.wait_ge(mlp_in, 64)
            act.wait_ge(h2_mm, 1)
            act.activation(h2_s[:, :], bank(0)[:, 96:128], ACT.Gelu, bias=b1_s[:, :]).then_inc(h2_act, 1)
            la_hi_part(1)
            act.wait_ge(nmax_made, 1)
            act.activation(ex[:, :], lg[:, :], ACT.Exp, bias=nmax[:, :], accum_out=esum[:, :]).then_inc(exp_made, 1)
            la_hi_part(2)
            la_hi_part(3)
            with nc.allow_non_contiguous_dma(reason="a few columns of small arrays"):
                act.dma_start(f_bias[:, :], f0_bias.partition_broadcast(P)).then_inc(fbias_in, 16)
                act.dma_start(b12_s[:, :, :], b12.rearrange("(h p j) -> p h j", h=2, j=NJ)).then_inc(b12_in, 16)
            act.wait_ge(las_mm, 1)
            act.wait_ge(setup_chain, 6)
            act.activation(la_hi[:, :, NG * RANK:], bank(1)[:, 256:512].rearrange("p (k r) -> p k r", r=RANK),
                           ACT.Copy).then_inc(las_hi_made, 1)
            for k in range(KT):
                if k == 4:
                    act.wait_ge(mix_stored, 16)
                n = RAW_WK + k
                act.wait_ge(raw_in[n % 4], 16 * (n // 4 + 1))
                act.activation(wk_hi[:, k, :].rearrange("p (q b) -> p q b", q=PH),
                               raw[n % 4][:, :].rearrange("p (b q) -> p q b", q=PH), ACT.Copy).then_inc(wk_hi_made, 1)

            def split_y(t, s, a):
                act.wait_ge(u_mm, t + 1)
                for h in range(2):
                    act.wait_ge(y_taken, t * 2 + h + 1)
                    act.activation(y_hi[s][:, a, 4 * h:4 * h + 4, :].rearrange("p k r -> p (k r)"),
                                   y_f[h][:, :], ACT.Copy).then_inc(y_hi_made, 1)

            act.wait_ge(ring_mm, N_RING)
            split_y(0, 0, 0)
            split_y(1, 0, 1)
            with act.Fori(0, 3) as i:
                for k in range(2, 6):
                    split_y(i * 4 + k, (k // 2) % 2, k % 2)
            for k in range(2, 4):
                split_y(TILES - 4 + k, 1, k % 2)

            def w12_hi_part(j, s, first=False):
                for half in range(2):
                    act.wait_ge(turned, j * 2 + half + 1)
                    if half == 0 and not first:
                        act.wait_ge(g2_mm, j * 4)
                    act.activation(w12_hi[s][:, half, :, :].rearrange("p q m -> p (q m)"), w_t[half][:, :],
                                   ACT.Copy).then_inc(w_hi_made, 1)

            w12_hi_part(0, 0, True)
            with act.Fori(0, 4) as i:
                for k in range(8):
                    act.wait_ge(c_taken, i * 8 + k + 9)
                    act.activation(c_hi[:, ds(i, 1), :, k * NC:(k + 1) * NC].rearrange("p a q (g o) -> p (a q) g o", g=GRP),
                                   c_f[k % 4][:, :].rearrange("p (g q o) -> p q g o", g=GRP, q=PH),
                                   ACT.Copy).then_inc(c_hi_made, 1)

            def silu(j, rb):
                if rb == 0:
                    act.wait_ge(silu_made, j * 4 + 1)
                    act.activation(b1_j[:, :], b12_s[:, 0, ds(j, 1)], ACT.Copy).then_inc(b1_made, 1)
                    act.wait_ge(b1_made, j + 1)
                act.wait_ge(g1_mm, j * 4 + rb + 1)
                act.wait_ge(h_made, j * 4 + rb + 3)
                act.activation(silu_s[rb % 2][:, :], bank(2 * rb), ACT.Silu, bias=b1_j[:, :]).then_inc(silu_made, 1)

            def w3_hi_part(c):
                half, col = c // 4, (c % 4) * P
                act.wait_ge(turned, W12_USES + c + 1)
                act.activation(w3_hi[half][:, :, col:col + P], w_t[c % 2][:, :].rearrange("p (j n) -> p j n", j=NJ),
                               ACT.Copy).then_inc(w_hi_made, 1)

            act.wait_ge(conv_mm, NB)
            act.wait_ge(b12_in, 16)
            with act.Fori(0, 3) as i:
                for k in range(2):
                    j = i * 2 + k
                    silu(j, 0)
                    w12_hi_part(i * 2 + k + 1, 1 - k)
                    for rb in range(1, RB):
                        silu(j, rb)
            silu(6, 0)
            w12_hi_part(7, 1)
            for rb in range(1, RB):
                silu(6, rb)
            silu(7, 0)
            w3_hi_part(0)
            w3_hi_part(1)
            silu(7, 1)
            w3_hi_part(2)
            w3_hi_part(3)

            def h_hi_part(t, s, loaded):
                act.wait_ge(h_loaded[s], loaded)
                act.wait_ge(o_mm, t * 2 + 2)
                act.activation(h_hi[s][:, :, :], h_in[s][:, :, :], ACT.Copy).then_inc(h_hi_made, 1)

            h_hi_part(0, 0, 16)
            silu(7, 2)
            h_hi_part(1, 1, 16)
            act.wait_ge(g2_mm, 4 * NJ + 3)
            for c in range(4, 8):
                w3_hi_part(c)
            silu(7, 3)
            with act.Fori(1, TILES // 2) as i:
                for s in range(2):
                    h_hi_part(i * 2 + s, s, i * 16 + 16)

        @block.vector
        def _(dve):
            steps = [0]

            def link(ins):
                steps[0] += 1
                ins.then_inc(setup_chain, 1)
                dve.wait_ge(setup_chain, steps[0])

            dve.sem_inc(x1_made, 2)
            dve.sem_inc(c_lo_made, 4)
            dve.sem_inc(h_made, 4)
            dve.sem_inc(out_made, 4)

            dve.wait_ge(consts_made, 2)
            link(dve.tensor_tensor(m32[:, :], ident[:, 0:32], ident[:, 32:64], ALU.add))
            link(dve.tensor_tensor(m32[:, :], m32[:, :], ident[:, 64:96], ALU.add))
            link(dve.tensor_tensor(m32[:, :], m32[:, :], ident[:, 96:128], ALU.add))
            dve.wait_ge(cond_t, 1)
            dve.tensor_copy(emb_t[:, :], bank(0)[:, 0:NB]).then_inc(emb_taken, 1)
            dve.wait_ge(gate_mm, 1)
            dve.tensor_copy(gate_c[:, :], bank(1)[:, 0:32]).then_inc(gate_taken, 1)
            dve.wait_ge(gate_taken, 1)
            dve.tensor_tensor(gate_e[:, :, :, :].rearrange("p k g r -> p (k g) r"),
                              gate_c[:, :].unsqueeze(2).to_broadcast([P, 4 * NG, RANK]),
                              m32[:, :].unsqueeze(1).to_broadcast([P, 4 * NG, RANK]), ALU.mult).then_inc(gate_made, 1)

            lb_tv = lb_t[:, :, :].rearrange("p k (b o) -> p k o b", b=32)

            def turn_lb(k):
                dve.wait_ge(raw_in[k % 4], 16)
                dve.transpose(lb_tv[:, k], raw[k % 4][:, :].rearrange("p (o r) -> p o r", r=RANK)).then_inc(raw_free, 1)

            def la_lo_part(n):
                dve.wait_ge(la_hi_made, n + 1)
                dve.tensor_tensor(la_lo[:, 2 * n:2 * n + 2, 0:NG * RANK], bank(4 + n).rearrange("p (a c) -> p a c", a=2),
                                  la_hi[:, 2 * n:2 * n + 2, 0:NG * RANK], ALU.subtract).then_inc(ring_taken, 1)

            dve.wait_ge(wpad_zeroed, 1)
            dve.wait_ge(small_in, 64)
            dve.tensor_copy(wpad[:, 8:8 + TAPS, :], w9_raw[:, :, :].rearrange("o c k -> o k c")).then_inc(wpad_made, 1)
            la_lo_part(0)
            la_lo_part(1)
            dve.wait_ge(lg_mm, 1)
            link(dve.tensor_tensor(lg[:, :], bank(0)[0:NB, 128:136], b2_s[:, :], ALU.add))
            dve.reduce_max(nmax[:, :], lg[:, :], AX.X, negate=True).then_inc(nmax_made, 1)
            dve.wait_ge(exp_made, 1)
            link(dve.reciprocal(rsum[:, :], esum[:, :]))
            dve.tensor_scalar(att[:, :], ex[:, :], rsum[:, :], None, ALU.mult).then_inc(att_made, 1)
            turn_lb(0)
            la_lo_part(2)
            dve.wait_ge(att_mm, 1)
            dve.tensor_copy(att_t[:, :], bank(0)[0:NE, 160:160 + NB]).then_inc(att_taken, 1)
            link(dve.tensor_copy(cw_t[:, :], bank(1)[:, 64:128]))
            la_lo_part(3)
            dve.wait_ge(bias_mm, 1)
            dve.tensor_copy(yb_c[:, :], bank(2)[0:NB, 0:NC]).then_inc(bias_made, 1)
            dve.tensor_tensor(cb_c[:, :], bank(2)[0:NB, NC:2 * NC], fside_s[:, :], ALU.add).then_inc(bias_made, 1)
            turn_lb(1)
            for n in range(8):
                dve.wait_ge(ring_mm, 4 + n + 1)
                dve.tensor_copy(mix_t[:, :, 8 * n:8 * n + 8].rearrange("b i o -> b o i"),
                                bank(4 + n % 4)[0:NB, :].rearrange("b (o i) -> b o i", o=8)).then_inc(ring_taken, 1)
            dve.wait_ge(las_hi_made, 1)
            dve.tensor_tensor(la_lo[:, :, NG * RANK:], bank(1)[:, 256:512].rearrange("p (k r) -> p k r", r=RANK),
                              la_hi[:, :, NG * RANK:], ALU.subtract).then_inc(las_lo_made, 1)
            turn_lb(2)
            turn_lb(3)
            dve.wait_ge(taps_mm, 1)
            for half in range(2):
                last = dve.tensor_copy(taps[:, :, half, :].rearrange("p g (q o) -> p g q o", q=PH),
                                       bank(2 + half).rearrange("p (q g o) -> p g q o", q=PH, g=GRP))
            last.then_inc(taps_made, 1)
            dve.wait_ge(taps_mm, 1)
            dve.wait_ge(raw_in[RAW_LBS % 4], 32)
            dve.transpose(lbs_t[:, :].rearrange("p (q b o) -> p o q b", b=32, q=PH),
                          raw[RAW_LBS % 4][0:32, :].rearrange("p (o q r) -> p o q r", r=RANK, q=PH)).then_inc(raw_free, 1)
            dve.wait_ge(raw_free, 5)
            dve.sem_inc(lb_turned, 5)

            for k in range(KT):
                dve.wait_ge(wk_hi_made, k + 1)
                n = RAW_WK + k
                dve.tensor_tensor(wk_lo[:, k, :].rearrange("p (q b) -> p q b", q=PH),
                                  raw[n % 4][:, :].rearrange("p (b q) -> p q b", q=PH),
                                  wk_hi[:, k, :].rearrange("p (q b) -> p q b", q=PH), ALU.subtract).then_inc(wk_lo_made, 1)
                dve.wait_ge(wk_lo_made, k + 1)
                dve.sem_inc(raw_free, 1)
                if k % 2:
                    m = k // 2
                    dve.wait_ge(ring_mm, 12 + m + 1)
                    half = slice(m % 2 * BLK // 2, (m % 2 + 1) * BLK // 2)
                    dve.tensor_copy(lb_c[:, m // 2, :].rearrange("p (q b) -> p b q", q=PH)[:, half, :],
                                    bank(4 + m).rearrange("p (b q) -> p b q", q=PH)).then_inc(ring_taken, 1)

            def take_y(t, s, a, first=False):
                for h in range(2):
                    dve.wait_ge(y_mm, t * 2 + h + 1)
                    if not first:
                        dve.wait_ge(y_lo_made, t * 2 + h - 1)
                    dve.tensor_tensor(y_f[h][:, :].rearrange("p (k r) -> p k r", r=P),
                                      bank(h).rearrange("p (k r) -> p k r", r=P),
                                      y_bias[:, ds(t * P, P)].unsqueeze(1).to_broadcast([P, 4, P]), ALU.add).then_inc(y_taken, 1)
                for h in range(2):
                    dve.wait_ge(y_hi_made, t * 2 + h + 1)
                    dve.tensor_tensor(y_lo[s][:, a, 4 * h:4 * h + 4, :].rearrange("p k r -> p (k r)"),
                                      y_f[h][:, :], y_hi[s][:, a, 4 * h:4 * h + 4, :].rearrange("p k r -> p (k r)"),
                                      ALU.subtract).then_inc(y_lo_made, 1)

            def take_z(g, s, first=False):
                dve.wait_ge(z_mm, g + 1)
                if not first:
                    dve.wait_ge(u_mm, g * 2 + 2)
                dve.tensor_copy(z_f[s][:, :], bank(6)[:, 0:ROWS_G]).then_inc(z_taken, 1)

            def take_x1(t, s):
                dve.wait_ge(u_mm, t + 5)
                dve.wait_ge(xb_made, t + 1)
                dve.tensor_tensor(x1_t[s][:, :], bank(2 + 2 * s, 2), x1_t[s][:, :], ALU.add).then_inc(x1_made, 1)

            dve.wait_ge(lb_stored, 32)
            dve.wait_ge(bias_loaded, 16)
            take_y(0, 0, 0, True)
            take_y(1, 0, 1)
            take_z(0, 0, True)
            with dve.Fori(0, 3) as i:
                for k in range(2):
                    t, g = i * 4 + 2 * k, i * 2 + k
                    take_y(t + 2, 1 - k, 0)
                    take_x1(t, 0)
                    take_y(t + 3, 1 - k, 1)
                    take_x1(t + 1, 1)
                    take_z(g + 1, 1 - k)
            take_y(14, 1, 0)
            take_x1(12, 0)
            take_y(15, 1, 1)
            take_x1(13, 1)
            take_z(7, 1)
            take_x1(14, 0)
            take_x1(15, 1)

            def turn(n_in, s, value, half, n_free):
                dve.wait_ge(w_in[s], value)
                if n_free is not None:
                    dve.wait_ge(w_lo_made, n_free)
                dve.transpose(w_t[half][:, :].rearrange("p (q m b) -> p q m b", q=PH, m=4),
                              raw[s][:, :].rearrange("p (m a q) -> p q m a", m=4, q=PH)).then_inc(turned, 1)
                dve.wait_ge(turned, n_in)
                dve.sem_inc(w_free, 1)

            def turn_w12(j, first=False):
                for half in range(2):
                    turn(j * 2 + half + 1, half, j * 64 + 64, half, None if first else j * 2 + half - 1)

            def w12_lo_part(j, s):
                for half in range(2):
                    dve.wait_ge(w_hi_made, j * 2 + half + 1)
                    dve.tensor_tensor(w12_lo[s][:, half, :, :].rearrange("p q m -> p (q m)"), w_t[half][:, :],
                                      w12_hi[s][:, half, :, :].rearrange("p q m -> p (q m)"), ALU.subtract).then_inc(w_lo_made, 1)

            def turn_w3(c):
                turn(W12_USES + c + 1, c % 2, 64 * (NJ + c // 2 + 1), c % 2, W12_USES + c - 1)

            def w3_lo_part(c):
                half, col = c // 4, (c % 4) * P
                dve.wait_ge(w_hi_made, W12_USES + c + 1)
                dve.tensor_tensor(w3_lo[half][:, :, col:col + P], w_t[c % 2][:, :].rearrange("p (j n) -> p j n", j=NJ),
                                  w3_hi[half][:, :, col:col + P], ALU.subtract).then_inc(w_lo_made, 1)

            turn_w12(0, True)
            w12_lo_part(0, 0)

            for s in range(2):
                dve.wait_ge(x1_stored[s], 16 * TILES // 2)

            def c_lo_part(i, k):
                dve.wait_ge(c_hi_made, i * 8 + k + 1)
                dve.tensor_tensor(c_lo[:, ds(i, 1), :, k * NC:(k + 1) * NC].rearrange("p a q (g o) -> p (a q) g o", g=GRP),
                                  c_f[k % 4][:, :].rearrange("p (g q o) -> p q g o", g=GRP, q=PH),
                                  c_hi[:, ds(i, 1), :, k * NC:(k + 1) * NC].rearrange("p a q (g o) -> p (a q) g o", g=GRP),
                                  ALU.subtract).then_inc(c_lo_made, 1)

            dve.wait_ge(c_bias_loaded, 16)
            with dve.Fori(0, RB) as i:
                for k in range(8):
                    b = i * 8 + k
                    dve.wait_ge(conv_mm, b + 1)
                    dve.wait_ge(c_lo_made, b + 1)
                    dve.tensor_tensor(c_f[k % 4][:, :].rearrange("p (g q o) -> p g q o", g=GRP, q=PH),
                                      bank(k).rearrange("p (g q o) -> p g q o", g=GRP, q=PH),
                                      c_bias[:, ds(b * NC, NC)].rearrange("p (g o) -> p g o", g=GRP)
                                      .unsqueeze(2).to_broadcast([P, GRP, PH, CG]), ALU.add).then_inc(c_taken, 1)
                    if k:
                        c_lo_part(i, k - 1)
                c_lo_part(i, 7)

            def hidden(j, rb):
                dve.wait_ge(g2_mm, j * 4 + rb + 5)
                dve.wait_ge(silu_made, j * 4 + rb + 2)
                if not (isinstance(j, int) and j == 0):
                    dve.wait_ge(h_stored[rb], j * 16)
                dve.scalar_tensor_tensor(out=h_s[rb][:, :], in0=bank(2 * rb + 1), scalar=b12_s[:, 1, ds(j, 1)],
                                         in1=silu_s[rb % 2][:, :], op0=ALU.add, op1=ALU.mult).then_inc(h_made, 1)

            dve.wait_ge(b12_in, 16)

            def gate_steps(i):
                for k in range(2):
                    j = i * 2 + k
                    hidden(j, 0)
                    turn_w12(j + 1)
                    hidden(j, 1)
                    w12_lo_part(j + 1, 1 - k)
                    hidden(j, 2)
                    hidden(j, 3)

            gate_steps(0)
            with dve.Fori(1, 3) as i:
                gate_steps(i)
            hidden(6, 0)
            turn_w12(7)
            hidden(6, 1)
            w12_lo_part(7, 1)
            hidden(6, 2)
            hidden(6, 3)

            def h_lo_part(t, s):
                dve.wait_ge(h_hi_made, t + 1)
                dve.tensor_tensor(h_lo[s][:, :, :], h_in[s][:, :, :], h_hi[s][:, :, :], ALU.subtract).then_inc(h_lo_made, 1)

            def take_out(t, s):
                dve.wait_ge(res_made, t + 1)
                for half in range(2):
                    dve.wait_ge(o_mm, t * 2 + half + 5)
                    cols = slice(half * HALF, (half + 1) * HALF)
                    dve.tensor_tensor(res[s][:, cols], bank(2 * s + half), res[s][:, cols], ALU.add).then_inc(out_made, 1)

            hidden(7, 0)
            turn_w3(0)
            turn_w3(1)
            w3_lo_part(0)
            w3_lo_part(1)
            hidden(7, 1)
            turn_w3(2)
            turn_w3(3)
            w3_lo_part(2)
            w3_lo_part(3)
            turn_w3(4)
            turn_w3(5)
            h_lo_part(0, 0)
            hidden(7, 2)
            h_lo_part(1, 1)
            w3_lo_part(4)
            w3_lo_part(5)
            turn_w3(6)
            turn_w3(7)
            w3_lo_part(6)
            w3_lo_part(7)
            hidden(7, 3)
            with dve.Fori(1, TILES // 2) as i:
                for s in range(2):
                    take_out(i * 2 + s - 2, s)
                    h_lo_part(i * 2 + s, s)
            for s in range(2):
                take_out(TILES - 2 + s, s)

        @block.tensor
        def _(pe):
            pe.sem_inc(u_mm, 4)
            pe.sem_inc(g2_mm, 4)
            pe.sem_inc(o_mm, 4)

            def mm(o, l, r, start, stop):
                return pe.matmul(o, l, r, start=start, stop=stop)

            def products(o, l_hi, l_lo, r_hi, r_lo, first, last):
                for n, (l, r) in enumerate(((l_hi, r_hi), (l_hi, r_lo), (l_lo, r_hi))):
                    for dst, src in zip(o, r):
                        ins = mm(dst, l, src, first and n == 0, last and n == 2)
                return ins

            ring = [0]

            def ring_bank():
                n = ring[0]
                ring[0] += 1
                if n >= 4:
                    pe.wait_ge(ring_taken, n - 3)
                return bank(4 + n % 4)

            def la_result(n):
                dst = ring_bank()
                for a in range(2):
                    for k in range(4):
                        c0 = (2 * n + a) * P
                        last = mm(dst[:, a * ROWS_G:(a + 1) * ROWS_G], la_raw[:, k, c0:c0 + P],
                                  gate_e[:, k, :, :].rearrange("p g r -> p (g r)"), k == 0, k == 3)
                last.then_inc(ring_mm, 1)

            pe.wait_ge(consts_made, 2)
            pe.wait_ge(cond_in, 48)
            pe.transpose(bank(0)[:, 0:NB], emb_s[:, :], ident[0:NB, 0:NB]).then_inc(cond_t, 1)
            pe.wait_ge(consts_made, 4)
            pe.wait_ge(gate_in, 16)
            for k in range(4):
                last = mm(bank(1)[:, NG * k:NG * (k + 1)], sel[:, k, :], gate_t[:, :], True, True)
            last.then_inc(gate_mm, 1)
            pe.wait_ge(emb_taken, 1)
            mm(bank(0)[:, 64:96], w0_s[:, :], emb_t[:, :], True, True).then_inc(h1_mm, 1)
            pe.wait_ge(gate_made, 1)
            pe.wait_ge(la_in, 16)
            la_result(0)
            pe.wait_ge(mlp_in, 64)
            pe.wait_ge(h1_act, 1)
            mm(bank(0)[:, 96:128], w1_s[:, :], h1_s[:, :], True, True).then_inc(h2_mm, 1)
            la_result(1)
            pe.wait_ge(h2_act, 1)
            mm(bank(0)[0:NB, 128:136], h2_s[:, :], w2_s[:, :], True, True).then_inc(lg_mm, 1)
            la_result(2)
            pe.wait_ge(small_in, 64)
            pe.wait_ge(las_in, 16)
            pe.transpose(bank(1)[:, 64:128], cw_raw[:, :], ident[0:NC, 0:NC])
            for k in range(KT):
                last = pe.transpose(bank(1)[:, 256 + k * RANK:256 + (k + 1) * RANK], las_raw[:, k * P:(k + 1) * P],
                                    ident[0:RANK, 0:RANK])
            last.then_inc(las_mm, 1)
            pe.wait_ge(att_made, 1)
            pe.transpose(bank(0)[0:NE, 160:160 + NB], att[:, :], ident[0:NB, 0:NB]).then_inc(att_mm, 1)
            la_result(3)
            pe.wait_ge(att_taken, 1)
            pe.wait_ge(setup_chain, 6)
            mm(bank(2)[0:NB, 0:NC], att_t[:, :], biask_s[:, :], True, True)
            mm(bank(2)[0:NB, NC:2 * NC], emb_t[:, :], cw_t[:, :], True, True).then_inc(bias_mm, 1)
            pe.wait_ge(expert_in, 16)
            for n in range(8):
                mm(ring_bank()[0:NB, :], att_t[:, :], expert[:, n * HALF:(n + 1) * HALF], True, True).then_inc(ring_mm, 1)
            pe.wait_ge(wpad_made, 1)
            pe.wait_ge(bias_made, 2)
            for half in range(2):
                for q in range(PH):
                    k0 = 8 + 8 * half - q
                    last = pe.transpose(bank(2 + half)[:, q * NC:(q + 1) * NC],
                                        wpad[:, k0:k0 + PH, :].rearrange("o k c -> o (k c)"), ident[0:NC, 0:NC])
            last.then_inc(taps_mm, 1)
            pe.wait_ge(raw_free, 4)
            for n in range(4):
                dst = ring_bank()
                for k in range(4):
                    last = mm(dst, gate_e[:, k, 4 * (n // 2):4 * (n // 2) + 4, :].rearrange("p g r -> p (g r)"),
                              lb_t[:, k, (n % 2) * HALF:(n % 2 + 1) * HALF], k == 0, k == 3)
                last.then_inc(ring_mm, 1)

            def y_tile(t, slot, loaded, first=False):
                pe.wait_ge(x_loaded[slot], loaded)
                for h in range(2):
                    if not first:
                        pe.wait_ge(y_taken, t * 2 + h - 1)
                    for k in range(4):
                        c0 = (4 * h + k) * P
                        last = mm(bank(h)[:, k * P:(k + 1) * P], x_in[slot][:, c0:c0 + P],
                                  mix[:, ds(t, 1), :].rearrange("p a r -> p (a r)"), True, True)
                    last.then_inc(y_mm, 1)

            def z_group(g, s, first=False):
                pe.wait_ge(la_gathered, g + 1)
                pe.wait_ge(y_lo_made, g * 4 + 4)
                if not first:
                    pe.wait_ge(z_taken, g)
                dst = bank(6)[:, 0:ROWS_G]
                for k in range(KT):
                    mm(dst, la_g[s][:, k, :], y_hi[s][:, :, k, :], k == 0, False)
                    last = mm(dst, la_g[s][:, k, :], y_lo[s][:, :, k, :], False, k == KT - 1)
                last.then_inc(z_mm, 1)

            def u_tile(t, s, a, lb_value, first=False):
                pe.wait_ge(y_lo_made, t * 2 + 2)
                pe.wait_ge(x1_made, t + 1)
                dst = [bank(2 + 2 * a), bank(3 + 2 * a)]
                for k in range(KT):
                    if first:
                        pe.wait_ge(wk_lo_made, k + 1)
                    products(dst, y_hi[s][:, a, k, :], y_lo[s][:, a, k, :],
                             [wk_hi[:, k, 0:HALF], wk_hi[:, k, HALF:]], [wk_lo[:, k, 0:HALF], wk_lo[:, k, HALF:]],
                             k == 0, False)
                if a == 0:
                    pe.wait_ge(lb_loaded[s], lb_value)
                return dst

            def u_lora(dst, t, s, a, g):
                pe.wait_ge(z_taken, g + 1)
                for half in range(2):
                    last = mm(dst[half], z_f[s][:, a * P:(a + 1) * P],
                              lb_g[s][:, half * HALF:(half + 1) * HALF], False, True)
                last.then_inc(u_mm, 1)

            pe.wait_ge(las_lo_made, 1)
            pe.wait_ge(mix_loaded, 32)
            y_tile(0, 0, 16, True)
            y_tile(1, 1, 16)
            z_group(0, 0, True)

            def groups(i, first=False):
                for k in range(2):
                    t, g = i * 4 + 2 * k, i * 2 + k
                    y_tile(t + 2, (2 * k + 2) % 4, i * 16 + (16 if k == 0 else 32))
                    u_lora(u_tile(t, k, 0, i * 32 + 64, first and k == 0), t, k, 0, g)
                    y_tile(t + 3, (2 * k + 3) % 4, i * 16 + (16 if k == 0 else 32))
                    u_lora(u_tile(t + 1, k, 1, None), t + 1, k, 1, g)
                    z_group(g + 1, 1 - k)

            groups(0, True)
            with pe.Fori(1, 3) as i:
                groups(i)
            y_tile(14, 2, 64)
            u_lora(u_tile(12, 0, 0, 160), 12, 0, 0, 6)
            y_tile(15, 3, 64)
            u_lora(u_tile(13, 0, 1, None), 13, 0, 1, 6)
            z_group(7, 1)
            u_lora(u_tile(14, 1, 0, 160), 14, 1, 0, 7)
            u_lora(u_tile(15, 1, 1, None), 15, 1, 1, 7)

            pe.wait_ge(taps_made, 1)
            pe.wait_ge(pads_made, 2)

            def convolve(i, first=False):
                for k in range(8):
                    if first and k in (2, 4):
                        pe.wait_ge(x1_made, TILES + k // 2)
                    if k % 4 == 0:
                        pe.wait_ge(x8_loaded[k // 4], i * 128 + 128)
                    pe.wait_ge(c_taken, i * 8 + k + 1)
                    for g in range(GRP):
                        src, dst = x8[k // 4][:, (k % 4) * GRP + g, :], bank(k)[:, g * P:(g + 1) * P]
                        mm(dst, src[:, 0:BLK], taps[:, g, 0, :], True, False)
                        last = mm(dst, src[:, 1:BLK + 1], taps[:, g, 1, :], False, True)
                    last.then_inc(conv_mm, 1)

            pe.wait_ge(y_taken, 2 * TILES)
            convolve(0, True)
            with pe.Fori(1, 4) as i:
                convolve(i)

            def gate_step(j, s):
                pe.wait_ge(w_lo_made, j * 2 + 2)
                for rb in range(RB):
                    pe.wait_ge(h_made, j * 4 + rb + 1)
                    for half, done in ((0, g1_mm), (1, g2_mm)):
                        for q in range(PH):
                            last = products([bank(2 * rb + half)], w12_hi[s][:, half, q, :], w12_lo[s][:, half, q, :],
                                            [c_hi[:, rb, q, :]], [c_lo[:, rb, q, :]], q == 0, q == PH - 1)
                        last.then_inc(done, 1)

            pe.wait_ge(c_lo_made, NB + 4)
            pe.wait_ge(c_taken, NB + 8)
            with pe.Fori(0, NJ // 2) as i:
                for k in range(2):
                    gate_step(i * 2 + k, k)

            def out_tile(t, s, first=False):
                pe.wait_ge(h_lo_made, t + 1)
                pe.wait_ge(out_made, t * 2 + 2)
                for half in range(2):
                    if first:
                        pe.wait_ge(w_lo_made, W12_USES + 4 * (half + 1))
                    for j in range(NJ):
                        last = products([bank(2 * s + half)], h_hi[s][:, j, :], h_lo[s][:, j, :],
                                        [w3_hi[half][:, j, :]], [w3_lo[half][:, j, :]], j == 0, j == NJ - 1)
                    last.then_inc(o_mm, 1)

            pe.wait_ge(h_made, 4 + 4 * (NJ - 1) + 2)
            out_tile(0, 0, True)
            out_tile(1, 1)
            with pe.Fori(1, TILES // 2) as i:
                for s in range(2):
                    out_tile(i * 2 + s, s)


_INS = ['x', 'cond_128', 'fside_S_0', 'L0_cond_W0', 'L0_cond_b0', 'L0_cond_W1', 'L0_cond_b1', 'L0_cond_W2', 'L0_cond_b2',
        'L0_cond_weight', 'L0_cond_bias_k', 'L0_ffn_gate', 'L0_ffn_kernel', 'L0_ffn_bias', 'L0_ffn_lora_A',
        'L0_ffn_lora_B', 'L0_ffn_lora_A_shared', 'L0_ffn_lora_B_shared', 'L1_cond_weight', 'L1_cond_c_weight',
        'L1_ffn_w12', 'L1_ffn_b12', 'L1_ffn_w3', 'L1_ffn_b3']


def kernel(**inputs):
    import concourse.bacc as bacc
    from concourse.bass_utils import run_bass_kernel_spmd

    nc = bacc.Bacc("TRN2", target_bir_lowering=False, num_devices=1)
    arrays, args = {}, []
    for name in _INS:
        a = np.ascontiguousarray(inputs[name])
        arrays[f"in_{name}"] = a
        args.append(nc.dram_tensor(f"in_{name}", a.shape, mybir.dt.from_np(a.dtype), kind="ExternalInput").ap())
    out = nc.dram_tensor("out", (NB, NC, NL), F32, kind="ExternalOutput").ap()
    layered_kernel(nc, *args, out)
    r = run_bass_kernel_spmd(nc, [arrays], core_ids=[0])
    return r.results[0]["out"]
```

```python
import numpy as np
import concourse.bass as bass
from concourse import mybir
from contextlib import ExitStack

F32 = mybir.dt.float32
F32R = mybir.dt.float32r
ALU = mybir.AluOpType
ACT = mybir.ActivationFunctionType
AX = mybir.AxisListType

P = 128
NB, NC, NL = 32, 64, 1024
ROWS = NB * NC
TILES = ROWS // P
KT = NL // P
HALF = 512
NE, ND = 8, 128
NG, ROWS_G = 8, ROWS // 8
TG = ROWS_G // P
NLORA, RANK = 16, 32
OC = 4
NPART = NC // OC
OCT, R8 = 4, 8
PH, BLK = 8, NL // 8
CG, GRP, TAPS = 16, 4, 9
PAD = TAPS // 2
RB = ROWS // HALF
NJ = NL // P


def layered_kernel(nc, x, cond, fside, c0_w0, c0_b0, c0_w1, c0_b1, c0_w2, c0_b2, c0_weight, c0_bias_k,
                   f0_gate, f0_kernel, f0_bias, lora_a, lora_b, lora_a_s, lora_b_s,
                   c1_weight, c1_c_weight, w12, b12, w3, b3, out):
    ds = bass.ds
    x_rows = x.rearrange("b c l -> (b c) l")
    out_rows = out.rearrange("b c l -> (b c) l")

    x1_dram = nc.dram_tensor("x1_scratch", [ROWS, NL], F32).ap()
    h_dram = nc.dram_tensor("h_scratch", [NJ, P, ROWS], F32).ap()
    lb_dram = nc.dram_tensor("lora_b_scratch", [NG + 1, 2, RANK, NL], F32).ap()
    bias_dram = nc.dram_tensor("bias_scratch", [2, ROWS], F32).ap()

    ctx = ExitStack()
    with ctx:
        BASE = -(-nc.sbuf_base // 64) * 64

        def at(name, shape, kb, dt=F32):
            return nc.alloc_sbuf_tensor_at(name, shape, dt, offset=BASE + int(kb * 1024))

        def sem(name):
            return ctx.enter_context(nc.semaphore(name))

        wk_hi = at("wk_hi", [P, KT, NL], 0, F32R)
        wk_lo = at("wk_lo", [P, KT, NL], 32, F32R)
        NA = (NG + 1) * RANK
        la_hi = at("la_hi", [P, KT, NA], 64, F32R)
        la_lo = at("la_lo", [P, KT, NA], 73, F32R)
        la_g = [at(f"la_g{s}", [P, KT, P], 82 + 4 * s, F32R) for s in range(2)]
        z_2 = [at(f"z_2{s}", [P, ROWS_G], 94 + s, F32R) for s in range(2)]
        y_hi = [at(f"y_hi{s}", [P, TG, KT, P], 96 + 16 * s, F32R) for s in range(2)]
        y_lo = [at(f"y_lo{s}", [P, TG, KT, P], 104 + 16 * s, F32R) for s in range(2)]
        x_in = [at(f"x_in{s}", [P, NL], 128 + 4 * s) for s in range(4)]
        x1_t = [at(f"x1_t{s}", [P, NL], 144.25 + 4 * s) for s in range(2)]
        y_f = [at(f"y_f{s}", [P, HALF], 152.25 + 2 * s) for s in range(2)]
        z_1 = [at(f"z_1{s}", [P, ROWS_G], 156.25 + s, F32R) for s in range(2)]
        lb_1 = [at(f"lb_1{s}", [P, NL], 158.25 + 4 * s, F32R) for s in range(2)]
        lb_2 = [at(f"lb_2{s}", [P, NL], 182.25 + 4 * s, F32R) for s in range(2)]
        y_bias = at("y_bias", [P, ROWS], 166.25)
        mix = at("mix", [P, TILES, P], 174.25)
        c_bias = at("c_bias", [P, ROWS], 182.25)
        taps = at("taps", [P, GRP, 2, P], 190.25)
        f_bias = at("f_bias", [P, NL], 194.25)
        ident = at("ident", [P, P], 198.25)
        b12_s = at("b12_s", [P, 2, NJ], 198.75)
        b1_j = at("b1_j", [P, 1], 198.875)
        gate_e = at("gate_e", [P, NG, R8], 199)
        raw = [at(f"raw{s}", [P, NL], k) for s, k in enumerate((199.75, 203.75, 90, 140))]
        expert = at("expert", [P, OC * NC], 152.25)
        att_s = at("att_s", [P, 4, 4, NB], 153.25)
        la_raw = at("la_raw", [P, OCT, NL], 112)
        lb_t = at("lb_t", [P, OCT, 4, PH, 32], 112)
        mix_t = at("mix_t", [P, 4 * OC, 2, NC], 144.25)
        lb_c = [at("lb_c_lo", [P, 2, NL], 182.25), at("lb_c_hi", [P, 2, NL], 158.25)][::-1]
        wpad = at("wpad", [NC, 24, CG], 136)
        w9_raw = at("w9_raw", [NC, CG, TAPS], 137.5)
        cw_raw = at("cw_raw", [NC, ND], 138.25)
        lbs_t = at("lbs_t", [RANK, NL], 186.25)
        lbs_c = [at("lbs_hi", [RANK, NL], 158.25), at("lbs_lo", [RANK, NL], 162.25)]
        sel = at("sel", [NLORA, P], 190.25)
        las_raw = at("las_raw", [RANK, NL], 186.25)
        small = iter(range(int(182.25 * 32), int(186.25 * 32)))

        def tiny(name, shape):
            k = next(small)
            for _ in range(-(-4 * int(np.prod(shape[1:])) // 32) - 1):
                next(small)
            return at(name, shape, k / 32)

        w0_s, w1_s = at("w0_s", [P, P], 138.75), at("w1_s", [P, P], 139.25)
        emb_s, emb_t = tiny("emb_s", [NB, ND]), tiny("emb_t", [ND, NB])
        cw_t, biask_s = tiny("cw_t", [ND, NC]), tiny("biask_s", [P, NC])
        fside_s = tiny("fside_s", [NB, NC])
        yb_c, cb_c = tiny("yb_c", [NB, NC]), tiny("cb_c", [NB, NC])
        h1_s, h2_s = tiny("h1_s", [P, NB]), tiny("h2_s", [P, NB])
        gate_c, warm = tiny("gate_c", [P, NG]), tiny("warm", [P, 1])
        m_r = [tiny(f"m{n}", [P, n]) for n in (64, 32, 16, 8)]
        w2_s, gate_t = tiny("w2_s", [P, NE]), tiny("gate_t", [NLORA, NG])
        b0_s, b1_s, b2_s = tiny("b0_s", [P, 1]), tiny("b1_s", [P, 1]), tiny("b2_s", [NB, NE])
        lg, ex, att = tiny("lg", [NB, NE]), tiny("ex", [NB, NE]), tiny("att", [NB, NE, NPART])
        nmax, esum, rsum = tiny("nmax", [NB, 1]), tiny("esum", [NB, 1]), tiny("rsum", [NB, 1])
        c_hi = at("c_hi", [P, RB, PH, HALF], 0, F32R)
        c_lo = at("c_lo", [P, RB, PH, HALF], 64, F32R)
        x8 = [at(f"x8_{s}", [P, 4 * GRP, BLK + 1], 128 + 8.0625 * s) for s in range(2)]
        c_f = [at(f"c_f{s}", [P, HALF], 144.25 + 2 * s) for s in range(4)]
        w_t = [at(f"w_t{s}", [P, NL], 152.25 + 4 * s) for s in range(2)]
        w12_hi = [at("w12_hi0", [P, 2, PH, P], 166.25, F32R), at("w12_hi1", [P, 2, PH, P], 128, F32R)]
        w12_lo = [at("w12_lo0", [P, 2, PH, P], 174.25, F32R), at("w12_lo1", [P, 2, PH, P], 136, F32R)]
        silu_s = [at(f"silu_s{s}", [P, HALF], 144.25 + 2 * s) for s in range(2)]
        h_s = [at(f"h_s{s}", [P, HALF], k) for s, k in enumerate((148.25, 150.25, 160.25, 162.25))]
        w3_hi = [at("w3_hi0", [P, NJ, HALF], 166.25, F32R), at("w3_hi1", [P, NJ, HALF], 32, F32R)]
        w3_lo = [at("w3_lo0", [P, NJ, HALF], 182.25, F32R), at("w3_lo1", [P, NJ, HALF], 96, F32R)]
        h_in = [at(f"h_in{s}", [P, NJ, P], 4 * s) for s in range(2)]
        h_hi = [at(f"h_hi{s}", [P, NJ, P], 8 + 4 * s, F32R) for s in range(2)]
        h_lo = [at(f"h_lo{s}", [P, NJ, P], 64 + 4 * s, F32R) for s in range(2)]
        x1_in = [at(f"x1_in{s}", [P, NL], 72 + 4 * s) for s in range(2)]
        res = [at(f"res{s}", [P, NL], 16 + 4 * s) for s in range(2)]
        b3_s = at("b3_s", [P, NL], 24)

        ps = ctx.enter_context(nc.psum_tensor("ps", [P, 8 * HALF], F32))

        def bank(n, k=1):
            return ps[:, n * HALF:(n + k) * HALF]

        cond_in = sem("cond_in")
        mlp_in = sem("mlp_in")
        biask_in = sem("biask_in")
        small_in = sem("small_in")
        gate_in, la_in, las_in = sem("gate_in"), sem("la_in"), sem("las_in")
        expert_in, fbias_in, b12_in = sem("expert_in"), sem("fbias_in"), sem("b12_in")
        raw_in = [sem(f"raw_in{s}") for s in range(4)]
        raw_free = sem("raw_free")
        w_in = [sem(f"w_in{s}") for s in range(2)]
        w_free = sem("w_free")
        x_loaded = [sem(f"x_loaded{s}") for s in range(4)]
        lb_loaded = [sem(f"lb_loaded{s}") for s in range(2)]
        consts_made = sem("consts_made")
        mix_zeroed, wpad_zeroed = sem("mix_zeroed"), sem("wpad_zeroed")
        setup_chain = sem("setup_chain")
        cond_t, emb_taken = sem("cond_t"), sem("emb_taken")
        gate_mm, gate_taken = sem("gate_mm"), sem("gate_taken")
        h1_mm, h1_act, h2_mm, h2_act = sem("h1_mm"), sem("h1_act"), sem("h2_mm"), sem("h2_act")
        lg_mm, nmax_made, exp_made = sem("lg_mm"), sem("nmax_made"), sem("exp_made")
        att_made, att_mm, att_taken = sem("att_made"), sem("att_mm"), sem("att_taken")
        part_mm, part_taken = sem("part_mm"), sem("part_taken")
        mix_mm, mix_made = sem("mix_mm"), sem("mix_made")
        bias_mm, bias_made = sem("bias_mm"), sem("bias_made")
        yb_stored, cb_stored, bias_loaded = sem("yb_stored"), sem("cb_stored"), sem("bias_loaded")
        bias_rest_loaded = sem("bias_rest_loaded")
        c_bias_loaded = [sem(f"c_bias_loaded{s}") for s in range(2)]
        wpad_made, taps_mm, taps_made = sem("wpad_made"), sem("taps_mm"), sem("taps_made")
        las_mm, las_hi_made, las_lo_made = sem("las_mm"), sem("las_hi_made"), sem("las_lo_made")
        gate_made = sem("gate_made")
        lbs_turned, lbs_made = sem("lbs_turned"), sem("lbs_made")
        lb_hi_made = sem("lb_hi_made")
        lora_mm = sem("lora_mm")
        lora_taken = sem("lora_taken")
        la_hi_made = sem("la_hi_made")
        lbs_stored, lb_stored = sem("lbs_stored"), [sem(f"lb_stored{n}") for n in range(2)]
        wk_hi_made, wk_lo_made, wk_lo_pool = sem("wk_hi_made"), sem("wk_lo_made"), sem("wk_lo_pool")
        lb_in = [sem(f"lb_in{c}") for c in range(4)]
        lb_turned = sem("lb_turned")
        la_gathered = sem("la_gathered")
        y_mm = sem("y_mm")
        y_taken = sem("y_taken")
        y_hi_made, y_lo_made = sem("y_hi_made"), sem("y_lo_made")
        z_mm, z_hi_made, z_taken = sem("z_mm"), sem("z_hi_made"), sem("z_taken")
        u_mm = sem("u_mm")
        xb_made = sem("xb_made")
        x1_made = sem("x1_made")
        x1_stored = [sem(f"x1_stored{s}") for s in range(2)]
        pads_made = sem("pads_made")
        x8_loaded = [sem(f"x8_loaded{s}") for s in range(2)]
        conv_mm = sem("conv_mm")
        c_taken = sem("c_taken")
        c_hi_made = sem("c_hi_made")
        c_lo_made = sem("c_lo_made")
        turned = sem("turned")
        w_hi_made, w_lo_made = sem("w_hi_made"), sem("w_lo_made")
        g1_mm = sem("g1_mm")
        g2_mm = sem("g2_mm")
        b1_made = sem("b1_made")
        silu_made = sem("silu_made")
        h_made = sem("h_made")
        h_stored = [sem(f"h_stored{s}") for s in range(RB)]
        b3_in = sem("b3_in")
        h_loaded = [sem(f"h_loaded{s}") for s in range(2)]
        x1_loaded = [sem(f"x1_loaded{s}") for s in range(2)]
        h_hi_made, h_lo_made = sem("h_hi_made"), sem("h_lo_made")
        res_made = sem("res_made")
        o_mm = sem("o_mm")
        out_made = sem("out_made")
        out_stored = [sem(f"out_stored{s}") for s in range(2)]

        N_LORA = 8
        LA_BANKS, LB_BANKS = (4, 5, 6, 7), (4, 5, 7, 6)
        RAW_LBS, RAW_LB = KT, KT + 1
        POOL_WK = (1, 2)

        def uses_of_dve(n):
            return sum(k not in POOL_WK for k in range(n))

        def wait_slot(eng, n):
            if n in POOL_WK:
                eng.wait_ge(wk_lo_pool, POOL_WK.index(n) + 1)
            else:
                eng.wait_ge(raw_free, uses_of_dve(n + 1))

        lb_raw = [at(f"lb_raw{s}", [P, NL], 144.25 + 4 * s) for s in range(2)] + [raw[(RAW_LB + c) % 4] for c in range(2)]
        LB_FIRST, LB_NEXT = 96, 48
        W12_USES = 2 * NJ

        def mix_result(a):
            v = ps[a * NC:(a + 1) * NC, 4 * HALF:].rearrange("p (o c t a) -> p a t c o", o=4 * OC, c=4, a=2)
            return v[:, a]

        def lb_result(n):
            return bank(LB_BANKS[n]).rearrange("p (c q b) -> p c q b", c=2, q=PH)

        def lb_part(hl, n):
            return (lb_c[hl][:, n % 2, :].rearrange("p (q c b) -> p c q b", c=4, q=PH)
                    [:, 2 * (n // 2):2 * (n // 2) + 2])

        block = ctx.enter_context(nc.Block())

        @block.sync
        def _(sp):
            def load_raw(n, src, rows=P):
                if n >= 4:
                    wait_slot(sp, n - 4)
                sp.dma_start(raw[n % 4][0:rows, :], src).then_inc(raw_in[n % 4], 16)

            sp.dma_start(emb_s[:, :], cond).then_inc(cond_in, 16)
            sp.dma_start(w1_s[:, :], c0_w1).then_inc(mlp_in, 16)
            sp.dma_start(w2_s[:, :], c0_w2).then_inc(mlp_in, 16)
            sp.dma_start(expert[:, :], c0_weight.rearrange("k (c o) i a -> (k c) (o i a)", o=OC)).then_inc(expert_in, 16)
            with nc.allow_non_contiguous_dma(reason="a gate of 8 x 16"):
                sp.dma_start(gate_t[:, :], f0_gate.rearrange("g n -> n g")).then_inc(gate_in, 16)
            la_v = lora_a.rearrange("n (k r) i -> k n r i", k=OCT)
            for k in range(OCT):
                sp.dma_start(la_raw[:, k, :], la_v[k]).then_inc(la_in, 16)
            for t in range(2):
                sp.dma_start(x_in[t][:, :], x_rows[t * P:(t + 1) * P, :]).then_inc(x_loaded[t], 16)
            def store_bias(n, src, stored):
                sp.wait_ge(bias_made, n + 1)
                sp.dma_start(bias_dram[n].rearrange("(b o) -> b o", o=NC), src[:, :]).then_inc(stored, 16)

            store_bias(0, yb_c, yb_stored)
            load_raw(0, f0_kernel[0:P, :])
            load_raw(1, f0_kernel[P:2 * P, :])
            sp.wait_ge(yb_stored, 16)
            def load_y_bias(r0, r1, loaded):
                sp.dma_start(y_bias[:, r0:r1], bias_dram[0, r0:r1].partition_broadcast(P)).then_inc(loaded, 16)

            load_y_bias(0, HALF, bias_loaded)
            for k in range(2, 4):
                load_raw(k, f0_kernel[k * P:(k + 1) * P, :])
            load_y_bias(HALF, ROWS, bias_rest_loaded)
            store_bias(1, cb_c, cb_stored)
            load_raw(4, f0_kernel[4 * P:5 * P, :])

            lb_v = lora_b.rearrange("(a n) (c b q) r -> c a b n (q r)", n=4, c=4, b=32)

            def load_lora_b(c):
                for a in range(4):
                    sp.dma_start(lb_raw[c][32 * a:32 * a + 32, :].rearrange("b (n e) -> b n e", n=4),
                                 lb_v[c, a]).then_inc(lb_in[c], 16)

            sp.wait_ge(mix_mm, 4)
            load_lora_b(0)
            load_lora_b(1)
            for k in range(5, KT):
                load_raw(k, f0_kernel[k * P:(k + 1) * P, :])
            sp.wait_ge(taps_mm, 1)
            sp.dma_start(x_in[2][:, :], x_rows[2 * P:3 * P, :]).then_inc(x_loaded[2], 16)
            load_raw(RAW_LBS, lora_b_s.rearrange("(b o) r -> b (o r)", b=32), rows=32)
            for c in (2, 3):
                wait_slot(sp, RAW_LB + c - 2 - 4)
                load_lora_b(c)
            sp.wait_ge(lbs_made, 2)
            for hl in range(2):
                sp.dma_start(lb_dram[NG, hl], lbs_c[hl][:, :]).then_inc(lbs_stored, 16)
            wait_slot(sp, KT - 1)
            sp.dma_start(x_in[3][:, :], x_rows[3 * P:4 * P, :]).then_inc(x_loaded[3], 16)

            lb_w = lb_dram[0:NG].rearrange("g h (k o r) n -> h o k g r n", k=2, o=2)
            for pair in range(2):
                sp.wait_ge(lora_taken, 4 + pair + 3)
                for hl in range(2):
                    for odd in range(2):
                        sp.dma_start(lb_w[hl, odd, pair], lb_c[hl][64 * odd:64 * odd + 64, pair, :]).then_inc(lb_stored[pair], 16)

            def store_x1(t, s, made):
                sp.wait_ge(x1_made, made)
                sp.dma_start(x1_dram[ds(t * P, P), :], x1_t[s][:, :]).then_inc(x1_stored[s], 16)

            def load_lb(s, src, top):
                for n in range(2):
                    sp.dma_start(lb_1[s][top + n * RANK:top + (n + 1) * RANK, :].bitcast(F32),
                                 src[0:RANK, :]).then_inc(lb_loaded[s], 16)
                sp.dma_start(lb_2[s][top:top + 2 * RANK, :].bitcast(F32), src).then_inc(lb_loaded[s], 16)

            def group_lb(g):
                return lb_dram[ds(g, 1)].rearrange("a h r n -> (a h r) n")

            def load_x(t, k):
                sp.dma_start(x_in[k][:, :], x_rows[ds(t * P, P), :]).then_inc(x_loaded[k], 16)

            sp.wait_ge(lbs_stored, 32)
            sp.wait_ge(lb_stored[0], 64)
            load_lb(0, group_lb(NG), 2 * RANK)
            sp.wait_ge(lb_stored[1], 64)
            load_lb(0, group_lb(0), 0)
            sp.wait_ge(y_mm, 4)
            sp.wait_ge(xb_made, 2)
            for t in (4, 5):
                load_x(t, t - 4)
            load_lb(1, group_lb(NG), 2 * RANK)
            load_lb(1, group_lb(1), 0)

            def rows_of_x1(i, first=False):
                for k in range(4):
                    if first and k >= 2:
                        sp.wait_ge(y_mm, 2 * k + 2)
                        sp.wait_ge(xb_made, k + 1)
                        load_x(k + 4, k)
                    store_x1(i * 4 + k, k % 2, i * 4 + k + 3)
                    if not first:
                        load_x(i * 4 + k + 4, k)
                    if k == 2:
                        sp.wait_ge(u_mm, i * 4 + 6)
                        load_lb(0, group_lb(i * 2 + 2), 0)
                sp.wait_ge(u_mm, i * 4 + 8)
                load_lb(1, group_lb(i * 2 + 3), 0)

            rows_of_x1(0, True)
            with sp.Fori(1, 3) as i:
                rows_of_x1(i)

            w12_v = w12.rearrange("(h m b j) l -> h j b m l", h=2, m=4, b=32, j=NJ)
            w3_v = w3.rearrange("(c m b) l -> c b m l", c=NJ, m=4, b=32)

            def load_w(s, src):
                for q in range(4):
                    dst = raw[s][32 * q:32 * q + 32, :].rearrange("b (m l) -> b m l", m=4)
                    sp.dma_start(dst, src(q)).then_inc(w_in[s], 16)

            def load_w12(j):
                for half in range(2):
                    if isinstance(j, int):
                        load_w(half, lambda q: w12_v[half, j, :, :, 256 * q:256 * q + 256])
                    else:
                        sp.wait_ge(w_free, j * 2 + half - 1)
                        load_w(half, lambda q: w12_v[half, ds(j, 1), :, :, 256 * q:256 * q + 256]
                               .rearrange("a b m l -> (a b) m l"))

            def load_w3(c):
                sp.wait_ge(w_free, W12_USES + c - 1)
                load_w(c % 2, lambda q: w3_v[c, :, :, 256 * q:256 * q + 256])

            x1_v = x1_dram.rearrange("(g c) e -> c g e", c=CG)

            def load_x8(cb, s):
                for p in range(PH):
                    q = (p + PAD) % PH
                    j0 = 1 if p >= PAD else 0
                    sp.dma_start(x8[s][q * CG:(q + 1) * CG, :, j0:j0 + BLK],
                                 x1_v[:, ds(cb * 4 * GRP, 4 * GRP), p * BLK:(p + 1) * BLK]).then_inc(x8_loaded[s], 16)

            store_x1(TILES - 4, 0, TILES - 1)
            store_x1(TILES - 3, 1, TILES)
            def load_c_bias(half):
                rows = slice(half * ROWS // 2, (half + 1) * ROWS // 2)
                sp.dma_start(c_bias[:, rows], bias_dram[1, rows].partition_broadcast(P)).then_inc(c_bias_loaded[half], 16)

            sp.wait_ge(cb_stored, 16)
            load_c_bias(0)
            load_w12(0)
            sp.wait_ge(y_mm, 2 * TILES)
            sp.wait_ge(xb_made, TILES)
            for cb in range(2):
                for s in range(2):
                    sp.wait_ge(x1_stored[s], 16 * (cb + 1))
                load_x8(cb, cb)
            store_x1(TILES - 2, 0, TILES + 1)
            store_x1(TILES - 1, 1, TILES + 2)
            load_c_bias(1)
            for s in range(2):
                sp.wait_ge(x1_stored[s], 16 * TILES // 2)
            with sp.Fori(0, 3) as i:
                for k in range(2):
                    sp.wait_ge(conv_mm, i * 8 + 4 * k + 4)
                    load_x8(i * 2 + 2 + k, k)

            def store_h(j, rb):
                sp.wait_ge(h_made, j * 4 + rb + 5)
                sp.dma_start(h_dram[ds(j, 1), :, rb * HALF:(rb + 1) * HALF].rearrange("a p r -> (a p) r"),
                             h_s[rb][:, :]).then_inc(h_stored[rb], 16)

            with sp.Fori(0, NJ - 1) as j:
                load_w12(j + 1)
                for rb in range(RB):
                    store_h(j, rb)

            def load_h(t, s):
                sp.dma_start(h_in[s][:, :, :], h_dram[:, :, ds(t * P, P)].rearrange("j p r -> p j r")).then_inc(h_loaded[s], 16)

            def load_x1(t, s):
                sp.dma_start(x1_in[s][:, :], x1_dram[ds(t * P, P), :]).then_inc(x1_loaded[s], 16)

            load_w3(0)
            load_w3(1)
            store_h(NJ - 1, 0)
            load_w3(2)
            load_w3(3)
            sp.wait_ge(g2_mm, 4 * NJ + 1)
            sp.wait_ge(h_stored[0], 16 * NJ)
            for t in range(2):
                load_h(t, t)
                load_x1(t, t)
            store_h(NJ - 1, 1)
            load_w3(4)
            load_w3(5)
            sp.wait_ge(g2_mm, 4 * NJ + 2)
            sp.dma_start(b3_s[:, :], b3.partition_broadcast(P)).then_inc(b3_in, 16)
            store_h(NJ - 1, 2)
            load_w3(6)
            load_w3(7)
            store_h(NJ - 1, 3)
            for rb in range(1, RB):
                sp.wait_ge(h_stored[rb], 16 * NJ)

            def store_out(t, s, made, cols=slice(0, NL)):
                sp.wait_ge(out_made, made)
                sp.dma_start(out_rows[ds(t * P, P), cols], res[s][:, cols]).then_inc(out_stored[s], 16)

            with sp.Fori(1, TILES // 2) as i:
                for s in range(2):
                    sp.wait_ge(h_lo_made, i * 2 + s - 1)
                    load_h(i * 2 + s, s)
                    sp.wait_ge(res_made, i * 2 + s - 1)
                    load_x1(i * 2 + s, s)
                    store_out(i * 2 + s - 2, s, i * 4 + 2 * s + 2)
            store_out(TILES - 2, 0, 2 * TILES + 2)
            for half in range(2):
                store_out(TILES - 1, 1, 2 * TILES + 3 + half, slice(half * HALF, (half + 1) * HALF))
            sp.wait_ge(out_stored[0], 16 * TILES // 2)
            sp.wait_ge(out_stored[1], 16 * TILES // 2 + 16)

        @block.gpsimd
        def _(pool):
            pool.memset(ident[:, :], 0.0).then_inc(consts_made, 1)
            pool.wait_ge(consts_made, 1)
            pool.affine_select(out=ident[:, :], in_=ident[:, :], compare_op=ALU.not_equal, fill=1.0,
                               base=0, pattern=[[-1, P]], channel_multiplier=1).then_inc(consts_made, 1)
            pool.memset(sel[:, :], 0.0).then_inc(consts_made, 1)
            pool.wait_ge(consts_made, 3)
            sel_v = sel[:, :].rearrange("n (a r) -> n a r", r=R8)
            pool.affine_select(out=sel_v, in_=sel_v, compare_op=ALU.not_equal, fill=1.0,
                               base=0, pattern=[[-1, NLORA], [0, R8]], channel_multiplier=1).then_inc(consts_made, 1)
            pool.memset(wpad[:, :, :], 0.0).then_inc(wpad_zeroed, 1)
            pool.memset(mix[:, :, :], 0.0).then_inc(mix_zeroed, 1)

            pool.dma_start(biask_s[:, :], c0_bias_k.unsqueeze(1).to_broadcast([NE, NPART, NC])).then_inc(biask_in, 16)
            pool.dma_start(las_raw[:, :], lora_a_s).then_inc(las_in, 16)
            for dst, src in ((cw_raw[:, :], c1_c_weight), (w9_raw[:, :, :], c1_weight),
                             (fside_s[:, :], fside.partition_broadcast(NB))):
                pool.dma_start(dst, src).then_inc(small_in, 16)


            def gather_la(g, s):
                for src, c0 in ((la_hi, 0), (la_lo, RANK)):
                    ins = pool.tensor_copy(la_g[s][:, :, c0:c0 + RANK], src[:, :, ds(g * RANK, RANK)].bitcast(F32))
                ins.then_inc(la_gathered, 1)

            for n, k in enumerate(POOL_WK):
                pool.wait_ge(wk_hi_made, k + 1)
                pool.tensor_tensor(wk_lo[:, k, :].rearrange("p (q b) -> p q b", q=PH),
                                   raw[k % 4][:, :].rearrange("p (b q) -> p q b", q=PH),
                                   wk_hi[:, k, :].rearrange("p (q b) -> p q b", q=PH), ALU.subtract).then_inc(wk_lo_pool, 1)
            pool.wait_ge(la_hi_made, 4)
            pool.wait_ge(lora_taken, 4)
            pool.wait_ge(las_hi_made, 1)
            pool.wait_ge(las_lo_made, 1)
            for s in range(2):
                for src, c0 in ((la_hi, 2 * RANK), (la_lo, 3 * RANK)):
                    pool.tensor_copy(la_g[s][:, :, c0:c0 + RANK], src[:, :, NG * RANK:].bitcast(F32))
                gather_la(s, s)

            fb_v = f_bias[:, :].rearrange("p (b q) -> p q b", q=PH)

            def x_plus_bias(slot, s):
                pool.tensor_tensor(x1_t[s][:, :].rearrange("p (q b) -> p q b", q=PH),
                                   x_in[slot][:, :].rearrange("p (b q) -> p q b", q=PH), fb_v, ALU.add).then_inc(xb_made, 1)

            pool.wait_ge(lbs_made, 1)
            pool.tensor_tensor(lbs_c[1][:, :].bitcast(F32R), lbs_t[:, :], lbs_c[0][:, :], ALU.subtract).then_inc(lbs_made, 1)
            pool.wait_ge(fbias_in, 16)
            pool.wait_ge(lb_turned, 2)
            for t in range(2):
                pool.wait_ge(x_loaded[t], 16)
                x_plus_bias(t, t)
            with pool.Fori(0, 3) as i:
                for k in range(4):
                    if k in (0, 3):
                        g = i * 2 + (2 if k == 0 else 3)
                        pool.wait_ge(z_mm, i * 2 + (1 if k == 0 else 2))
                        gather_la(g, 0 if k == 0 else 1)
                    pool.wait_ge(x1_stored[k % 2], i * 32 + 16 * (k // 2 + 1))
                    pool.wait_ge(x_loaded[(k + 2) % 4], i * 16 + (16 if k < 2 else 32))
                    x_plus_bias((k + 2) % 4, k % 2)
            for t in range(TILES - 4, TILES - 2):
                pool.wait_ge(x1_stored[t % 2], 16 * (t // 2 + 1))
                pool.wait_ge(x_loaded[(t + 2) % 4], 16 * ((t + 2) // 4 + 1))
                x_plus_bias((t + 2) % 4, t % 2)
            pool.wait_ge(y_mm, 2 * TILES)
            pool.wait_ge(xb_made, TILES)
            for s in range(2):
                pool.memset(x8[s][0:P // 2, :, 0:1], 0.0)
                pool.memset(x8[s][P // 2:P, :, BLK:BLK + 1], 0.0).then_inc(pads_made, 1)

            pool.wait_ge(b3_in, 16)

            def residual(s, loaded, free):
                pool.wait_ge(x1_loaded[s], loaded)
                if free is not None:
                    pool.wait_ge(out_stored[s], free)
                pool.tensor_tensor(res[s][:, :].rearrange("p (b q) -> p q b", q=PH),
                                   x1_in[s][:, :].rearrange("p (q b) -> p q b", q=PH),
                                   b3_s[:, :].rearrange("p (b q) -> p q b", q=PH), ALU.add).then_inc(res_made, 1)

            for s in range(2):
                residual(s, 16, None)
            with pool.Fori(0, TILES // 2 - 1) as i:
                for s in range(2):
                    residual(s, i * 16 + 32, i * 16 + 16)

        @block.scalar
        def _(act):
            act.sem_inc(c_taken, 8)
            act.sem_inc(silu_made, 1)
            act.dma_start(w0_s[:, :], c0_w0).then_inc(cond_in, 16)
            with nc.allow_non_contiguous_dma(reason="a few columns of small arrays"):
                act.dma_start(b0_s[:, :], c0_b0.rearrange("(p a) -> p a", a=1)).then_inc(cond_in, 16)
                act.dma_start(b1_s[:, :], c0_b1.rearrange("(p a) -> p a", a=1)).then_inc(mlp_in, 16)
                act.dma_start(b2_s[:, :], c0_b2.partition_broadcast(NB)).then_inc(mlp_in, 16)
            act.wait_ge(consts_made, 2)
            act.activation(warm[:, :], ident[:, 0:1], ACT.Gelu)

            def la_hi_part(n):
                act.wait_ge(lora_mm, n + 1)
                act.activation(la_hi[:, 2 * n:2 * n + 2, 0:NG * RANK],
                               bank(LA_BANKS[n]).rearrange("p (a c) -> p a c", a=2), ACT.Copy).then_inc(la_hi_made, 1)

            act.wait_ge(cond_in, 48)
            act.wait_ge(h1_mm, 1)
            act.activation(h1_s[:, :], bank(0)[:, 64:96], ACT.Gelu, bias=b0_s[:, :]).then_inc(h1_act, 1)
            act.wait_ge(mlp_in, 64)
            act.wait_ge(h2_mm, 1)
            act.activation(h2_s[:, :], bank(0)[:, 96:128], ACT.Gelu, bias=b1_s[:, :]).then_inc(h2_act, 1)
            act.wait_ge(nmax_made, 1)
            act.activation(ex[:, :], lg[:, :], ACT.Exp, bias=nmax[:, :], accum_out=esum[:, :]).then_inc(exp_made, 1)

            def wk_hi_part(k):
                act.wait_ge(raw_in[k % 4], 16 * (k // 4 + 1))
                act.activation(wk_hi[:, k, :].rearrange("p (q b) -> p q b", q=PH),
                               raw[k % 4][:, :].rearrange("p (b q) -> p q b", q=PH), ACT.Copy).then_inc(wk_hi_made, 1)

            act.wait_ge(mix_zeroed, 1)
            act.wait_ge(mix_mm, 4)
            act.activation(mix[NC:, :, NC:].rearrange("p t (c o) -> p t c o", c=4), mix_result(1), ACT.Copy).then_inc(mix_made, 1)
            act.wait_ge(las_mm, 1)
            act.wait_ge(setup_chain, 7)
            act.activation(la_hi[:, :, NG * RANK:], bank(1)[:, 256:512].rearrange("p (k r) -> p k r", r=RANK),
                           ACT.Copy).then_inc(las_hi_made, 1)
            def split_y(t, s, a):
                act.wait_ge(u_mm, t + 1)
                for h in range(2):
                    act.wait_ge(y_taken, t * 2 + h + 1)
                    act.activation(y_hi[s][:, a, 4 * h:4 * h + 4, :].rearrange("p k r -> p (k r)"),
                                   y_f[h][:, :], ACT.Copy).then_inc(y_hi_made, 1)

            wk_hi_part(0)
            act.wait_ge(taps_mm, 1)
            for half in range(2):
                last = act.activation(taps[:, :, half, :].rearrange("p g (q o) -> p g q o", q=PH),
                                      bank(2 + half).rearrange("p (q g o) -> p g q o", q=PH, g=GRP), ACT.Copy)
            last.then_inc(taps_made, 1)
            split_y(0, 0, 0)
            for k in range(3):
                wk_hi_part(k + 1)
                la_hi_part(k)
            la_hi_part(3)
            wk_hi_part(4)
            split_y(1, 0, 1)
            for k in range(5, KT):
                wk_hi_part(k)
            with nc.allow_non_contiguous_dma(reason="a few columns of small arrays"):
                act.dma_start(f_bias[:, :], f0_bias.partition_broadcast(P)).then_inc(fbias_in, 16)
                act.dma_start(b12_s[:, :, :], b12.rearrange("(h p j) -> p h j", h=2, j=NJ)).then_inc(b12_in, 16)

            act.wait_ge(lbs_turned, 1)
            act.activation(lbs_c[0][:, :].bitcast(F32R), lbs_t[:, :], ACT.Copy).then_inc(lbs_made, 1)
            act.wait_ge(lbs_stored, 32)
            for n in range(4):
                act.wait_ge(lora_mm, 4 + n + 1)
                act.activation(lb_part(0, n).bitcast(F32R), lb_result(n), ACT.Copy).then_inc(lb_hi_made, 1)
            with act.Fori(0, 3) as i:
                for k in range(2, 6):
                    split_y(i * 4 + k, (k // 2) % 2, k % 2)
            for k in range(2, 4):
                split_y(TILES - 4 + k, 1, k % 2)

            def w12_hi_part(j, s, first=False):
                for half in range(2):
                    act.wait_ge(turned, j * 2 + half + 1)
                    if half == 0 and not first:
                        act.wait_ge(g2_mm, j * 4)
                    act.activation(w12_hi[s][:, half, :, :].rearrange("p q m -> p (q m)"), w_t[half][:, :],
                                   ACT.Copy).then_inc(w_hi_made, 1)

            w12_hi_part(0, 0, True)
            with act.Fori(0, 4) as i:
                for k in range(8):
                    act.wait_ge(c_taken, i * 8 + k + 9)
                    act.activation(c_hi[:, ds(i, 1), :, k * NC:(k + 1) * NC].rearrange("p a q (g o) -> p (a q) g o", g=GRP),
                                   c_f[k % 4][:, :].rearrange("p (g q o) -> p q g o", g=GRP, q=PH),
                                   ACT.Copy).then_inc(c_hi_made, 1)

            def silu(j, rb):
                if rb == 0:
                    act.wait_ge(silu_made, j * 4 + 1)
                    act.activation(b1_j[:, :], b12_s[:, 0, ds(j, 1)], ACT.Copy).then_inc(b1_made, 1)
                    act.wait_ge(b1_made, j + 1)
                act.wait_ge(g1_mm, j * 4 + rb + 1)
                act.wait_ge(h_made, j * 4 + rb + 3)
                act.activation(silu_s[rb % 2][:, :], bank(2 * rb), ACT.Silu, bias=b1_j[:, :]).then_inc(silu_made, 1)

            def w3_hi_part(c):
                half, col = c // 4, (c % 4) * P
                act.wait_ge(turned, W12_USES + c + 1)
                act.activation(w3_hi[half][:, :, col:col + P], w_t[c % 2][:, :].rearrange("p (j n) -> p j n", j=NJ),
                               ACT.Copy).then_inc(w_hi_made, 1)

            act.wait_ge(c_lo_made, NB + 4)
            act.wait_ge(conv_mm, NB)
            act.wait_ge(b12_in, 16)
            with act.Fori(0, 3) as i:
                for k in range(2):
                    j = i * 2 + k
                    silu(j, 0)
                    w12_hi_part(i * 2 + k + 1, 1 - k)
                    for rb in range(1, RB):
                        silu(j, rb)
            silu(6, 0)
            w12_hi_part(7, 1)
            for rb in range(1, RB):
                silu(6, rb)
            silu(7, 0)
            w3_hi_part(0)
            w3_hi_part(1)
            silu(7, 1)
            w3_hi_part(2)
            w3_hi_part(3)

            def h_hi_part(t, s, loaded):
                act.wait_ge(h_loaded[s], loaded)
                act.wait_ge(o_mm, t * 2 + 2)
                act.activation(h_hi[s][:, :, :], h_in[s][:, :, :], ACT.Copy).then_inc(h_hi_made, 1)

            h_hi_part(0, 0, 16)
            silu(7, 2)
            h_hi_part(1, 1, 16)
            act.wait_ge(g2_mm, 4 * NJ + 3)
            for c in range(4, 8):
                w3_hi_part(c)
            silu(7, 3)
            with act.Fori(1, TILES // 2) as i:
                for s in range(2):
                    h_hi_part(i * 2 + s, s, i * 16 + 16)

        @block.vector
        def _(dve):
            steps = [0]

            def link(ins):
                steps[0] += 1
                ins.then_inc(setup_chain, 1)
                dve.wait_ge(setup_chain, steps[0])

            dve.sem_inc(x1_made, 2)
            dve.sem_inc(c_lo_made, 4)
            dve.sem_inc(h_made, 4)
            dve.sem_inc(out_made, 4)

            dve.wait_ge(consts_made, 2)
            for n, m in enumerate(m_r):
                src, w = (m_r[n - 1] if n else ident), m.shape[1]
                link(dve.tensor_tensor(m[:, :], src[:, 0:w], src[:, w:2 * w], ALU.add))
            dve.wait_ge(cond_t, 1)
            dve.tensor_copy(emb_t[:, :], bank(0)[:, 0:NB]).then_inc(emb_taken, 1)
            dve.wait_ge(gate_mm, 1)
            dve.tensor_copy(gate_c[:, :], bank(1)[:, 0:NG]).then_inc(gate_taken, 1)
            dve.wait_ge(gate_taken, 1)
            dve.tensor_tensor(gate_e[:, :, :], gate_c[:, :].unsqueeze(2).to_broadcast([P, NG, R8]),
                              m_r[-1][:, :].unsqueeze(1).to_broadcast([P, NG, R8]), ALU.mult).then_inc(gate_made, 1)

            def la_lo_part(n):
                dve.wait_ge(la_hi_made, n + 1)
                dve.tensor_tensor(la_lo[:, 2 * n:2 * n + 2, 0:NG * RANK], bank(LA_BANKS[n]).rearrange("p (a c) -> p a c", a=2),
                                  la_hi[:, 2 * n:2 * n + 2, 0:NG * RANK], ALU.subtract).then_inc(lora_taken, 1)

            def wk_lo_part(k):
                dve.wait_ge(wk_hi_made, k + 1)
                dve.tensor_tensor(wk_lo[:, k, :].rearrange("p (q b) -> p q b", q=PH),
                                  raw[k % 4][:, :].rearrange("p (b q) -> p q b", q=PH),
                                  wk_hi[:, k, :].rearrange("p (q b) -> p q b", q=PH), ALU.subtract).then_inc(wk_lo_made, 1)
                dve.wait_ge(wk_lo_made, uses_of_dve(k + 1))
                dve.sem_inc(raw_free, 1)

            dve.wait_ge(lg_mm, 1)
            link(dve.tensor_tensor(lg[:, :], bank(0)[0:NB, 128:136], b2_s[:, :], ALU.add))
            dve.reduce_max(nmax[:, :], lg[:, :], AX.X, negate=True).then_inc(nmax_made, 1)
            dve.wait_ge(exp_made, 1)
            link(dve.reciprocal(rsum[:, :], esum[:, :]))
            dve.tensor_scalar(att[:, :, :], ex[:, :].unsqueeze(2).to_broadcast([NB, NE, NPART]), rsum[:, :], None,
                              ALU.mult).then_inc(att_made, 1)
            dve.wait_ge(att_mm, 1)
            dve.tensor_tensor(att_s[:, :, :, :], bank(0)[:, 160:160 + NB].unsqueeze(1).unsqueeze(1).to_broadcast([P, 4, 4, NB]),
                              m_r[2][:, :].rearrange("p (c q) -> p q c", c=4).unsqueeze(3).to_broadcast([P, 4, 4, NB]),
                              ALU.mult).then_inc(att_taken, 1)
            dve.wait_ge(bias_mm, 1)
            dve.tensor_copy(yb_c[:, :], bank(0)[0:NB, 256:256 + NC]).then_inc(bias_made, 1)
            for q in range(4):
                dve.wait_ge(part_mm, q + 1)
                dve.tensor_copy(mix_t[:, OC * q:OC * (q + 1), :, :],
                                bank(4 + q)[:, 0:OC * NC].rearrange("p (o i) -> p o i", o=OC).unsqueeze(2)
                                .to_broadcast([P, OC, 2, NC])).then_inc(part_taken, 1)
            dve.wait_ge(mix_zeroed, 1)
            dve.wait_ge(mix_mm, 4)
            dve.tensor_copy(mix[0:NC, :, 0:NC].rearrange("p t (c o) -> p t c o", c=4), mix_result(0)).then_inc(mix_made, 1)
            dve.wait_ge(las_mm, 1)
            link(dve.tensor_copy(cw_t[:, :], bank(1)[:, 64:128]))
            dve.wait_ge(wpad_zeroed, 1)
            dve.wait_ge(small_in, 48)
            dve.tensor_copy(wpad[:, 8:8 + TAPS, :], w9_raw[:, :, :].rearrange("o c k -> o k c")).then_inc(wpad_made, 1)
            dve.wait_ge(bias_mm, 2)
            dve.tensor_tensor(cb_c[:, :], bank(0)[0:NB, 320:320 + NC], fside_s[:, :], ALU.add).then_inc(bias_made, 1)
            dve.wait_ge(las_hi_made, 1)
            dve.tensor_tensor(la_lo[:, :, NG * RANK:], bank(1)[:, 256:512].rearrange("p (k r) -> p k r", r=RANK),
                              la_hi[:, :, NG * RANK:], ALU.subtract).then_inc(las_lo_made, 1)
            def take_y(t, s, a, first=False):
                for h in range(2):
                    dve.wait_ge(y_mm, t * 2 + h + 1)
                    if not first:
                        dve.wait_ge(y_lo_made, t * 2 + h - 1)
                    dve.tensor_tensor(y_f[h][:, :].rearrange("p (k r) -> p k r", r=P),
                                      bank(h).rearrange("p (k r) -> p k r", r=P),
                                      y_bias[:, ds(t * P, P)].unsqueeze(1).to_broadcast([P, 4, P]), ALU.add).then_inc(y_taken, 1)
                for h in range(2):
                    dve.wait_ge(y_hi_made, t * 2 + h + 1)
                    dve.tensor_tensor(y_lo[s][:, a, 4 * h:4 * h + 4, :].rearrange("p k r -> p (k r)"),
                                      y_f[h][:, :], y_hi[s][:, a, 4 * h:4 * h + 4, :].rearrange("p k r -> p (k r)"),
                                      ALU.subtract).then_inc(y_lo_made, 1)

            def take_z(g, s, first=False):
                dve.wait_ge(z_mm, g + 1)
                if not first:
                    dve.wait_ge(u_mm, g * 2 + 2)
                z = bank(6)[:, 0:ROWS_G]
                dve.tensor_copy(z_1[s][:, :], z).then_inc(z_hi_made, 1)
                dve.wait_ge(z_hi_made, g + 1)
                for top in (0, 2 * RANK):
                    a, b = slice(top, top + RANK), slice(top + RANK, top + 2 * RANK)
                    dve.tensor_tensor(z_2[s][a, :], z[a, :], z_1[s][a, :], ALU.subtract)
                    last = dve.tensor_copy(z_2[s][b, :], z_1[s][a, :])
                last.then_inc(z_taken, 1)

            def take_x1(t, s):
                dve.wait_ge(u_mm, t + 5)
                dve.wait_ge(xb_made, t + 1)
                dve.tensor_tensor(x1_t[s][:, :], bank(2 + 2 * s, 2), x1_t[s][:, :], ALU.add).then_inc(x1_made, 1)

            wk_lo_part(0)
            dve.wait_ge(bias_loaded, 16)
            take_y(0, 0, 0, True)
            la_lo_part(0)
            la_lo_part(1)
            wk_lo_part(3)
            la_lo_part(2)
            la_lo_part(3)
            wk_lo_part(4)
            take_y(1, 0, 1)
            for k in range(5, KT):
                wk_lo_part(k)
            dve.wait_ge(raw_in[RAW_LBS % 4], 16 * (RAW_LBS // 4 + 1))
            dve.transpose(lbs_t[:, :].rearrange("p (q b o) -> p o q b", b=32, q=PH),
                          raw[RAW_LBS % 4][0:32, :].rearrange("p (o q r) -> p o q r", r=RANK, q=PH)).then_inc(lbs_turned, 1)
            dve.wait_ge(lbs_turned, 1)
            dve.sem_inc(raw_free, 1)
            for c in range(4):
                dve.wait_ge(lb_in[c], 64)
                src = lb_raw[c][:, :].rearrange("p (n q k r) -> p k q n r", n=4, q=PH, k=OCT)
                for k in range(OCT):
                    last = dve.transpose(lb_t[:, k, c], src[:, k])
                last.then_inc(lb_turned, 1)
            take_z(0, 0, True)
            for n in range(4):
                dve.wait_ge(lb_hi_made, n + 1)
                dve.tensor_tensor(lb_part(1, n).bitcast(F32R), lb_result(n), lb_part(0, n), ALU.subtract).then_inc(lora_taken, 1)
            take_y(2, 1, 0)
            take_y(3, 1, 1)
            take_x1(0, 0)
            take_x1(1, 1)
            take_z(1, 1, True)

            def take_group(i, k):
                t, g = i * 4 + 2 * k, i * 2 + k
                take_y(t + 2, 1 - k, 0)
                take_x1(t, 0)
                take_y(t + 3, 1 - k, 1)
                take_x1(t + 1, 1)
                take_z(g + 1, 1 - k)

            dve.wait_ge(bias_rest_loaded, 16)
            take_group(0, 1)
            with dve.Fori(1, 3) as i:
                for k in range(2):
                    take_group(i, k)
            take_y(14, 1, 0)
            take_x1(12, 0)
            take_y(15, 1, 1)
            take_x1(13, 1)
            take_z(7, 1)
            take_x1(14, 0)
            take_x1(15, 1)

            def turn(n_in, s, value, half, n_free):
                dve.wait_ge(w_in[s], value)
                if n_free is not None:
                    dve.wait_ge(w_lo_made, n_free)
                dve.transpose(w_t[half][:, :].rearrange("p (q m b) -> p q m b", q=PH, m=4),
                              raw[s][:, :].rearrange("p (m a q) -> p q m a", m=4, q=PH)).then_inc(turned, 1)
                dve.wait_ge(turned, n_in)
                dve.sem_inc(w_free, 1)

            def turn_w12(j, first=False):
                for half in range(2):
                    turn(j * 2 + half + 1, half, j * 64 + 64, half, None if first else j * 2 + half - 1)

            def w12_lo_part(j, s):
                for half in range(2):
                    dve.wait_ge(w_hi_made, j * 2 + half + 1)
                    dve.tensor_tensor(w12_lo[s][:, half, :, :].rearrange("p q m -> p (q m)"), w_t[half][:, :],
                                      w12_hi[s][:, half, :, :].rearrange("p q m -> p (q m)"), ALU.subtract).then_inc(w_lo_made, 1)

            def turn_w3(c):
                turn(W12_USES + c + 1, c % 2, 64 * (NJ + c // 2 + 1), c % 2, W12_USES + c - 1)

            def w3_lo_part(c):
                half, col = c // 4, (c % 4) * P
                dve.wait_ge(w_hi_made, W12_USES + c + 1)
                dve.tensor_tensor(w3_lo[half][:, :, col:col + P], w_t[c % 2][:, :].rearrange("p (j n) -> p j n", j=NJ),
                                  w3_hi[half][:, :, col:col + P], ALU.subtract).then_inc(w_lo_made, 1)

            turn_w12(0, True)
            w12_lo_part(0, 0)

            for s in range(2):
                dve.wait_ge(x1_stored[s], 16 * TILES // 2)

            def c_lo_part(i, k):
                dve.wait_ge(c_hi_made, i * 8 + k + 1)
                dve.tensor_tensor(c_lo[:, ds(i, 1), :, k * NC:(k + 1) * NC].rearrange("p a q (g o) -> p (a q) g o", g=GRP),
                                  c_f[k % 4][:, :].rearrange("p (g q o) -> p q g o", g=GRP, q=PH),
                                  c_hi[:, ds(i, 1), :, k * NC:(k + 1) * NC].rearrange("p a q (g o) -> p (a q) g o", g=GRP),
                                  ALU.subtract).then_inc(c_lo_made, 1)

            def take_c(i):
                for k in range(8):
                    b = i * 8 + k
                    dve.wait_ge(conv_mm, b + 1)
                    dve.wait_ge(c_lo_made, b + 1)
                    dve.tensor_tensor(c_f[k % 4][:, :].rearrange("p (g q o) -> p g q o", g=GRP, q=PH),
                                      bank(k).rearrange("p (g q o) -> p g q o", g=GRP, q=PH),
                                      c_bias[:, ds(b * NC, NC)].rearrange("p (g o) -> p g o", g=GRP)
                                      .unsqueeze(2).to_broadcast([P, GRP, PH, CG]), ALU.add).then_inc(c_taken, 1)
                    if k:
                        c_lo_part(i, k - 1)
                c_lo_part(i, 7)

            for half in range(2):
                dve.wait_ge(c_bias_loaded[half], 16)
                with dve.Fori(2 * half, 2 * half + 2) as i:
                    take_c(i)

            def hidden(j, rb):
                dve.wait_ge(g2_mm, j * 4 + rb + 5)
                dve.wait_ge(silu_made, j * 4 + rb + 2)
                if not (isinstance(j, int) and j == 0):
                    dve.wait_ge(h_stored[rb], j * 16)
                dve.scalar_tensor_tensor(out=h_s[rb][:, :], in0=bank(2 * rb + 1), scalar=b12_s[:, 1, ds(j, 1)],
                                         in1=silu_s[rb % 2][:, :], op0=ALU.add, op1=ALU.mult).then_inc(h_made, 1)

            dve.wait_ge(b12_in, 16)
            dve.wait_ge(c_lo_made, NB + 4)

            def gate_steps(i):
                for k in range(2):
                    j = i * 2 + k
                    hidden(j, 0)
                    turn_w12(j + 1)
                    hidden(j, 1)
                    w12_lo_part(j + 1, 1 - k)
                    hidden(j, 2)
                    hidden(j, 3)

            gate_steps(0)
            with dve.Fori(1, 3) as i:
                gate_steps(i)
            hidden(6, 0)
            turn_w12(7)
            hidden(6, 1)
            w12_lo_part(7, 1)
            hidden(6, 2)
            hidden(6, 3)

            def h_lo_part(t, s):
                dve.wait_ge(h_hi_made, t + 1)
                dve.tensor_tensor(h_lo[s][:, :, :], h_in[s][:, :, :], h_hi[s][:, :, :], ALU.subtract).then_inc(h_lo_made, 1)

            def take_out(t, s):
                dve.wait_ge(res_made, t + 1)
                for half in range(2):
                    dve.wait_ge(o_mm, t * 2 + half + 5)
                    cols = slice(half * HALF, (half + 1) * HALF)
                    dve.tensor_tensor(res[s][:, cols], bank(2 * s + half), res[s][:, cols], ALU.add).then_inc(out_made, 1)

            hidden(7, 0)
            turn_w3(0)
            turn_w3(1)
            w3_lo_part(0)
            w3_lo_part(1)
            hidden(7, 1)
            turn_w3(2)
            turn_w3(3)
            w3_lo_part(2)
            w3_lo_part(3)
            turn_w3(4)
            turn_w3(5)
            h_lo_part(0, 0)
            hidden(7, 2)
            h_lo_part(1, 1)
            w3_lo_part(4)
            w3_lo_part(5)
            turn_w3(6)
            turn_w3(7)
            w3_lo_part(6)
            w3_lo_part(7)
            hidden(7, 3)
            with dve.Fori(1, TILES // 2) as i:
                for s in range(2):
                    take_out(i * 2 + s - 2, s)
                    h_lo_part(i * 2 + s, s)
            for s in range(2):
                take_out(TILES - 2 + s, s)

        @block.tensor
        def _(pe):
            pe.sem_inc(u_mm, 4)
            pe.sem_inc(g2_mm, 4)
            pe.sem_inc(o_mm, 4)

            def mm(o, l, r, start, stop):
                return pe.matmul(o, l, r, start=start, stop=stop)

            def products(o, l_hi, l_lo, r_hi, r_lo, first, last):
                for n, (l, r) in enumerate(((l_hi, r_hi), (l_hi, r_lo), (l_lo, r_hi))):
                    for dst, src in zip(o, r):
                        ins = mm(dst, l, src, first and n == 0, last and n == 2)
                return ins

            def la_result(n):
                dst = bank(LA_BANKS[n])
                for a in range(2):
                    cols = dst[:, a * ROWS_G:(a + 1) * ROWS_G].rearrange("p (g k r) -> p k g r", k=OCT, r=R8)
                    for k in range(OCT):
                        c0 = (2 * n + a) * P
                        last = mm(cols[:, k], la_raw[:, k, c0:c0 + P], gate_e[:, :, :].rearrange("p g r -> p (g r)"),
                                  True, True)
                last.then_inc(lora_mm, 1)

            pe.wait_ge(consts_made, 2)
            pe.wait_ge(cond_in, 48)
            pe.transpose(bank(0)[:, 0:NB], emb_s[:, :], ident[0:NB, 0:NB]).then_inc(cond_t, 1)
            pe.wait_ge(emb_taken, 1)
            mm(bank(0)[:, 64:96], w0_s[:, :], emb_t[:, :], True, True).then_inc(h1_mm, 1)
            pe.wait_ge(consts_made, 4)
            pe.wait_ge(gate_in, 16)
            mm(bank(1)[:, 0:NG], sel[:, :], gate_t[:, :], True, True).then_inc(gate_mm, 1)
            pe.wait_ge(mlp_in, 64)
            pe.wait_ge(h1_act, 1)
            mm(bank(0)[:, 96:128], w1_s[:, :], h1_s[:, :], True, True).then_inc(h2_mm, 1)
            pe.wait_ge(h2_act, 1)
            mm(bank(0)[0:NB, 128:136], h2_s[:, :], w2_s[:, :], True, True).then_inc(lg_mm, 1)
            pe.wait_ge(att_made, 1)
            pe.transpose(bank(0)[:, 160:160 + NB], att[:, :, :].rearrange("b e c -> b (e c)"), ident[0:NB, 0:NB]).then_inc(att_mm, 1)
            pe.wait_ge(att_taken, 1)
            pe.wait_ge(biask_in, 16)
            mm(bank(0)[0:NB, 256:256 + NC], att_s[:, 0, 0, :], biask_s[:, :], True, True).then_inc(bias_mm, 1)
            pe.wait_ge(expert_in, 16)
            for q in range(4):
                mm(bank(4 + q)[:, 0:OC * NC], att_s[:, q, :, :].rearrange("p c b -> p (c b)"), expert[:, :],
                   True, True).then_inc(part_mm, 1)
            for q in range(4):
                pe.wait_ge(part_taken, q + 1)
                for o in range(OC):
                    last = pe.transpose(bank(4 + q)[:, o * P:(o + 1) * P],
                                        mix_t[:, OC * q + o, :, :].rearrange("p d i -> p (d i)"), ident[:, :])
                last.then_inc(mix_mm, 1)
            pe.wait_ge(gate_made, 1)
            pe.wait_ge(small_in, 48)
            pe.wait_ge(las_in, 16)
            pe.transpose(bank(1)[:, 64:128], cw_raw[:, :], ident[0:NC, 0:NC])
            for k in range(KT):
                last = pe.transpose(bank(1)[:, 256 + k * RANK:256 + (k + 1) * RANK], las_raw[:, k * P:(k + 1) * P],
                                    ident[0:RANK, 0:RANK])
            last.then_inc(las_mm, 1)
            pe.wait_ge(setup_chain, 7)
            mm(bank(0)[0:NB, 320:320 + NC], emb_t[:, :], cw_t[:, :], True, True).then_inc(bias_mm, 1)
            pe.wait_ge(wpad_made, 1)
            for half in range(2):
                for q in range(PH):
                    k0 = 8 + 8 * half - q
                    last = pe.transpose(bank(2 + half)[:, q * NC:(q + 1) * NC],
                                        wpad[:, k0:k0 + PH, :].rearrange("o k c -> o (k c)"), ident[0:NC, 0:NC])
            last.then_inc(taps_mm, 1)
            def lb_results():
                for n in range(4):
                    pe.wait_ge(lb_turned, 2 * (n // 2) + 2)
                    if n == 3:
                        pe.wait_ge(z_taken, 1)
                    dst = bank(LB_BANKS[n])
                    for odd in range(2):
                        src = lb_t[:, 2 * (n % 2) + odd, 2 * (n // 2):2 * (n // 2) + 2].rearrange("p c q b -> p (c q b)")
                        last = mm(dst[64 * odd:64 * odd + 64, :], gate_e[:, :, :].rearrange("p g r -> p (g r)"), src,
                                  True, True)
                    last.then_inc(lora_mm, 1)

            def y_tile(t, slot, loaded, first=False):
                pe.wait_ge(x_loaded[slot], loaded)
                for h in range(2):
                    if not first:
                        pe.wait_ge(y_taken, t * 2 + h - 1)
                    for k in range(4):
                        c0 = (4 * h + k) * P
                        last = mm(bank(h)[:, k * P:(k + 1) * P], x_in[slot][:, c0:c0 + P],
                                  mix[:, ds(t, 1), :].rearrange("p a r -> p (a r)"), True, True)
                    last.then_inc(y_mm, 1)

            def z_group(g, s, first=False):
                pe.wait_ge(la_gathered, g + 1)
                pe.wait_ge(y_lo_made, g * 4 + 4)
                if not first:
                    pe.wait_ge(z_taken, g)
                dst = bank(6)[:, 0:ROWS_G]
                for k in range(KT):
                    mm(dst, la_g[s][:, k, :], y_hi[s][:, :, k, :], k == 0, False)
                    last = mm(dst, la_g[s][:, k, :], y_lo[s][:, :, k, :], False, k == KT - 1)
                last.then_inc(z_mm, 1)

            def u_tile(t, s, a, lb_value, first=False):
                pe.wait_ge(y_lo_made, t * 2 + 2)
                pe.wait_ge(x1_made, t + 1)
                dst = [bank(2 + 2 * a), bank(3 + 2 * a)]
                for k in range(KT):
                    if first:
                        if k in POOL_WK:
                            pe.wait_ge(wk_lo_pool, POOL_WK.index(k) + 1)
                        else:
                            pe.wait_ge(wk_lo_made, uses_of_dve(k + 1))
                    products(dst, y_hi[s][:, a, k, :], y_lo[s][:, a, k, :],
                             [wk_hi[:, k, 0:HALF], wk_hi[:, k, HALF:]], [wk_lo[:, k, 0:HALF], wk_lo[:, k, HALF:]],
                             k == 0, False)
                if lb_value is not None:
                    pe.wait_ge(lb_loaded[s], lb_value)
                return dst

            def u_lora(dst, t, s, a, g):
                pe.wait_ge(z_taken, g + 1)
                rows = slice(a * P, (a + 1) * P)
                for z, b in ((z_1, lb_1), (z_2, lb_2)):
                    for half in range(2):
                        last = mm(dst[half], z[s][:, rows], b[s][:, half * HALF:(half + 1) * HALF], False, b is lb_2)
                last.then_inc(u_mm, 1)

            pe.wait_ge(mix_made, 2)
            pe.wait_ge(bias_made, 2)
            pe.wait_ge(las_lo_made, 1)
            y_tile(0, 0, 16, True)
            y_tile(1, 1, 16)
            pe.wait_ge(la_in, 16 * OCT)
            for n in range(4):
                la_result(n)
            pe.wait_ge(taps_made, 1)
            dst = u_tile(0, 0, 0, None, True)
            y_tile(2, 2, 16)
            pe.wait_ge(lora_taken, 4)
            z_group(0, 0, True)
            lb_results()
            pe.wait_ge(lora_taken, N_LORA - 2)
            dst1 = u_tile(1, 0, 1, None)
            y_tile(3, 3, 16)
            pe.wait_ge(lb_loaded[0], LB_FIRST)
            u_lora(dst, 0, 0, 0, 0)
            u_lora(dst1, 1, 0, 1, 0)
            pe.wait_ge(lora_taken, N_LORA)
            z_group(1, 1)

            def group(i, k):
                t, g = i * 4 + 2 * k, i * 2 + k
                y_tile(t + 2, (2 * k + 2) % 4, i * 16 + (16 if k == 0 else 32))
                u_lora(u_tile(t, k, 0, i * LB_NEXT + LB_FIRST), t, k, 0, g)
                y_tile(t + 3, (2 * k + 3) % 4, i * 16 + (16 if k == 0 else 32))
                u_lora(u_tile(t + 1, k, 1, None), t + 1, k, 1, g)
                z_group(g + 1, 1 - k)

            group(0, 1)
            with pe.Fori(1, 3) as i:
                for k in range(2):
                    group(i, k)
            y_tile(14, 2, 64)
            u_lora(u_tile(12, 0, 0, LB_FIRST + 3 * LB_NEXT), 12, 0, 0, 6)
            y_tile(15, 3, 64)
            u_lora(u_tile(13, 0, 1, None), 13, 0, 1, 6)
            z_group(7, 1)
            u_lora(u_tile(14, 1, 0, LB_FIRST + 3 * LB_NEXT), 14, 1, 0, 7)
            u_lora(u_tile(15, 1, 1, None), 15, 1, 1, 7)

            pe.wait_ge(pads_made, 2)

            def convolve(i, first=False):
                for k in range(8):
                    if first and k in (2, 4):
                        pe.wait_ge(x1_made, TILES + k // 2)
                    if k % 4 == 0:
                        pe.wait_ge(x8_loaded[k // 4], i * 128 + 128)
                    pe.wait_ge(c_taken, i * 8 + k + 1)
                    for g in range(GRP):
                        src, dst = x8[k // 4][:, (k % 4) * GRP + g, :], bank(k)[:, g * P:(g + 1) * P]
                        mm(dst, src[:, 0:BLK], taps[:, g, 0, :], True, False)
                        last = mm(dst, src[:, 1:BLK + 1], taps[:, g, 1, :], False, True)
                    last.then_inc(conv_mm, 1)

            pe.wait_ge(y_taken, 2 * TILES)
            convolve(0, True)
            with pe.Fori(1, 4) as i:
                convolve(i)

            def gate_step(j, s, first=False):
                pe.wait_ge(w_lo_made, j * 2 + 2)
                for rb in range(RB):
                    if first:
                        pe.wait_ge(c_lo_made, 8 * (rb + 1) + 4)
                        pe.wait_ge(c_taken, NB - 8 + 2 * (rb + 1) + 8)
                    pe.wait_ge(h_made, j * 4 + rb + 1)
                    for half, done in ((0, g1_mm), (1, g2_mm)):
                        for q in range(PH):
                            last = products([bank(2 * rb + half)], w12_hi[s][:, half, q, :], w12_lo[s][:, half, q, :],
                                            [c_hi[:, rb, q, :]], [c_lo[:, rb, q, :]], q == 0, q == PH - 1)
                        last.then_inc(done, 1)

            gate_step(0, 0, True)
            gate_step(1, 1)
            with pe.Fori(1, NJ // 2) as i:
                for k in range(2):
                    gate_step(i * 2 + k, k)

            def out_tile(t, s, first=False):
                pe.wait_ge(h_lo_made, t + 1)
                pe.wait_ge(out_made, t * 2 + 2)
                for half in range(2):
                    if first:
                        pe.wait_ge(w_lo_made, W12_USES + 4 * (half + 1))
                    for j in range(NJ):
                        last = products([bank(2 * s + half)], h_hi[s][:, j, :], h_lo[s][:, j, :],
                                        [w3_hi[half][:, j, :]], [w3_lo[half][:, j, :]], j == 0, j == NJ - 1)
                    last.then_inc(o_mm, 1)

            pe.wait_ge(h_made, 4 + 4 * (NJ - 1) + 2)
            out_tile(0, 0, True)
            out_tile(1, 1)
            with pe.Fori(1, TILES // 2) as i:
                for s in range(2):
                    out_tile(i * 2 + s, s)


_INS = ['x', 'cond_128', 'fside_S_0', 'L0_cond_W0', 'L0_cond_b0', 'L0_cond_W1', 'L0_cond_b1', 'L0_cond_W2', 'L0_cond_b2',
        'L0_cond_weight', 'L0_cond_bias_k', 'L0_ffn_gate', 'L0_ffn_kernel', 'L0_ffn_bias', 'L0_ffn_lora_A',
        'L0_ffn_lora_B', 'L0_ffn_lora_A_shared', 'L0_ffn_lora_B_shared', 'L1_cond_weight', 'L1_cond_c_weight',
        'L1_ffn_w12', 'L1_ffn_b12', 'L1_ffn_w3', 'L1_ffn_b3']


def kernel(**inputs):
    import concourse.bacc as bacc
    from concourse.bass_utils import run_bass_kernel_spmd

    nc = bacc.Bacc("TRN2", target_bir_lowering=False, num_devices=1)
    arrays, args = {}, []
    for name in _INS:
        a = np.ascontiguousarray(inputs[name])
        arrays[f"in_{name}"] = a
        args.append(nc.dram_tensor(f"in_{name}", a.shape, mybir.dt.from_np(a.dtype), kind="ExternalInput").ap())
    out = nc.dram_tensor("out", (NB, NC, NL), F32, kind="ExternalOutput").ap()
    layered_kernel(nc, *args, out)
    r = run_bass_kernel_spmd(nc, [arrays], core_ids=[0])
    return r.results[0]["out"]
```
